# Optimizing a Trainium2 kernel written in Bass

```python
import numpy as np
import jax
import jax.numpy as jnp

def _softmax(x, axis=-1):
    return jax.nn.softmax(x, axis=axis)

def _gelu(x):
    return jax.nn.gelu(x, approximate=True)

def _silu(x):
    return jax.nn.silu(x)

def _sigmoid(x):
    return jax.nn.sigmoid(x)

def _layernorm(x, axis=-1, eps=1e-05):
    m = jnp.mean(x, axis=axis, keepdims=True)
    v = jnp.var(x, axis=axis, keepdims=True)
    return (x - m) / jnp.sqrt(v + eps)

def _scatter_add(tgt, idx, src, axis=0):
    return tgt.at[idx].add(src)

def _segment_sum(src, seg, n):
    return jax.ops.segment_sum(src, seg, n)
kernel_name = 'mk_perceiver_d2_seqx_r2_dd84e4'

def setup_inputs(seed: int=0):
    np.random.seed(seed)
    _w = jnp.asarray

    def _rec_inputs():
        import jax
        import jax.numpy as jnp
        _rk = jax.random.key(seed)
        x = 0.0002417 + 0.9998 * jax.random.normal(jax.random.fold_in(_rk, 1), (1, 512, 512), jnp.float32)
        _lenS = 512 - jax.random.randint(jax.random.fold_in(_rk, 7), (1,), 0, max(1, 512 // 4) + 1, jnp.int32)
        _lenS2 = 8192 - jax.random.randint(jax.random.fold_in(_rk, 8), (1,), 0, max(1, 8192 // 4) + 1, jnp.int32)
        _ctx_1024P = jax.random.normal(jax.random.fold_in(_rk, 11), (1, 16, 512), jnp.float32)
        _ctx_1024c = jax.random.dirichlet(jax.random.fold_in(_rk, 511), 0.3 * jnp.ones((16,), jnp.float32), (1, 8192))
        _ctx_1024t = jnp.einsum('bsk,bkd->bsd', _ctx_1024c, _ctx_1024P)
        _ctx_1024t = _ctx_1024t * jax.lax.rsqrt(jnp.mean(jnp.square(_ctx_1024t)) + 1e-12) * 0.953939
        ctx_1024 = 7.22013e-05 + 1.00017 * (_ctx_1024t + 0.3 * jax.random.normal(jax.random.fold_in(_rk, 611), (1, 8192, 512), jnp.float32))
        pos_BxS2 = jnp.broadcast_to(jnp.arange(8192, dtype=jnp.int32), (1, 8192))
        _validS = jnp.arange(512)[None, :] < _lenS[:, None]
        _validS2 = jnp.arange(8192)[None, :] < _lenS2[:, None]
        _causal = jnp.tril(jnp.ones((512, 512), dtype=bool))
        mask_Bx1xSxS2_ik1 = jnp.where(jnp.broadcast_to(_validS2[:, None, None, :], (1, 1, 512, 8192)), 1, 0).astype(jnp.int32)
        return (x, ctx_1024, pos_BxS2, mask_Bx1xSxS2_ik1)
    x, ctx_1024, pos_BxS2, mask_Bx1xSxS2_ik1 = _rec_inputs()

    def _L0_xattn_setup():
        import jax, jax.numpy as jnp
        import numpy as np
        EMBED = 512
        HEADS = 16
        HEAD_DIM = EMBED // HEADS
        N, SEQ = (4, 1024)
        key = jax.random.key(seed)
        ks = jax.random.split(key, 9)
        values = jax.random.normal(ks[0], (N, SEQ, EMBED), dtype=jnp.float32)
        keys = jax.random.normal(ks[1], (N, SEQ, EMBED), dtype=jnp.float32)
        query = jax.random.normal(ks[2], (N, SEQ, EMBED), dtype=jnp.float32)
        mask = jax.random.randint(ks[3], (N, 1, SEQ, SEQ), 0, 2, dtype=jnp.int32)
        s_h = 1.0 / np.sqrt(HEAD_DIM)
        s_e = 1.0 / np.sqrt(EMBED)
        Wv = jax.random.normal(ks[4], (HEAD_DIM, HEAD_DIM), dtype=jnp.float32) * s_h
        Wk = jax.random.normal(ks[5], (HEAD_DIM, HEAD_DIM), dtype=jnp.float32) * s_h
        Wq = jax.random.normal(ks[6], (HEAD_DIM, HEAD_DIM), dtype=jnp.float32) * s_h
        Wo = jax.random.normal(ks[7], (EMBED, EMBED), dtype=jnp.float32) * s_e
        bo = jax.random.normal(ks[8], (EMBED,), dtype=jnp.float32) * 0.01
        return {'values': values, 'keys': keys, 'query': query, 'mask': mask, 'Wv': Wv, 'Wk': Wk, 'Wq': Wq, 'Wo': Wo, 'bo': bo}
    _L0_xattn_all = _L0_xattn_setup()
    _L0_xattn_in = {k: v for k, v in _L0_xattn_all.items() if k in ('Wv', 'Wk', 'Wq', 'Wo', 'bo')}
    del _L0_xattn_all

    def _L0_attn_setup():
        import jax, jax.numpy as jnp
        import numpy as np
        from jax import lax

        def layer_norm(x, g, b, eps=1e-05):
            m = jnp.mean(x, axis=-1, keepdims=True)
            v = jnp.var(x, axis=-1, keepdims=True)
            return (x - m) * lax.rsqrt(v + eps) * g + b

        def depthwise_causal_conv(u, w, b):
            Din = u.shape[-1]
            k = w.shape[1]
            x = jnp.transpose(u, (0, 2, 1))
            x = jnp.pad(x, ((0, 0), (0, 0), (k - 1, 0)))
            out = lax.conv_general_dilated(x, w[:, None, :], window_strides=(1,), padding='VALID', dimension_numbers=('NCH', 'OIH', 'NCH'), feature_group_count=Din)
            out = out + b[None, :, None]
            return jnp.transpose(out, (0, 2, 1))

        def selective_scan(u, delta, A, Bm, Cm, D):
            dA = jnp.exp(delta[..., None] * A)
            dBu = delta[..., None] * Bm[:, :, None, :] * u[..., None]

            def step(h, xs):
                dA_t, dBu_t, C_t = xs
                h = dA_t * h + dBu_t
                y = jnp.einsum('bdn,bn->bd', h, C_t)
                return (h, y)
            Bsz, L, Din, N = dA.shape
            h0 = jnp.zeros((Bsz, Din, N), dtype=u.dtype)
            _, ys = lax.scan(step, h0, (jnp.moveaxis(dA, 1, 0), jnp.moveaxis(dBu, 1, 0), jnp.moveaxis(Cm, 1, 0)))
            y = jnp.moveaxis(ys, 0, 1)
            return y + u * D
        key = jax.random.key(seed)
        B, L, Dm = (2, 1024, 512)
        Din, N, k = (2 * Dm, 16, 4)
        dt_rank = Dm // 16
        ks = jax.random.split(key, 8)
        s = 0.02
        return {'x': jax.random.normal(ks[0], (B, L, Dm), jnp.float32), 'in_proj_w': jax.random.normal(ks[1], (Dm, 2 * Din), jnp.float32) * s, 'conv_w': jax.random.normal(ks[2], (Din, k), jnp.float32) * 0.1, 'conv_b': jnp.zeros((Din,), jnp.float32), 'x_proj_w': jax.random.normal(ks[3], (Din, dt_rank + 2 * N), jnp.float32) * s, 'dt_proj_w': jax.random.normal(ks[4], (dt_rank, Din), jnp.float32) * s, 'dt_proj_b': jax.random.uniform(ks[5], (Din,), jnp.float32, -4.0, -2.0), 'A_log': jnp.log(jnp.tile(jnp.arange(1, N + 1, dtype=jnp.float32)[None, :], (Din, 1))), 'D': jnp.ones((Din,), jnp.float32), 'out_proj_w': jax.random.normal(ks[6], (Din, Dm), jnp.float32) * s, 'ln_g': jnp.ones((Dm,), jnp.float32), 'ln_b': jnp.zeros((Dm,), jnp.float32)}
    _L0_attn_all = _L0_attn_setup()
    _L0_attn_in = {k: v for k, v in _L0_attn_all.items() if k in ('in_proj_w', 'conv_w', 'conv_b', 'x_proj_w', 'dt_proj_w', 'dt_proj_b', 'A_log', 'D', 'out_proj_w', 'ln_g', 'ln_b')}
    del _L0_attn_all

    def _L0_ffn_setup():
        import jax, jax.numpy as jnp
        import numpy as np
        B, S, H, E, K = (2, 512, 512, 8, 2)
        F = 4 * H
        key = jax.random.key(seed)
        ks = jax.random.split(key, 8)
        std = 0.02
        return {'x': jax.random.normal(ks[0], (B, S, H), jnp.float32), 'gate_w': jax.random.normal(ks[1], (E, H), jnp.float32) * (std / np.sqrt(H)), 'gate_bias': jnp.zeros((E,), jnp.float32), 'Wu': jax.random.normal(ks[2], (E, F, H), jnp.float32) * std, 'bu': jnp.zeros((E, F), jnp.float32), 'Wd': jax.random.normal(ks[3], (E, H, F), jnp.float32) * std, 'bd': jnp.zeros((E, H), jnp.float32), 'sWu': jax.random.normal(ks[4], (F, H), jnp.float32) * std, 'sbu': jnp.zeros((F,), jnp.float32), 'sWd': jax.random.normal(ks[5], (H, F), jnp.float32) * std, 'sbd': jnp.zeros((H,), jnp.float32)}
    _L0_ffn_all = _L0_ffn_setup()
    _L0_ffn_in = {k: v for k, v in _L0_ffn_all.items() if k in ('gate_w', 'gate_bias', 'Wu', 'bu', 'Wd', 'bd', 'sWu', 'sbu', 'sWd', 'sbd')}
    del _L0_ffn_all

    def _L1_xattn_setup():
        import jax, jax.numpy as jnp
        import numpy as np
        DIM = 512
        NUM_HEADS = 16
        HEAD_DIM = DIM // NUM_HEADS
        SCALE = HEAD_DIM ** (-0.5)
        B, NQ, NK = (4, 1024, 1024)
        key = jax.random.key(seed)
        ks = jax.random.split(key, 10)
        s = 0.02
        return {'query': jax.random.normal(ks[0], (B, NQ, DIM), dtype=jnp.float32), 'key': jax.random.normal(ks[1], (B, NK, DIM), dtype=jnp.float32), 'value': jax.random.normal(ks[2], (B, NK, DIM), dtype=jnp.float32), 'qpos': jnp.arange(B * NQ, dtype=jnp.int64).reshape(B, NQ) % NQ, 'kpos': jnp.arange(B * NK, dtype=jnp.int64).reshape(B, NK) % NK, 'Wq': jax.random.normal(ks[3], (DIM, DIM), dtype=jnp.float32) * s, 'Wk': jax.random.normal(ks[4], (DIM, DIM), dtype=jnp.float32) * s, 'Wv': jax.random.normal(ks[5], (DIM, DIM), dtype=jnp.float32) * s, 'Wo': jax.random.normal(ks[6], (DIM, DIM), dtype=jnp.float32) * s, 'bo': jnp.zeros((DIM,), dtype=jnp.float32)}
    _L1_xattn_all = _L1_xattn_setup()
    _L1_xattn_in = {k: v for k, v in _L1_xattn_all.items() if k in ('Wq', 'Wk', 'Wv', 'Wo', 'bo')}
    del _L1_xattn_all

    def _L1_attn_setup():
        import jax, jax.numpy as jnp
        import numpy as np
        N_EMBD = 512
        N_HEAD = 8
        HEAD_DIM = N_EMBD // N_HEAD
        EPS = 1e-06

        def _lrpe(xh, theta, n):
            idx = jnp.arange(n, dtype=xh.dtype).reshape(1, n, 1)
            th = theta * idx
            th = th[None]
            return jnp.concatenate([xh * jnp.cos(th), xh * jnp.sin(th)], axis=-1)

        def _srmsnorm(y):
            ms = jnp.mean(jnp.square(y), axis=-1, keepdims=True)
            return y * jax.lax.rsqrt(ms + EPS)
        key = jax.random.key(seed)
        ks = jax.random.split(key, 8)
        b, n = (2, 1024)
        x = jax.random.normal(ks[0], (b, n, N_EMBD), dtype=jnp.float32)
        slope_rate = -jax.random.uniform(ks[1], (N_HEAD, 1, 1), dtype=jnp.float32)
        s = 0.02
        qkvu_w = jax.random.normal(ks[2], (4 * N_EMBD, N_EMBD), dtype=jnp.float32) * s
        qkvu_b = jnp.zeros((4 * N_EMBD,), dtype=jnp.float32)
        out_w = jax.random.normal(ks[3], (N_EMBD, N_EMBD), dtype=jnp.float32) * s
        out_b = jnp.zeros((N_EMBD,), dtype=jnp.float32)
        d = N_EMBD
        theta = (10000.0 ** (-2.0 / d * jnp.arange(d, dtype=jnp.float32))).reshape(N_HEAD, 1, HEAD_DIM)
        return {'x': x, 'slope_rate': slope_rate, 'qkvu_w': qkvu_w, 'qkvu_b': qkvu_b, 'out_w': out_w, 'out_b': out_b, 'theta': theta}
    _L1_attn_all = _L1_attn_setup()
    _L1_attn_in = {k: v for k, v in _L1_attn_all.items() if k in ('slope_rate', 'qkvu_w', 'qkvu_b', 'out_w', 'out_b', 'theta')}
    del _L1_attn_all

    def _L1_ffn_setup():
        import jax, jax.numpy as jnp
        import numpy as np
        B, S, D, H, E, K, F = (1, 512, 512, 16, 8, 2, 2048)

        def layernorm(x, g, b, eps=1e-05):
            m = x.mean(-1, keepdims=True)
            v = ((x - m) ** 2).mean(-1, keepdims=True)
            return (x - m) * jax.lax.rsqrt(v + eps) * g + b
        key = jax.random.key(seed)
        ks = jax.random.split(key, 8)
        n = lambda k, shape, sc: jax.random.normal(k, shape, dtype=jnp.float32) * sc
        return {'x': n(ks[0], (B, S, D), 1.0), 'w_qkv': n(ks[1], (D, 3 * D), D ** (-0.5)), 'w_o': n(ks[2], (D, D), D ** (-0.5)), 'g1': jnp.ones((D,), jnp.float32), 'b1': jnp.zeros((D,), jnp.float32), 'wg': n(ks[3], (D, E), D ** (-0.5)), 'w1': n(ks[4], (E, D, F), D ** (-0.5)), 'bb1': jnp.zeros((E, F), jnp.float32), 'w2': n(ks[5], (E, F, D), F ** (-0.5)), 'bb2': jnp.zeros((E, D), jnp.float32), 'g2': jnp.ones((D,), jnp.float32), 'b2': jnp.zeros((D,), jnp.float32)}
    _L1_ffn_all = _L1_ffn_setup()
    _L1_ffn_in = {k: v for k, v in _L1_ffn_all.items() if k in ('w_qkv', 'w_o', 'g1', 'b1', 'wg', 'w1', 'bb1', 'w2', 'bb2', 'g2', 'b2')}
    del _L1_ffn_all
    return {'x': x, 'ctx_1024': ctx_1024, 'pos_BxS2': pos_BxS2, 'mask_Bx1xSxS2_ik1': mask_Bx1xSxS2_ik1, 'L0_xattn_Wv': _L0_xattn_in['Wv'], 'L0_xattn_Wk': _L0_xattn_in['Wk'], 'L0_xattn_Wq': _L0_xattn_in['Wq'], 'L0_xattn_Wo': _L0_xattn_in['Wo'], 'L0_xattn_bo': _L0_xattn_in['bo'], 'L0_attn_in_proj_w': _L0_attn_in['in_proj_w'], 'L0_attn_conv_w': _L0_attn_in['conv_w'], 'L0_attn_conv_b': _L0_attn_in['conv_b'], 'L0_attn_x_proj_w': _L0_attn_in['x_proj_w'], 'L0_attn_dt_proj_w': _L0_attn_in['dt_proj_w'], 'L0_attn_dt_proj_b': _L0_attn_in['dt_proj_b'], 'L0_attn_A_log': _L0_attn_in['A_log'], 'L0_attn_D': _L0_attn_in['D'], 'L0_attn_out_proj_w': _L0_attn_in['out_proj_w'], 'L0_attn_ln_g': _L0_attn_in['ln_g'], 'L0_attn_ln_b': _L0_attn_in['ln_b'], 'L0_ffn_gate_w': _L0_ffn_in['gate_w'], 'L0_ffn_gate_bias': _L0_ffn_in['gate_bias'], 'L0_ffn_Wu': _L0_ffn_in['Wu'], 'L0_ffn_bu': _L0_ffn_in['bu'], 'L0_ffn_Wd': _L0_ffn_in['Wd'], 'L0_ffn_bd': _L0_ffn_in['bd'], 'L0_ffn_sWu': _L0_ffn_in['sWu'], 'L0_ffn_sbu': _L0_ffn_in['sbu'], 'L0_ffn_sWd': _L0_ffn_in['sWd'], 'L0_ffn_sbd': _L0_ffn_in['sbd'], 'L1_xattn_Wq': _L1_xattn_in['Wq'], 'L1_xattn_Wk': _L1_xattn_in['Wk'], 'L1_xattn_Wv': _L1_xattn_in['Wv'], 'L1_xattn_Wo': _L1_xattn_in['Wo'], 'L1_xattn_bo': _L1_xattn_in['bo'], 'L1_attn_slope_rate': _L1_attn_in['slope_rate'], 'L1_attn_qkvu_w': _L1_attn_in['qkvu_w'], 'L1_attn_qkvu_b': _L1_attn_in['qkvu_b'], 'L1_attn_out_w': _L1_attn_in['out_w'], 'L1_attn_out_b': _L1_attn_in['out_b'], 'L1_attn_theta': _L1_attn_in['theta'], 'L1_ffn_w_qkv': _L1_ffn_in['w_qkv'], 'L1_ffn_w_o': _L1_ffn_in['w_o'], 'L1_ffn_g1': _L1_ffn_in['g1'], 'L1_ffn_b1': _L1_ffn_in['b1'], 'L1_ffn_wg': _L1_ffn_in['wg'], 'L1_ffn_w1': _L1_ffn_in['w1'], 'L1_ffn_bb1': _L1_ffn_in['bb1'], 'L1_ffn_w2': _L1_ffn_in['w2'], 'L1_ffn_bb2': _L1_ffn_in['bb2'], 'L1_ffn_g2': _L1_ffn_in['g2'], 'L1_ffn_b2': _L1_ffn_in['b2']}

def reference(x, ctx_1024, pos_BxS2, mask_Bx1xSxS2_ik1, L0_xattn_Wv, L0_xattn_Wk, L0_xattn_Wq, L0_xattn_Wo, L0_xattn_bo, L0_attn_in_proj_w, L0_attn_conv_w, L0_attn_conv_b, L0_attn_x_proj_w, L0_attn_dt_proj_w, L0_attn_dt_proj_b, L0_attn_A_log, L0_attn_D, L0_attn_out_proj_w, L0_attn_ln_g, L0_attn_ln_b, L0_ffn_gate_w, L0_ffn_gate_bias, L0_ffn_Wu, L0_ffn_bu, L0_ffn_Wd, L0_ffn_bd, L0_ffn_sWu, L0_ffn_sbu, L0_ffn_sWd, L0_ffn_sbd, L1_xattn_Wq, L1_xattn_Wk, L1_xattn_Wv, L1_xattn_Wo, L1_xattn_bo, L1_attn_slope_rate, L1_attn_qkvu_w, L1_attn_qkvu_b, L1_attn_out_w, L1_attn_out_b, L1_attn_theta, L1_ffn_w_qkv, L1_ffn_w_o, L1_ffn_g1, L1_ffn_b1, L1_ffn_wg, L1_ffn_w1, L1_ffn_bb1, L1_ffn_w2, L1_ffn_bb2, L1_ffn_g2, L1_ffn_b2):
    import jax
    import jax.numpy as jnp

    def _L0_xattn_ref(values, keys, query, mask, Wv, Wk, Wq, Wo, bo):
        import jax, jax.numpy as jnp
        import numpy as np
        EMBED = 512
        HEADS = 16
        HEAD_DIM = EMBED // HEADS
        N, SEQ = (4, 1024)
        n, q_len = (query.shape[0], query.shape[1])
        k_len, v_len = (keys.shape[1], values.shape[1])
        v = values.reshape(n, v_len, HEADS, HEAD_DIM)
        k = keys.reshape(n, k_len, HEADS, HEAD_DIM)
        q = query.reshape(n, q_len, HEADS, HEAD_DIM)
        v = jnp.einsum('nlhd,ed->nlhe', v, Wv)
        k = jnp.einsum('nlhd,ed->nlhe', k, Wk)
        q = jnp.einsum('nlhd,ed->nlhe', q, Wq)
        energy = jnp.einsum('nqhd,nkhd->nhqk', q, k)
        energy = jnp.where(mask == 0, jnp.float32(-1e+20), energy)
        attention = jax.nn.softmax(energy / jnp.sqrt(jnp.float32(EMBED)), axis=3)
        out = jnp.einsum('nhql,nlhd->nqhd', attention, v).reshape(n, q_len, EMBED)
        return out @ Wo.T + bo

    def _L0_attn_ref(x, in_proj_w, conv_w, conv_b, x_proj_w, dt_proj_w, dt_proj_b, A_log, D, out_proj_w, ln_g, ln_b):
        import jax, jax.numpy as jnp
        import numpy as np
        from jax import lax

        def layer_norm(x, g, b, eps=1e-05):
            m = jnp.mean(x, axis=-1, keepdims=True)
            v = jnp.var(x, axis=-1, keepdims=True)
            return (x - m) * lax.rsqrt(v + eps) * g + b

        def depthwise_causal_conv(u, w, b):
            Din = u.shape[-1]
            k = w.shape[1]
            x = jnp.transpose(u, (0, 2, 1))
            x = jnp.pad(x, ((0, 0), (0, 0), (k - 1, 0)))
            out = lax.conv_general_dilated(x, w[:, None, :], window_strides=(1,), padding='VALID', dimension_numbers=('NCH', 'OIH', 'NCH'), feature_group_count=Din)
            out = out + b[None, :, None]
            return jnp.transpose(out, (0, 2, 1))

        def selective_scan(u, delta, A, Bm, Cm, D):
            dA = jnp.exp(delta[..., None] * A)
            dBu = delta[..., None] * Bm[:, :, None, :] * u[..., None]

            def step(h, xs):
                dA_t, dBu_t, C_t = xs
                h = dA_t * h + dBu_t
                y = jnp.einsum('bdn,bn->bd', h, C_t)
                return (h, y)
            Bsz, L, Din, N = dA.shape
            h0 = jnp.zeros((Bsz, Din, N), dtype=u.dtype)
            _, ys = lax.scan(step, h0, (jnp.moveaxis(dA, 1, 0), jnp.moveaxis(dBu, 1, 0), jnp.moveaxis(Cm, 1, 0)))
            y = jnp.moveaxis(ys, 0, 1)
            return y + u * D
        residual = x
        xn = layer_norm(x, ln_g, ln_b)
        xz = xn @ in_proj_w
        Din = in_proj_w.shape[1] // 2
        u, z = (xz[..., :Din], xz[..., Din:])
        u = jax.nn.silu(depthwise_causal_conv(u, conv_w, conv_b))
        N = A_log.shape[1]
        dt_rank = x_proj_w.shape[1] - 2 * N
        dbc = u @ x_proj_w
        dt = dbc[..., :dt_rank]
        Bm = dbc[..., dt_rank:dt_rank + N]
        Cm = dbc[..., dt_rank + N:]
        delta = jax.nn.softplus(dt @ dt_proj_w + dt_proj_b)
        A = -jnp.exp(A_log)
        y = selective_scan(u, delta, A, Bm, Cm, D)
        y = y * jax.nn.silu(z)
        out = y @ out_proj_w
        return residual + out

    def _L0_ffn_ref(x, gate_w, gate_bias, Wu, bu, Wd, bd, sWu, sbu, sWd, sbd):
        import jax, jax.numpy as jnp
        import numpy as np
        B, S, H, E, K = (2, 512, 512, 8, 2)
        F = 4 * H
        b, s, h = x.shape
        x_flat = x.reshape(-1, h)
        T = x_flat.shape[0]
        scores = jax.nn.sigmoid(x_flat @ gate_w.T + gate_bias)
        top_scores, top_idx = jax.lax.top_k(scores, K)
        top_scores = top_scores / (top_scores.sum(-1, keepdims=True) + 1e-06)
        w = jnp.zeros((T, E), x.dtype).at[jnp.arange(T)[:, None], top_idx].add(top_scores)
        h1 = jnp.einsum('th,efh->etf', x_flat, Wu) + bu[:, None, :]
        a1 = jax.nn.gelu(h1, approximate=False)
        y = jnp.einsum('etf,ehf->eth', a1, Wd) + bd[:, None, :]
        combined = jnp.einsum('te,eth->th', w, y)
        sh = jax.nn.gelu(x_flat @ sWu.T + sbu, approximate=False)
        shared = (sh @ sWd.T + sbd) * 0.1
        return (combined + shared).reshape(b, s, h)

    def _L1_xattn_ref(query, key, value, qpos, kpos, Wq, Wk, Wv, Wo, bo):
        import jax, jax.numpy as jnp
        import numpy as np
        DIM = 512
        NUM_HEADS = 16
        HEAD_DIM = DIM // NUM_HEADS
        SCALE = HEAD_DIM ** (-0.5)
        B, NQ, NK = (4, 1024, 1024)
        Bsz, Nq, C = query.shape
        H, D = (NUM_HEADS, HEAD_DIM)
        q = (query @ Wq.T).reshape(Bsz, Nq, H, D).transpose(0, 2, 1, 3)
        k = (key @ Wk.T).reshape(Bsz, -1, H, D).transpose(0, 2, 1, 3)
        v = (value @ Wv.T).reshape(Bsz, -1, H, D).transpose(0, 2, 1, 3)
        attn = jnp.einsum('bhqd,bhkd->bhqk', q, k) * SCALE
        attn = jax.nn.softmax(attn, axis=-1)
        x = jnp.einsum('bhqk,bhkd->bhqd', attn, v)
        x = x.transpose(0, 2, 1, 3).reshape(Bsz, Nq, C)
        return x @ Wo.T + bo

    def _L1_attn_ref(x, slope_rate, qkvu_w, qkvu_b, out_w, out_b, theta):
        import jax, jax.numpy as jnp
        import numpy as np
        N_EMBD = 512
        N_HEAD = 8
        HEAD_DIM = N_EMBD // N_HEAD
        EPS = 1e-06

        def _lrpe(xh, theta, n):
            idx = jnp.arange(n, dtype=xh.dtype).reshape(1, n, 1)
            th = theta * idx
            th = th[None]
            return jnp.concatenate([xh * jnp.cos(th), xh * jnp.sin(th)], axis=-1)

        def _srmsnorm(y):
            ms = jnp.mean(jnp.square(y), axis=-1, keepdims=True)
            return y * jax.lax.rsqrt(ms + EPS)
        b, n, hd = x.shape
        h = N_HEAD
        qkvu = x @ qkvu_w.T + qkvu_b
        q, k, v, u = jnp.split(qkvu, 4, axis=-1)

        def to_heads(t):
            return t.reshape(b, n, h, hd // h).transpose(0, 2, 1, 3)
        q, k, v = (to_heads(q), to_heads(k), to_heads(v))
        q = jax.nn.silu(q)
        k = jax.nn.silu(k)
        q = _lrpe(q, theta, n)
        k = _lrpe(k, theta, n)
        tril = jnp.tril(jnp.ones((n, n), dtype=x.dtype))
        mask = jnp.exp(slope_rate * tril)
        energy = jnp.einsum('bhne,bhme->bhnm', q, k) * mask[None]
        out = jnp.einsum('bhnm,bhmd->bhnd', energy, v)
        out = out.transpose(0, 2, 1, 3).reshape(b, n, hd)
        out = _srmsnorm(out)
        out = u * out
        out = out @ out_w.T + out_b
        return out

    def _L1_ffn_ref(x, w_qkv, w_o, g1, b1, wg, w1, bb1, w2, bb2, g2, b2):
        import jax, jax.numpy as jnp
        import numpy as np
        B, S, D, H, E, K, F = (1, 512, 512, 16, 8, 2, 2048)

        def layernorm(x, g, b, eps=1e-05):
            m = x.mean(-1, keepdims=True)
            v = ((x - m) ** 2).mean(-1, keepdims=True)
            return (x - m) * jax.lax.rsqrt(v + eps) * g + b
        b, s, d = x.shape
        hd = d // H
        qkv = x @ w_qkv
        q, k, v = jnp.split(qkv, 3, axis=-1)
        to_heads = lambda t: t.reshape(b, s, H, hd).transpose(0, 2, 1, 3)
        q, k, v = (to_heads(q), to_heads(k), to_heads(v))
        scores = jnp.einsum('bhqd,bhkd->bhqk', q, k) / jnp.sqrt(jnp.float32(hd))
        causal = jnp.tril(jnp.ones((s, s), bool))
        scores = jnp.where(causal, scores, jnp.finfo(scores.dtype).min)
        attn = jax.nn.softmax(scores, axis=-1)
        o = jnp.einsum('bhqk,bhkd->bhqd', attn, v)
        o = o.transpose(0, 2, 1, 3).reshape(b, s, d) @ w_o
        h = layernorm(x + o, g1, b1)
        probs = jax.nn.softmax(h @ wg, axis=-1)
        topv, topi = jax.lax.top_k(probs, K)
        topv = topv / topv.sum(-1, keepdims=True)
        w = (topv[..., None] * jax.nn.one_hot(topi, E, dtype=h.dtype)).sum(-2)
        h1 = jax.nn.gelu(jnp.einsum('bsd,edf->ebsf', h, w1) + bb1[:, None, None, :])
        y = jnp.einsum('ebsf,efd->ebsd', h1, w2) + bb2[:, None, None, :]
        moe = jnp.einsum('ebsd,bse->bsd', y, w)
        return layernorm(h + moe, g2, b2)
    x = x + _L0_xattn_ref(ctx_1024, ctx_1024, _layernorm(x, axis=-1), mask_Bx1xSxS2_ik1, L0_xattn_Wv, L0_xattn_Wk, L0_xattn_Wq, L0_xattn_Wo, L0_xattn_bo)
    x = x + _L0_attn_ref(_layernorm(x, axis=-1), L0_attn_in_proj_w, L0_attn_conv_w, L0_attn_conv_b, L0_attn_x_proj_w, L0_attn_dt_proj_w, L0_attn_dt_proj_b, L0_attn_A_log, L0_attn_D, L0_attn_out_proj_w, L0_attn_ln_g, L0_attn_ln_b)
    x = x + _L0_ffn_ref(_layernorm(x, axis=-1), L0_ffn_gate_w, L0_ffn_gate_bias, L0_ffn_Wu, L0_ffn_bu, L0_ffn_Wd, L0_ffn_bd, L0_ffn_sWu, L0_ffn_sbu, L0_ffn_sWd, L0_ffn_sbd)
    x = x + _L1_xattn_ref(_layernorm(x, axis=-1), ctx_1024, ctx_1024, pos_BxS2, pos_BxS2, L1_xattn_Wq, L1_xattn_Wk, L1_xattn_Wv, L1_xattn_Wo, L1_xattn_bo)
    x = x + _L1_attn_ref(_layernorm(x, axis=-1), L1_attn_slope_rate, L1_attn_qkvu_w, L1_attn_qkvu_b, L1_attn_out_w, L1_attn_out_b, L1_attn_theta)
    x = x + _L1_ffn_ref(_layernorm(x, axis=-1), L1_ffn_w_qkv, L1_ffn_w_o, L1_ffn_g1, L1_ffn_b1, L1_ffn_wg, L1_ffn_w1, L1_ffn_bb1, L1_ffn_w2, L1_ffn_bb2, L1_ffn_g2, L1_ffn_b2)
    return x

_drawn_inputs = setup_inputs


def setup_inputs(seed=0):
    import zlib

    import numpy as np

    out = dict(_drawn_inputs(seed))
    spreads = {'L0_attn_conv_b': (0.0, 0.1),
     'L0_attn_D': (1.0, 0.2),
     'L0_attn_ln_g': (1.0, 0.2),
     'L0_attn_ln_b': (0.0, 0.1),
     'L0_ffn_gate_bias': (0.0, 0.1),
     'L0_ffn_bu': (0.0, 0.1),
     'L0_ffn_bd': (0.0, 0.1),
     'L0_ffn_sbu': (0.0, 0.1),
     'L0_ffn_sbd': (0.0, 0.1),
     'L1_xattn_bo': (0.0, 0.1),
     'L1_attn_qkvu_b': (0.0, 0.1),
     'L1_attn_out_b': (0.0, 0.1),
     'L1_ffn_g1': (1.0, 0.2),
     'L1_ffn_b1': (0.0, 0.1),
     'L1_ffn_bb1': (0.0, 0.1),
     'L1_ffn_bb2': (0.0, 0.1),
     'L1_ffn_g2': (1.0, 0.2),
     'L1_ffn_b2': (0.0, 0.1)}
    factors = {}
    for name, (base, spread) in spreads.items():
        noise = np.random.default_rng([zlib.crc32(name.encode()), seed]).standard_normal(out[name].shape)
        drawn = base * np.exp(spread * noise) if base else spread * noise
        out[name] = jnp.asarray(drawn.astype(out[name].dtype))
    for name, factor in factors.items():
        out[name] = (out[name] * factor).astype(out[name].dtype)
    return out
```

```python
from contextlib import ExitStack

import concourse.bass as bass
from concourse import mybir

F32 = mybir.dt.float32
F32R = mybir.dt.float32r
BF16 = mybir.dt.bfloat16
F8 = mybir.dt.float8e4
I32 = mybir.dt.int32
ALU = mybir.AluOpType
ACT = mybir.ActivationFunctionType
AXIS_X = mybir.AxisListType.X

P = 128
T = 512
D = 512
S2 = 8192
TT = T // P
DT = D // P
H = 16
DH = D // H
E = 8
FF = 2048
BIG = 2.0 ** 67
NEG_BIG = -BIG

KC = 1024
NKC = S2 // KC
KRING = NKC + 2
KT = S2 // P
PAIRS = KT // 2
QROWS = 3 * DH

DIN = 1024
NST = 16
DTR = 32
GT = DIN // P

LH = 8
LD = D // LH

FU = 4
NU = FF // (FU * P)


class EngineQueues:

    NAMES = ("pe", "act", "dve", "pool", "sp")

    def __init__(self, nc, ctx):
        self.nc = nc
        self.sem = {n: ctx.enter_context(nc.semaphore("s_" + n)) for n in self.NAMES}
        self.count = {n: 0 for n in self.NAMES}
        self.dma_count = {}
        self.items = {n: [] for n in self.NAMES}
        self.waited = {n: {} for n in self.NAMES}
        self.stores = {}

    def wait(self, eng, *after):
        for token in after:
            if token is None:
                continue
            name, sem, value = token
            if self.waited[eng].get(name, 0) < value:
                self.waited[eng][name] = value
                self.items[eng].append(("wait", sem, value))

    def do(self, eng, fn, *after, sig=True):
        self.wait(eng, *after)
        if sig:
            self.count[eng] += 1
            self.items[eng].append(("op", fn, self.sem[eng], 1))
            return (eng, self.sem[eng], self.count[eng])
        self.items[eng].append(("op", fn, None, 0))
        return None

    def dma(self, eng, out, in_, sem, *after, store=False):
        self.wait(eng, *after)
        name = sem.name
        self.dma_count[name] = self.dma_count.get(name, 0) + 16
        self.items[eng].append(("op", lambda e: e.dma_start(out, in_), sem, 16))
        token = (name, sem, self.dma_count[name])
        if store:
            self.stores[name] = token
        return token

    def emit(self):
        items, self.items = self.items, {n: [] for n in self.NAMES}
        with self.nc.Block() as block:
            for name, where in (("sp", block.sync), ("pe", block.tensor), ("act", block.scalar),
                                ("dve", block.vector), ("pool", block.gpsimd)):
                if not items[name]:
                    continue

                def run(eng, todo=items[name]):
                    for item in todo:
                        if item[0] == "wait":
                            eng.wait_ge(item[1], item[2])
                        else:
                            ins = item[1](eng)
                            if item[2] is not None:
                                ins.then_inc(item[2], item[3])

                where(run)


class Bank:

    def __init__(self, tensor):
        self.t = tensor
        self.free = None


class Kernel:
    def __init__(self, nc, ins, out, ctx):
        self.nc = nc
        self.i = ins
        self.out = out
        self.ctx = ctx
        self.q = EngineQueues(nc, ctx)
        self.nsem = 0
        self.last_pool = None
        self.ntmp = 0
        sb = self.sbuf
        self.ident = sb(ctx, "ident", [P, P], F32)
        self.ident_big = sb(ctx, "ident_big", [P, P], BF16)
        self.ones = sb(ctx, "ones", [P, P], F32)
        self.x = sb(ctx, "x", [P, TT, D], F32)
        self.xnT = sb(ctx, "xnT", [P, DT, T], F32)
        self.x_ready = None
        self.psum = ctx.enter_context(nc.psum_tensor("psum", [P, 8, 512], F32))
        self.banks = [Bank(self.psum[:, i, :]) for i in range(8)]

    def sbuf(self, ctx, name, shape, dt):
        self.ntmp += 1
        return ctx.enter_context(self.nc.sbuf_tensor(f"{name}_{self.ntmp}", shape, dt))

    def sem(self, name):
        self.nsem += 1
        return self.ctx.enter_context(self.nc.semaphore(f"{name}_{self.nsem}"))

    def pe(self, fn, *after, sig=False):
        return self.q.do("pe", fn, *after, sig=sig)

    def act(self, fn, *after, sig=True):
        return self.q.do("act", fn, *after, sig=sig)

    def dve(self, fn, *after, sig=True):
        return self.q.do("dve", fn, *after, sig=sig)

    def pool(self, fn, *after):
        self.last_pool = self.q.do("pool", fn, *after, self.last_pool)
        return self.last_pool

    def load(self, out, in_, sem, *after, eng="sp"):
        return self.q.dma(eng, out, in_, sem, *after)

    def store(self, out, in_, sem, *after, eng="sp"):
        return self.q.dma(eng, out, in_, sem, *after, store=True)

    def gather(self, out, terms, *after, sig=True, start=True, stop=True):
        token = None
        for n, (lhsT, rhs) in enumerate(terms):
            last = n == len(terms) - 1
            token = self.pe(lambda e, a=lhsT, b=rhs, s=start and n == 0, z=stop and last:
                            e.matmul(out, a, b, start=s, stop=z), *(after if n == 0 else ()), sig=last and sig)
        return token

    def split(self, hi, lo, src, *after, hi_on="dve"):
        if hi_on == "act":
            t_hi = self.act(lambda e: e.activation(hi, src, ACT.Copy), *after)
        else:
            t_hi = self.dve(lambda e: e.tensor_copy(hi, src), *after)
        t_lo = self.dve(lambda e: e.tensor_tensor(lo, src, hi.bitcast(F32), ALU.subtract), t_hi, *after)
        return t_hi, t_lo

    def constants(self):
        zero = self.pool(lambda e: e.memset(self.ident[:], 0.0))
        self.pool(lambda e: e.affine_select(out=self.ident[:], in_=self.ident[:], compare_op=ALU.not_equal,
                                            fill=1.0, base=0, pattern=[[-1, P]], channel_multiplier=1), zero)
        zero = self.pool(lambda e: e.memset(self.ident_big[:], 0.0))
        self.pool(lambda e: e.affine_select(out=self.ident_big[:], in_=self.ident_big[:],
                                            compare_op=ALU.not_equal, fill=BIG, base=0, pattern=[[-1, P]],
                                            channel_multiplier=1), zero)
        self.pool(lambda e: e.memset(self.ones[:], 1.0))
        self.q.wait("sp", self.load(self.x[:], self.i["x"].rearrange("o (i p) d -> p (o i) d", p=P),
                                    self.sem("s_x")))

    def finish(self):
        self.store(self.out.rearrange("o (i p) d -> p (o i) d", p=P), self.x[:], self.sem("s_out"))
        self.q.wait("sp", *self.q.stores.values())
        self.q.emit()

    def layernorm(self, ctx, dst, src, *after):
        stats = self.sbuf(ctx, "ln_stats", [P, TT, 6], F32)
        mv = self.sbuf(ctx, "ln_mean_var", [P, TT, 2], F32)
        rstd = self.sbuf(ctx, "ln_rstd", [P, TT], F32)
        for i in range(TT):
            st = self.dve(lambda e, i=i: e.bn_stats(stats[:, i, :], src[:, i, :]), *after)
            agg = self.dve(lambda e, i=i: e.bn_aggr(mv[:, i, :], stats[:, i, :]), st)
        eps = self.dve(lambda e: e.tensor_scalar(rstd[:], mv[:, :, 1], 1e-5, None, ALU.add), agg)
        root = self.act(lambda e: e.activation(rstd[:], rstd[:], ACT.Sqrt), eps)
        rec = self.dve(lambda e: e.reciprocal(rstd[:], rstd[:]), root)
        for i in range(TT):
            done = self.dve(lambda e, i=i: e.tensor_scalar(dst[:, i, :], src[:, i, :], mv[:, i, 0:1],
                                                           rstd[:, i:i + 1], ALU.subtract, ALU.mult), rec)
        return done

    def transpose_all(self, dstT, src, *after, gain=None):
        for c in range(DT):
            bank = self.banks[c % 2]
            for i in range(TT):
                tr = self.pe(lambda e, b=bank, c=c, i=i: e.transpose(
                    b.t[:, i * P:(i + 1) * P], src[:, i, c * P:(c + 1) * P], self.ident[:]),
                    *after, bank.free, sig=i == TT - 1)
            if gain is None:
                bank.free = self.dve(lambda e, b=bank, c=c: e.tensor_copy(dstT[:, c, :], b.t[:]), tr)
            else:
                bank.free = self.dve(lambda e, b=bank, c=c: e.tensor_scalar(
                    dstT[:, c, :], b.t[:], gain[0][:, c:c + 1], gain[1][:, c:c + 1], ALU.mult, ALU.add), tr)
        return bank.free

    def normalized_T(self, ctx, *after):
        xn = self.sbuf(ctx, "xn", [P, TT, D], F32)
        done = self.layernorm(ctx, xn, self.x, *after)
        return self.transpose_all(self.xnT, xn, done), xn

    def project_residual(self, lhsT, w, bias_row, kt, *after, first_bank=0):
        for i in range(TT):
            bank = self.banks[first_bank + i]
            terms = [(lhsT[:, k, i * P:(i + 1) * P], w[:, k, :]) for k in range(kt)]
            if bias_row is not None:
                terms.append((self.ones[0:1, :], bias_row))
            tok = self.gather(bank.t[:], terms, *after, bank.free)
            bank.free = self.dve(lambda e, b=bank, i=i: e.tensor_tensor(
                self.x[:, i, :], self.x[:, i, :], b.t[:], ALU.add), tok)
        return bank.free

    def prepare_context(self):
        nc, i = self.nc, self.i
        self.k0 = [nc.dram_tensor(f"k0_{n}", [D, S2], F32, kind="Internal").ap() for n in ("hi", "lo")]
        self.k1 = [nc.dram_tensor(f"k1_{n}", [D, S2], F32, kind="Internal").ap() for n in ("hi", "lo")]
        self.v1 = nc.dram_tensor("v1_heads", [H, P, KT * DH], F32, kind="Internal").ap()
        CH = 512
        VT = CH // P
        with ExitStack() as ctx:
            wraw = self.sbuf(ctx, "w_raw", [P, DT, D], F32)
            wk = [self.sbuf(ctx, f"wk{n}", [P, DT, D], F32R) for n in ("hi", "lo")]
            wv = [self.sbuf(ctx, f"wv{n}", [P, DT, D], F32R) for n in ("hi", "lo")]
            raw = [self.sbuf(ctx, "ctxT", [P, DT, CH], F32) for _ in range(2)]
            cx = [[self.sbuf(ctx, f"ctx{n}", [P, DT, CH], F32R) for n in ("hi", "lo")] for _ in range(2)]
            kst = [[self.sbuf(ctx, f"k1{n}", [P, DT, CH], F32R) for n in ("hi", "lo")] for _ in range(2)]
            vst = [self.sbuf(ctx, "v1", [P, H, VT, DH], F32) for _ in range(2)]
            s_w = self.sem("s_ctxw")
            s_raw = [self.sem("s_raw") for _ in range(2)]
            s_out = [self.sem("s_ctxout") for _ in range(2)]
            free = None
            for name, parts in (("L1_xattn_WkT", wk), ("L1_xattn_WvT", wv)):
                ld = self.load(wraw[:], i[name].rearrange("(k p) n -> p k n", p=P), s_w, free)
                _, free = self.split(parts[0][:], parts[1][:], wraw[:], ld)
            w_ready = free
            raw_free = [None, None]
            cx_free = [(), ()]
            st_free = [None, None]
            ctxT = i["ctxT"].rearrange("(k p) n -> p k n", p=P)
            for s in range(S2 // CH):
                b = s % 2
                cols = slice(s * CH, (s + 1) * CH)
                ld = self.load(raw[b][:], ctxT[:, :, cols], s_raw[b], raw_free[b])
                _, raw_free[b] = self.split(cx[b][0][:], cx[b][1][:], raw[b][:], ld, *cx_free[b])
                split_done = raw_free[b]
                for m in range(DT):
                    bank = self.banks[m]
                    rows = slice(m * P, (m + 1) * P)
                    tok = self.gather(bank.t[:], [
                        (wk[a][:, k, rows], cx[b][c][:, k, :])
                        for k in range(DT) for a, c in ((0, 0), (0, 1), (1, 0))], split_done, w_ready, bank.free)
                    _, bank.free = self.split(kst[b][0][:, m, :], kst[b][1][:, m, :], bank.t[:], tok,
                                              st_free[b], hi_on="act")
                k_done = bank.free
                for t in range(VT):
                    bank = self.banks[4 + t]
                    rows = slice(t * P, (t + 1) * P)
                    tok = self.gather(bank.t[:], [
                        (cx[b][c][:, k, rows], wv[a][:, k, :])
                        for k in range(DT) for a, c in ((0, 0), (0, 1), (1, 0))], bank.free)
                    bank.free = self.act(lambda e, bank=bank, b=b, t=t: e.activation(
                        vst[b][:, :, t, :], bank.t[:].rearrange("p (h d) -> p h d", h=H), ACT.Copy),
                        tok, st_free[b])
                st = None
                for n in range(2):
                    self.store(self.k0[n].rearrange("(k p) n -> p k n", p=P)[:, :, cols], cx[b][n][:].bitcast(F32),
                               s_out[b], split_done)
                for n in range(2):
                    self.store(self.k1[n].rearrange("(k p) n -> p k n", p=P)[:, :, cols], kst[b][n][:].bitcast(F32),
                               s_out[b], k_done)
                st = self.store(self.v1.rearrange("h p n -> p h n")[:, :, s * VT * DH:(s + 1) * VT * DH],
                                vst[b][:].rearrange("p h t d -> p h (t d)"), s_out[b], bank.free)
                cx_free[b] = (tok, st)
                st_free[b] = st
            self.q.wait("sp", st_free[0], st_free[1])
            self.q.emit()

    def build_masks(self, ctx):
        mask_q = self.sbuf(ctx, "mask_q", [P, TT, S2], BF16)
        mask_k = self.sbuf(ctx, "mask_k", [P, KT, T], F8)
        CH = 4096
        with ExitStack() as tmp:
            raw = [self.sbuf(tmp, "mask_raw", [P, CH], I32) for _ in range(4)]
            sems = [self.sem("s_mask") for _ in range(4)]
            free = [None] * 4
            srcq = self.i["mask"].rearrange("(i p) k -> p i k", p=P)
            srck = self.i["maskT"].rearrange("(i p) q -> p i q", p=P)
            n = 0
            for i in range(TT):
                for c in range(S2 // CH):
                    b = n % 4
                    ld = self.load(raw[b][:], srcq[:, i, c * CH:(c + 1) * CH], sems[b], free[b])
                    free[b] = self.dve(lambda e, i=i, c=c, b=b: e.tensor_scalar(
                        mask_q[:, i, c * CH:(c + 1) * CH], raw[b][:], 0, NEG_BIG, ALU.is_equal, ALU.mult), ld)
                    n += 1
            per = CH // T
            for c in range(KT // per):
                b = n % 4
                ld = self.load(raw[b][:].rearrange("p (k q) -> p k q", q=T), srck[:, c * per:(c + 1) * per, :],
                               sems[b], free[b])
                free[b] = self.dve(lambda e, c=c, b=b: e.tensor_scalar(
                    mask_k[:, c * per:(c + 1) * per, :], raw[b][:].rearrange("p (k q) -> p k q", q=T),
                    0, -1.0, ALU.is_equal, ALU.mult, saturate=False), ld)
                n += 1
            self.q.emit()
        return mask_q, mask_k

    def cross_attention(self, ctx, k_hi_lo, v_heads, emit_query, comb, scale, masks, attT, ready):
        q_stack = [self.sbuf(ctx, "q_stack", [QROWS + 2, T], F32R) for _ in range(2)]
        k_ring = self.sbuf(ctx, "k_ring", [QROWS + 2, KRING, KC], F32R)
        v_raw = self.sbuf(ctx, "v_raw", [P, KT * DH], F32)
        v_one = [self.sbuf(ctx, "v_one", [P, KT, DH + 1], F32) for _ in range(2)]
        prob = [self.sbuf(ctx, "prob", [P, 2, T], F32) for _ in range(2)]
        trash = [self.sbuf(ctx, "max_trash", [P, 512], BF16) for _ in range(2)]
        row_max = [self.sbuf(ctx, "row_max", [P, TT, S2 // 512], F32) for _ in range(2)]
        top = self.sbuf(ctx, "row_top", [P, TT], F32)
        top2 = self.sbuf(ctx, "row_top2", [P, TT, 2], F32)
        m_hi = self.sbuf(ctx, "m_hi", [QROWS + 2, T], F32R)
        lo_sign = self.sbuf(ctx, "lo_sign", [QROWS + 2, 1], F32)
        o_sb = self.sbuf(ctx, "o_sb", [97, T], F32)
        rden = self.sbuf(ctx, "rden", [P, T], F32)
        den_sel = self.sbuf(ctx, "den_sel", [97, DH], F32)
        s_k = [self.sem("s_k") for _ in range(KRING)]
        s_v = self.sem("s_v")
        ring_init = self.pool(lambda e: e.memset(k_ring[QROWS:QROWS + 2, :, :].bitcast(F32), -1.0))
        for b in range(2):
            ring_init = self.pool(lambda e, b=b: e.memset(v_one[b][:, :, DH:DH + 1], 1.0))
        z = self.pool(lambda e: e.memset(o_sb[:], 0.0))
        sgn = self.pool(lambda e: e.memset(lo_sign[QROWS:QROWS + 2, :], -1.0), z)
        sgn = self.pool(lambda e: e.memset(lo_sign[QROWS:QROWS + 1, :], 0.0), sgn)
        z = self.pool(lambda e: e.memset(den_sel[:], 0.0))
        z = self.pool(lambda e: e.memset(den_sel[32:33, :], 1.0), z)
        consts = self.pool(lambda e: e.memset(den_sel[96:97, :], 1.0), z)

        score = [(self.banks[0], self.banks[1]), (self.banks[2], self.banks[3])]
        maxbank = [self.banks[4], self.banks[5]]
        vbank, misc = self.banks[6], self.banks[7]

        k_loaded, k_used = {}, {}
        v_loaded = {}
        v_ready, v_used = {}, {}
        q_ready, m_ready = {}, {}
        state = {"vraw_free": None, "top_read": None, "o_read": None}

        def load_k(n):
            h, c = divmod(n, NKC)
            if h >= H:
                return
            slot = n % KRING
            rows, cols = slice(h * DH, (h + 1) * DH), slice(c * KC, (c + 1) * KC)
            for g, part in enumerate((0, 0, 1)):
                k_loaded[n] = self.load(k_ring[g * DH:(g + 1) * DH, slot, :].bitcast(F32), k_hi_lo[part][rows, cols],
                                        s_k[slot], k_used.get(n - KRING))

        def load_v(h):
            if h >= H:
                return
            v_loaded[h] = self.load(v_raw[:], v_heads[h], s_v, state["vraw_free"])
            v_ready[h] = state["vraw_free"] = self.pool(lambda e, h=h: e.tensor_copy(
                v_one[h % 2][:, :, 0:DH], v_raw[:].rearrange("p (k d) -> p k d", d=DH)),
                v_loaded[h], v_used.get(h - 2))

        def query(h):
            tok = emit_query(h, misc.t[0:QROWS, :], ready, misc.free)
            qs = q_stack[h % 2]
            hi = self.dve(lambda e: e.tensor_copy(qs[0:QROWS, :], misc.t[0:QROWS, :]), tok, v_used.get(h - 2))
            misc.free = q_ready[h] = self.dve(lambda e: e.tensor_tensor(
                qs[DH:2 * DH, :], misc.t[DH:2 * DH, :], qs[DH:2 * DH, :].bitcast(F32), ALU.subtract), hi)

        def max_step(h, n):
            chunk, i = divmod(n, TT)
            bank = maxbank[n % 2]
            number = h * NKC + chunk * 512 // KC
            off = chunk * 512 % KC
            tok = self.gather(bank.t[:], [(q_stack[h % 2][0:QROWS, i * P:(i + 1) * P],
                                           k_ring[0:QROWS, number % KRING, off:off + 512])],
                              q_ready[h], k_loaded[number], bank.free)
            out = row_max[h % 2][:, i, chunk:chunk + 1]
            if masks is None:
                bank.free = self.dve(lambda e: e.reduce_max(out, bank.t[:], AXIS_X), tok)
            else:
                bank.free = self.dve(lambda e: e.tensor_tensor_reduce(
                    out=trash[n % 2][:], in0=bank.t[:], in1=masks[0][:, i, chunk * 512:(chunk + 1) * 512], scale=1.0,
                    scalar=-3.0e38, op0=ALU.add, op1=ALU.max, accum_out=out), tok, bank.free)

        def max_rows(h):
            t = self.dve(lambda e: e.tensor_reduce(top[:], row_max[h % 2][:], AXIS_X, ALU.max),
                         maxbank[0].free, maxbank[1].free, state["top_read"])
            t = self.dve(lambda e: e.tensor_copy(top2[:, :, 0:1], top[:].unsqueeze(2)), t, state["top_read"])
            t = self.dve(lambda e: e.tensor_copy(top2[:, :, 1:2], top[:].unsqueeze(2)), t)
            for i in range(TT):
                tok = self.pe(lambda e, i=i: e.matmul(misc.t[QROWS:QROWS + 2, i * P:(i + 1) * P], top2[:, i, :],
                                                      self.ident[:], start=True, stop=True),
                              t, misc.free, sig=i == TT - 1)
            state["top_read"] = tok
            rows = slice(QROWS, QROWS + 2)
            hi = self.dve(lambda e: e.tensor_copy(m_hi[rows, :], misc.t[rows, :]), tok)
            misc.free = m_ready[h] = self.dve(lambda e: e.scalar_tensor_tensor(
                out=q_stack[h % 2][rows, :], in0=m_hi[rows, :].bitcast(F32), scalar=lo_sign[rows, :],
                in1=misc.t[rows, :], op0=ALU.mult, op1=ALU.add), hi, consts, v_used.get(h - 2))

        def score_step(h, p):
            banks = score[p % 2]
            for j in range(2):
                kt = 2 * p + j
                number = h * NKC + kt * P // KC
                off = kt * P % KC
                after = (m_ready[h], k_loaded[number], banks[0].free, ring_init)
                if masks is not None:
                    self.pe(lambda e, j=j, kt=kt: e.matmul(banks[j].t[:], self.ident_big[:], masks[1][:, kt, :],
                                                           start=True, stop=False), *after)
                tok = self.pe(lambda e, j=j, n=number, off=off: e.matmul(
                    banks[j].t[:], k_ring[:, n % KRING, off:off + P], q_stack[h % 2][:],
                    start=masks is None, stop=True), *after, sig=True)
                if (kt + 1) * P % KC == 0:
                    k_used[number] = tok
            first = 2 * (p % 2)
            banks[0].free = exp_done[p % 2] = self.act(lambda e: e.activation(
                prob[p % 2][:], self.psum[:, first:first + 2, :], ACT.Exp, scale=scale), tok, prob_free[p % 2])

        prob_free = [None, None]
        exp_done = [None, None]

        def value_step(h, p):
            for j in range(2):
                tok = self.pe(lambda e, j=j: e.matmul(
                    vbank.t[64 * j:64 * j + DH + 1, :], v_one[h % 2][:, 2 * p + j, :], prob[p % 2][:, j, :],
                    start=p == 0, stop=p == PAIRS - 1, skip_group_check=True),
                    exp_done[p % 2], v_ready[h], vbank.free, sig=j == 1)
            prob_free[p % 2] = tok
            if p == PAIRS - 1:
                v_used[h] = tok

        def take_values(h):
            a = self.dve(lambda e: e.tensor_copy(o_sb[0:DH + 1, :], vbank.t[0:DH + 1, :]), v_used[h], consts,
                         state["o_read"])
            vbank.free = self.dve(lambda e: e.tensor_copy(o_sb[64:97, :], vbank.t[64:97, :]), a)
            return vbank.free

        def head_out(h, taken):
            g = slice(DH * (h % 4), DH * (h % 4) + DH)
            tok = self.pe(lambda e: e.matmul(misc.t[g, :], den_sel[:], o_sb[:], start=True, stop=True),
                          taken, misc.free, sig=True)
            rec = self.dve(lambda e: e.reciprocal(rden[g, :], misc.t[g, :]), tok)
            tok = self.pe(lambda e: e.matmul(misc.t[g, :], comb, o_sb[:], start=True, stop=True), rec, sig=True)
            state["o_read"] = tok
            misc.free = self.dve(lambda e: e.tensor_tensor(attT[g, h // 4, :], misc.t[g, :], rden[g, :],
                                                           ALU.mult), tok, rec)

        for n in range(KRING):
            load_k(n)
        load_v(0)
        query(0)
        n_max = TT * (S2 // 512)
        for n in range(n_max):
            max_step(0, n)
        max_rows(0)
        taken = None
        spread = PAIRS - 4
        for h in range(H):
            load_v(h + 1)
            if h + 1 < H:
                query(h + 1)
            done = 0
            for p in range(PAIRS):
                score_step(h, p)
                if (2 * p + 2) * P % KC == 0:
                    load_k(h * NKC + 2 * p * P // KC + KRING)
                if p > 0:
                    value_step(h, p - 1)
                if p == 2 and h > 0:
                    head_out(h - 1, taken)
                if h + 1 < H:
                    want = min(n_max, n_max * (p + 1) // spread)
                    while done < want:
                        max_step(h + 1, done)
                        done += 1
                    if p == spread + 1:
                        max_rows(h + 1)
            value_step(h, PAIRS - 1)
            taken = take_values(h)
        head_out(H - 1, taken)
        return misc.free

    def output_projection(self, attT, w_name, b_name):
        with ExitStack() as ctx:
            w = self.sbuf(ctx, "wo", [P, DT, D], F32)
            b = self.sbuf(ctx, "bo", [1, D], F32)
            s = self.sem("s_wo")
            self.load(w[:], self.i[w_name].rearrange("(k p) n -> p k n", p=P), s)
            ld = self.load(b[:], self.i[b_name].rearrange("(o n) -> o n", o=1), s)
            self.project_residual(attT, w, b[:], DT, ld)
            self.q.emit()

    def l0_cross(self):
        with ExitStack() as outer:
            attT = self.sbuf(outer, "attT", [P, DT, T], F32)
            with ExitStack() as ctx:
                m4 = self.sbuf(ctx, "m4", [P, QROWS], F32)
                comb = self.sbuf(ctx, "comb", [97, DH], F32)
                with ExitStack() as tmp:
                    wq = self.sbuf(tmp, "wq", [DH, DH], F32)
                    wk = self.sbuf(tmp, "wk", [DH, DH], F32)
                    s = self.sem("s_l0w")
                    z = self.pool(lambda e: e.memset(comb[:], 0.0))
                    self.load(wq[:], self.i["L0_xattn_Wq"], s)
                    self.load(wk[:], self.i["L0_xattn_Wk"], s)
                    self.load(comb[0:DH, :], self.i["L0_xattn_WvT"], s, z)
                    ld = self.load(comb[64:64 + DH, :], self.i["L0_xattn_WvT"], s)
                    bank = self.banks[7]
                    for g in range(4):
                        for r in range(3):
                            tok = self.pe(lambda e, g=g, r=r: e.matmul(
                                bank.t[DH * g:DH * (g + 1), DH * r:DH * (r + 1)], wq[:], wk[:], start=True,
                                stop=True), ld, bank.free, sig=True)
                    self.dve(lambda e: e.tensor_copy(m4[:], bank.t[:, 0:QROWS]), tok)
                    self.normalized_T(tmp)
                    self.q.emit()
                masks = self.build_masks(ctx)

                def emit_query(h, out, *after):
                    rows = slice(DH * (h % 4), DH * (h % 4) + DH)
                    return self.gather(out, [(m4[rows, :], self.xnT[rows, h // 4, :])], *after)

                self.cross_attention(ctx, self.k0, self.i["ctx_heads"], emit_query, comb[:], D ** -0.5, masks,
                                     attT, None)
                self.q.emit()
            self.output_projection(attT, "L0_xattn_WoT", "L0_xattn_bo")

    def l1_cross(self):
        with ExitStack() as outer:
            attT = self.sbuf(outer, "attT", [P, DT, T], F32)
            with ExitStack() as ctx:
                wq = self.sbuf(ctx, "wq3", [P, DT, H * QROWS], F32)
                comb = self.sbuf(ctx, "comb", [97, DH], F32)
                with ExitStack() as tmp:
                    wq_loaded = self.load(wq[:], self.i["L1_xattn_WqT3"].rearrange("(k p) n -> p k n", p=P),
                                          self.sem("s_wq3"))
                    z = self.pool(lambda e: e.memset(comb[:], 0.0))
                    z = self.pool(lambda e: e.tensor_copy(comb[0:DH, :], self.ident[0:DH, 0:DH]), z)
                    self.pool(lambda e: e.tensor_copy(comb[64:64 + DH, :], self.ident[64:64 + DH, 64:64 + DH]), z)
                    self.normalized_T(tmp)
                    self.q.emit()

                def emit_query(h, out, *after):
                    cols = slice(h * QROWS, (h + 1) * QROWS)
                    return self.gather(out, [(wq[:, k, cols], self.xnT[:, k, :]) for k in range(DT)], *after,
                                       wq_loaded)

                self.cross_attention(ctx, self.k1, self.v1, emit_query, comb[:], DH ** -0.5, None, attT, None)
                self.q.emit()
            self.output_projection(attT, "L1_xattn_WoT", "L1_xattn_bo")

    def l0_scan(self):
        with ExitStack() as outer:
            u = self.sbuf(outer, "u", [P, GT, T], F32)
            zs = self.sbuf(outer, "z_silu", [P, GT, T], F32)
            with ExitStack() as ctx:
                w = self.sbuf(ctx, "in_proj", [P, DT, 2 * DIN], F32)
                xn = self.sbuf(ctx, "xn", [P, TT, D], F32)
                xm = self.sbuf(ctx, "xm", [P, TT, D], F32)
                col = self.sbuf(ctx, "ln_gb", [P, 2, DT], F32)
                cw = self.sbuf(ctx, "conv_w", [P, GT, 4], F32)
                cb = self.sbuf(ctx, "conv_b", [P, GT], F32)
                PAD = 3
                up = [self.sbuf(ctx, "u_pad", [P, PAD + T], F32) for _ in range(3)]
                s_w, s_c = self.sem("s_inw"), self.sem("s_cols")
                ld_w = self.load(w[:], self.i["L0_attn_in_proj_w"].rearrange("(k p) n -> p k n", p=P), s_w)
                self.load(col[:, 0, :], self.i["L0_attn_ln_gC"], s_c)
                self.load(col[:, 1, :], self.i["L0_attn_ln_bC"], s_c)
                self.load(cw[:], self.i["L0_attn_conv_w"].rearrange("(k p) n -> p k n", p=P), s_c)
                ld_c = self.load(cb[:], self.i["L0_attn_conv_bC"], s_c)
                done = self.layernorm(ctx, xn, self.x)
                for i in range(TT):
                    self.dve(lambda e, i=i: e.tensor_tensor(self.x[:, i, :], self.x[:, i, :], xn[:, i, :],
                                                            ALU.add), done)
                done = self.layernorm(ctx, xm, xn, done)
                ready = self.transpose_all(self.xnT, xm, done, ld_c, gain=(col[:, 0, :], col[:, 1, :]))
                up_free = [None] * 3
                pads = [self.pool(lambda e, b=b: e.memset(up[b][:, 0:PAD], 0.0)) for b in range(3)]
                for m in range(2 * GT):
                    bank = self.banks[2 + m % 4]
                    tok = self.gather(bank.t[:], [(w[:, k, m * P:(m + 1) * P], self.xnT[:, k, :])
                                                  for k in range(DT)], ready, ld_w, bank.free)
                    if m >= GT:
                        bank.free = self.act(lambda e, b=bank, m=m: e.activation(zs[:, m - GT, :], b.t[:],
                                                                                 ACT.Silu), tok)
                        continue
                    b = m % 3
                    bank.free = c = self.act(lambda e, k=bank, b=b: e.activation(up[b][:, PAD:], k.t[:], ACT.Copy),
                                             tok, up_free[b])
                    for j in range(4):
                        if j == 0:
                            c = self.dve(lambda e, b=b, m=m: e.tensor_scalar(
                                u[:, m, :], up[b][:, 0:T], cw[:, m, 0:1], None, ALU.mult), c, pads[b], ld_c)
                        else:
                            c = self.dve(lambda e, b=b, m=m, j=j: e.scalar_tensor_tensor(
                                out=u[:, m, :], in0=up[b][:, j:j + T], scalar=cw[:, m, j:j + 1],
                                in1=u[:, m, :], op0=ALU.mult, op1=ALU.add), c)
                    up_free[b] = c
                    self.act(lambda e, m=m: e.activation(u[:, m, :], u[:, m, :], ACT.Silu, bias=cb[:, m:m + 1]), c)
                self.q.emit()
            NH = 4
            with ExitStack() as ctx:
                delta = self.sbuf(ctx, "delta", [P, GT, T], F32)
                du = self.sbuf(ctx, "delta_u", [P, GT, T], F32)
                bc = [self.sbuf(ctx, f"{n}_all", [P, NST, T], F32) for n in "BC"]
                xp = self.sbuf(ctx, "x_proj", [P, GT, DTR + 2 * NST], F32)
                dtw = self.sbuf(ctx, "dt_proj", [DTR, DIN], F32)
                dtb = self.sbuf(ctx, "dt_bias", [P, GT], F32)
                dcol = self.sbuf(ctx, "D_col", [P, GT], F32)
                a = self.sbuf(ctx, "A", [P, GT, NST], F32)
                dbc = self.sbuf(ctx, "dbc", [DTR + 2 * NST, T], F32)
                with ExitStack() as tmp:
                    sel = self.sbuf(tmp, "row_select", [DTR + 2 * NST, 2 * NST, P], F32)
                    mag = self.sbuf(tmp, "minus_abs", [P, GT, T], F32)
                    s = self.sem("s_scanw")
                    self.load(xp[:], self.i["L0_attn_x_proj_w"].rearrange("(k p) n -> p k n", p=P), s)
                    self.load(dtw[:], self.i["L0_attn_dt_proj_w"], s)
                    self.load(dtb[:], self.i["L0_attn_dt_proj_bC"], s)
                    self.load(dcol[:], self.i["L0_attn_DC"], s)
                    ld = self.load(a[:], self.i["L0_attn_A_log"].rearrange("(k p) n -> p k n", p=P), s)
                    ea = self.act(lambda e: e.activation(a[:], a[:], ACT.Exp), ld)
                    self.dve(lambda e: e.tensor_scalar(a[:], a[:], -1.0, None, ALU.mult), ea)
                    rows = DTR + 2 * NST
                    t_sel = self.dve(lambda e: e.tensor_copy(
                        sel[:], self.ident[0:rows, DTR:rows].unsqueeze(2).to_broadcast([rows, 2 * NST, P])))
                    bank = self.banks[0]
                    tok = self.gather(bank.t[0:rows, :], [(xp[:, m, :], u[:, m, :]) for m in range(GT)],
                                      ld, bank.free)
                    t_dbc = bank.free = self.dve(lambda e, b=bank: e.tensor_copy(dbc[:], b.t[0:rows, :]), tok)
                    for m in range(GT):
                        bank = self.banks[1 + m % 2]
                        tok = self.gather(bank.t[:], [(dtw[:, m * P:(m + 1) * P], dbc[0:DTR, :])], t_dbc,
                                          bank.free)
                        bank.free = pre = self.dve(lambda e, b=bank, m=m: e.tensor_scalar(
                            delta[:, m, :], b.t[:], dtb[:, m:m + 1], None, ALU.add), tok)
                    ab = self.act(lambda e: e.activation(mag[:], delta[:], ACT.Abs), pre)
                    ex = self.act(lambda e: e.activation(mag[:], mag[:], ACT.Exp, scale=-1.0), ab)
                    ln = self.act(lambda e: e.activation(mag[:], mag[:], ACT.Ln, bias=1.0), ex)
                    for m in range(GT):
                        d = self.dve(lambda e, m=m: e.scalar_tensor_tensor(
                            out=delta[:, m, :], in0=delta[:, m, :], scalar=0.0, in1=mag[:, m, :], op0=ALU.max,
                            op1=ALU.add), ln)
                        self.dve(lambda e, m=m: e.tensor_tensor(du[:, m, :], delta[:, m, :], u[:, m, :],
                                                                ALU.mult), d)
                    for n in range(2 * NST):
                        bank = self.banks[3 + n % 4]
                        tok = self.gather(bank.t[:], [(sel[:, n, :], dbc[:])], t_sel, t_dbc, bank.free)
                        bank.free = self.act(lambda e, b=bank, n=n: e.activation(
                            bc[n // NST][:, n % NST, :], b.t[:], ACT.Copy), tok)
                    self.q.emit()
                with ExitStack() as tmp:
                    da = [self.sbuf(tmp, "dA", [P, NH, T], F32) for _ in range(2)]
                    db = [self.sbuf(tmp, "dB_u", [P, NH, T], F32) for _ in range(2)]
                    da_free, db_free = [None, None], [None, None]
                    for m in range(GT):
                        ybank = self.banks[m % 2]
                        for g in range(NST // NH):
                            b = g % 2
                            for j in range(NH):
                                n = g * NH + j
                                t_a = self.act(lambda e, b=b, j=j, m=m, n=n: e.activation(
                                    da[b][:, j, :], delta[:, m, :], ACT.Exp, scale=a[:, m, n:n + 1]), da_free[b])
                            t_a = self.dve(lambda e, b=b: e.memset(da[b][:, :, 0:1], 0.0), t_a)
                            t_b = self.pool(lambda e, b=b, m=m, g=g: e.tensor_tensor(
                                db[b][:], du[:, m, :].unsqueeze(1).to_broadcast([P, NH, T]),
                                bc[0][:, g * NH:(g + 1) * NH, :], ALU.mult), db_free[b])
                            t_h = da_free[b] = self.dve(lambda e, b=b: e.tensor_tensor_scan(
                                out=db[b][:].rearrange("p n t -> p (n t)"),
                                data0=da[b][:].rearrange("p n t -> p (n t)"),
                                data1=db[b][:].rearrange("p n t -> p (n t)"), initial=0.0, op0=ALU.mult,
                                op1=ALU.add), t_a, t_b)
                            t_c = self.dve(lambda e, b=b, g=g: e.tensor_tensor(
                                db[b][:], db[b][:], bc[1][:, g * NH:(g + 1) * NH, :], ALU.mult), t_h)
                            for j in range(NH):
                                first, last = g == 0 and j == 0, g == NST // NH - 1 and j == NH - 1
                                db_free[b] = tok = self.pe(lambda e, b=b, j=j, y=ybank, f=first, z=last: e.matmul(
                                    y.t[:], self.ident[:], db[b][:, j, :], start=f, stop=z), t_c,
                                    ybank.free if first else None, sig=j == NH - 1)
                        y = self.dve(lambda e, m=m, y=ybank: e.scalar_tensor_tensor(
                            out=u[:, m, :], in0=u[:, m, :], scalar=dcol[:, m:m + 1], in1=y.t[:], op0=ALU.mult,
                            op1=ALU.add), tok)
                        ybank.free = y
                        self.dve(lambda e, m=m: e.tensor_tensor(zs[:, m, :], zs[:, m, :], u[:, m, :], ALU.mult), y)
                    self.q.emit()
            with ExitStack() as ctx:
                w = self.sbuf(ctx, "out_proj", [P, GT, D], F32)
                ld = self.load(w[:], self.i["L0_attn_out_proj_w"].rearrange("(k p) n -> p k n", p=P),
                               self.sem("s_outw"))
                self.project_residual(zs, w, None, GT, ld)
                self.q.emit()

    def gate(self, ctx, weights, w_gate, bias_row, softmax, ready):
        s = self.sbuf(ctx, "scores", [P, TT, E], F32)
        before = self.sbuf(ctx, "before", [P, E, E], F32)
        beats = self.sbuf(ctx, "beats", [P, E, E], F32)
        ties = self.sbuf(ctx, "ties", [P, E, E], F32)
        rank = self.sbuf(ctx, "rank", [P, E], F32)
        tot = self.sbuf(ctx, "score_sum", [P, TT], F32)
        one = self.pool(lambda e: e.memset(before[:], 1.0))
        tri = self.pool(lambda e: e.affine_select(out=before[:], in_=before[:], compare_op=ALU.is_gt, fill=0.0,
                                                  base=0, pattern=[[1, E], [-1, E]], channel_multiplier=0), one)
        bank = self.banks[7]
        for i in range(TT):
            terms = [(self.xnT[:, k, i * P:(i + 1) * P], w_gate[:, k, :]) for k in range(DT)]
            if bias_row is not None:
                terms.append((self.ones[0:1, :], bias_row))
            tok = self.gather(bank.t[:, i * E:(i + 1) * E], terms, ready, bank.free)
        logits = bank.t[:, 0:TT * E].rearrange("p (i e) -> p i e", e=E)
        if softmax:
            t = self.dve(lambda e: e.tensor_reduce(tot[:], logits, AXIS_X, ALU.max), tok)
            t = self.dve(lambda e: e.tensor_tensor(s[:], logits, tot[:].unsqueeze(2).to_broadcast([P, TT, E]),
                                                   ALU.subtract), t)
            bank.free = t
            t = self.act(lambda e: e.activation(s[:], s[:], ACT.Exp), t)
            t = self.dve(lambda e: e.tensor_reduce(tot[:], s[:], AXIS_X, ALU.add), t)
            t = self.dve(lambda e: e.reciprocal(tot[:], tot[:]), t)
            t = self.dve(lambda e: e.tensor_tensor(s[:], s[:], tot[:].unsqueeze(2).to_broadcast([P, TT, E]),
                                                   ALU.mult), t)
        else:
            t = bank.free = self.act(lambda e: e.activation(s[:], logits, ACT.Sigmoid), tok)
        for i in range(TT):
            mine = s[:, i, :].unsqueeze(2).to_broadcast([P, E, E])
            other = s[:, i, :].unsqueeze(1).to_broadcast([P, E, E])
            t = self.dve(lambda e, a=other, b=mine: e.tensor_tensor(beats[:], a, b, ALU.is_gt), t)
            t = self.dve(lambda e, a=other, b=mine: e.tensor_tensor(ties[:], a, b, ALU.is_equal), t)
            t = self.dve(lambda e: e.tensor_tensor(ties[:], ties[:], before[:], ALU.mult), t, tri)
            t = self.dve(lambda e: e.tensor_tensor(beats[:], beats[:], ties[:], ALU.add), t)
            t = self.dve(lambda e: e.tensor_reduce(rank[:], beats[:], AXIS_X, ALU.add), t)
            t = self.dve(lambda e: e.tensor_scalar(rank[:], rank[:], 1.5, None, ALU.is_lt), t)
            t = self.dve(lambda e, i=i: e.tensor_tensor(weights[:, i, 0:E], s[:, i, :], rank[:], ALU.mult), t)
            t = self.dve(lambda e, i=i: e.tensor_reduce(tot[:, i:i + 1], weights[:, i, 0:E], AXIS_X, ALU.add), t)
            if not softmax:
                t = self.dve(lambda e, i=i: e.tensor_scalar(tot[:, i:i + 1], tot[:, i:i + 1], 1e-6, None,
                                                            ALU.add), t)
            t = self.dve(lambda e, i=i: e.reciprocal(tot[:, i:i + 1], tot[:, i:i + 1]), t)
            t = self.dve(lambda e, i=i: e.tensor_scalar(weights[:, i, 0:E], weights[:, i, 0:E], tot[:, i:i + 1],
                                                        None, ALU.mult), t)
        return t

    def experts(self, ctx, up_w, down_w, up_b, down_b, weights, acc, func, ready):
        n_exp = down_b.shape[0]
        n_load = n_exp * NU
        per_exp = NU * FU
        x_part = [self.sbuf(ctx, f"x_{n}", [P, DT, T], F32R) for n in ("hi", "lo")]
        raw = [[self.sbuf(ctx, f"{n}_raw", [P, FU, D], F32) for n in ("up", "down")] for _ in range(2)]
        part = [[[self.sbuf(ctx, f"{n}_{k}", [P, FU, D], F32R) for k in ("hi", "lo")] for n in ("up", "down")]
                for _ in range(2)]
        hidden = [self.sbuf(ctx, "hidden", [P, T], F32) for _ in range(3)]
        h_part = [[self.sbuf(ctx, f"hidden_{k}", [P, T], F32R) for k in ("hi", "lo")] for _ in range(3)]
        wT = self.sbuf(ctx, "weights_T", [n_exp, TT, P], F32)
        s_raw = [[self.sem("s_up"), self.sem("s_down")] for _ in range(2)]
        _, x_ready = self.split(x_part[0][:], x_part[1][:], self.xnT[:], ready)
        raw_free = [[None, None], [None, None]]
        part_free = [[None, None], [None, None]]
        part_ready = {}
        loaded = {}

        def load(u):
            for n, src in enumerate((up_w, down_w)):
                loaded[u, n] = self.load(raw[u % 2][n][:], src(*divmod(u, NU)), s_raw[u % 2][n],
                                         raw_free[u % 2][n])

        def split(u, n):
            b = u % 2
            _, raw_free[b][n] = self.split(part[b][n][0][:], part[b][n][1][:], raw[b][n][:], loaded[u, n],
                                           part_free[b][n])
            part_ready[u, n] = raw_free[b][n]

        hid_ready, hid_free = {}, [None] * 3

        def up(s):
            u, j = divmod(s, FU)
            b, r = u % 2, s % 3
            bank = self.banks[4 + s % 3]
            tok = self.gather(bank.t[:], [(part[b][0][a][:, j, k * P:(k + 1) * P], x_part[c][:, k, :])
                                          for k in range(DT) for a, c in ((0, 0), (0, 1), (1, 0))],
                              part_ready[u, 0], x_ready, bank.free)
            if j == FU - 1:
                part_free[b][0] = tok
            bank.free = t = self.act(lambda e: e.activation(hidden[r][:], bank.t[:], func, bias=up_b[:, s:s + 1]),
                                     tok, hid_free[r])
            t_hi = self.act(lambda e: e.activation(h_part[r][0][:], hidden[r][:], ACT.Copy), t)
            hid_ready[s] = self.dve(lambda e: e.tensor_tensor(h_part[r][1][:], hidden[r][:],
                                                              h_part[r][0][:].bitcast(F32), ALU.subtract), t_hi)

        def down(s):
            u, j = divmod(s, FU)
            b, r = u % 2, s % 3
            first, last = s % per_exp == 0, s % per_exp == per_exp - 1
            for i in range(TT):
                bank = self.banks[i]
                cols = slice(i * P, (i + 1) * P)
                tok = self.gather(bank.t[:], [(h_part[r][a][:, cols], part[b][1][c][:, j, :])
                                              for a, c in ((0, 0), (0, 1), (1, 0))],
                                  hid_ready[s], part_ready[u, 1], bank.free if first else None,
                                  sig=last or i == TT - 1, start=first, stop=last)
                if last:
                    ex = s // per_exp
                    bank.free = self.dve(lambda e, i=i, k=bank: e.scalar_tensor_tensor(
                        out=acc[:, i, :], in0=k.t[:], scalar=weights[:, i, ex:ex + 1], in1=acc[:, i, :],
                        op0=ALU.mult, op1=ALU.add), tok, bank.free)
            hid_free[r] = tok
            if j == FU - 1:
                part_free[b][1] = tok

        load(0)
        load(1)
        for i in range(TT):
            tok = self.pe(lambda e, i=i: e.transpose(self.banks[7].t[0:n_exp, i * P:(i + 1) * P],
                                                     weights[:, i, :], self.ident[:]),
                          ready, self.banks[7].free, sig=i == TT - 1)
        t = self.banks[7].free = self.dve(lambda e: e.tensor_copy(
            wT[:], self.banks[7].t[0:n_exp, :].rearrange("p (i q) -> p i q", q=P)), tok)
        for i in range(TT):
            bank = self.banks[i]
            tok = self.gather(bank.t[:], [(wT[:, i, :], down_b[:])], t, bank.free)
            bank.free = self.dve(lambda e, i=i, k=bank: e.tensor_tensor(acc[:, i, :], acc[:, i, :], k.t[:],
                                                                        ALU.add), tok)
        split(0, 0)
        split(0, 1)
        for s in range(n_load * FU + 2):
            u, j = divmod(s, FU)
            if s < n_load * FU:
                up(s)
            if s >= 2:
                down(s - 2)
            if u + 1 < n_load and j in (1, 2):
                split(u + 1, j - 1)
                if j == 2 and u + 2 < n_load:
                    load(u + 2)
        return self.banks[TT - 1].free

    def l0_experts(self):
        n_exp = E + 1
        with ExitStack() as ctx:
            weights = self.sbuf(ctx, "weights", [P, TT, n_exp], F32)
            up_b = self.sbuf(ctx, "up_b", [P, n_exp * FF // P], F32)
            down_b = self.sbuf(ctx, "down_b", [n_exp, D], F32)
            gw = self.sbuf(ctx, "gate_w", [P, DT, E], F32)
            gb = self.sbuf(ctx, "gate_b", [1, E], F32)
            s = self.sem("s_moe0")
            with ExitStack() as tmp:
                nb = E * FF // P
                self.load(up_b[:, 0:nb], self.i["L0_ffn_buC"], s)
                self.load(up_b[:, nb:], self.i["L0_ffn_sbuC"], s)
                self.load(down_b[0:E, :], self.i["L0_ffn_bd"], s)
                self.load(down_b[E:, :], self.i["L0_ffn_sbd"].rearrange("(o n) -> o n", o=1), s)
                self.load(gw[:], self.i["L0_ffn_gate_wT"].rearrange("(k p) n -> p k n", p=P), s)
                ld = self.load(gb[:], self.i["L0_ffn_gate_bias"].rearrange("(o n) -> o n", o=1), s)
                ready, _ = self.normalized_T(tmp)
                self.dve(lambda e: e.memset(weights[:, :, E:], 0.1))
                self.q.wait("pe", ready)
                self.gate(tmp, weights, gw, gb[:], False, ld)
                self.q.emit()

            def up_w(e, u):
                return self.i["L0_ffn_Wu"][e, u] if e < E else self.i["L0_ffn_sWu"][u]

            def down_w(e, u):
                return self.i["L0_ffn_Wd"][e, u] if e < E else self.i["L0_ffn_sWd"][u]

            self.experts(ctx, up_w, down_w, up_b, down_b, weights, self.x, ACT.Gelu, None)
            self.q.emit()

    def l1_linear(self):
        with ExitStack() as ctx:
            w = {n: self.sbuf(ctx, f"w_{n}", [P, DT, c], F32)
                 for n, c in (("q", LH * P), ("k", LH * P), ("v", D), ("u", D), ("o", D))}
            tab = self.sbuf(ctx, "cos_sin", [P, LH, T], F32)
            qk = [self.sbuf(ctx, "qk_cat", [P, T], F32) for _ in range(4)]
            theta = self.sbuf(ctx, "theta", [P, LH], F32)
            shift = self.sbuf(ctx, "shift", [P, 1], F32)
            bqk = self.sbuf(ctx, "b_qk", [P, 2, LH], F32)
            bu = self.sbuf(ctx, "b_u", [P, DT], F32)
            bv = self.sbuf(ctx, "b_v", [1, D], F32)
            bo = self.sbuf(ctx, "b_o", [1, D], F32)
            slope = self.sbuf(ctx, "slope", [P, LH], F32)
            v = self.sbuf(ctx, "v", [P, TT, D], F32)
            uT = self.sbuf(ctx, "uT", [P, DT, T], F32)
            oT = self.sbuf(ctx, "oT", [P, DT, T], F32)
            tril = self.sbuf(ctx, "tril", [P, TT, T], F32)
            s_w, s_c = self.sem("s_linw"), self.sem("s_linc")
            for n, key in (("q", "qT2"), ("k", "kT2"), ("v", "vT"), ("u", "uT")):
                ld_w = self.load(w[n][:], self.i["L1_attn_w_" + key].rearrange("(k p) n -> p k n", p=P), s_w)
            ld_w = self.load(w["o"][:], self.i["L1_attn_out_wT"].rearrange("(k p) n -> p k n", p=P), s_w)
            self.load(theta[:], self.i["L1_attn_theta2"], s_c)
            self.load(bqk[:, 0, :], self.i["L1_attn_b_q2"], s_c)
            self.load(bqk[:, 1, :], self.i["L1_attn_b_k2"], s_c)
            self.load(bu[:], self.i["L1_attn_b_uC"], s_c)
            self.load(bv[:], self.i["L1_attn_b_v"], s_c)
            self.load(bo[:], self.i["L1_attn_out_b"].rearrange("(o n) -> o n", o=1), s_c)
            ld_c = self.load(slope[:], self.i["L1_attn_slope_rate"].rearrange("h a b -> (h a b)")
                             .partition_broadcast(P), s_c)
            one = self.pool(lambda e: e.memset(tril[:], 1.0))
            for m in range(TT):
                t_tril = self.pool(lambda e, m=m: e.affine_select(
                    out=tril[:, m, :], in_=tril[:, m, :], compare_op=ALU.is_ge, fill=0.0, base=-m * P,
                    pattern=[[1, T]], channel_multiplier=-1), one)
            with ExitStack() as tmp:
                PI = 3.141592653589793
                MAGIC = 12582912.0
                C1 = 6.28125
                C2 = 0.0019350051879882812
                C3 = 2 * PI - C1 - C2
                idx = self.sbuf(tmp, "idx", [P, T], F32)
                turns = self.sbuf(tmp, "turns", [P, T], F32)
                t_idx = self.pool(lambda e: e.iota(idx[:], [[1, T]], base=0, channel_multiplier=0,
                                                   allow_small_or_imprecise_dtypes=True))
                z = self.pool(lambda e: e.memset(shift[0:LD, :], PI / 2))
                z = self.pool(lambda e: e.memset(shift[LD:, :], 0.0))
                frac = self.sbuf(tmp, "turn_shift", [P, 1], F32)
                z = self.dve(lambda e: e.tensor_scalar(frac[:], shift[:], 1 / (2 * PI), None, ALU.mult), z)
                for h in range(LH):
                    ang = tab[:, h, :]
                    t = self.dve(lambda e, h=h, ang=ang: e.tensor_scalar(ang, idx[:], theta[:, h:h + 1], None,
                                                                         ALU.mult), t_idx, ld_c)
                    t = self.dve(lambda e, ang=ang: e.tensor_scalar(turns[:], ang, 1 / (2 * PI), frac[:], ALU.mult,
                                                                    ALU.add), t, z)
                    t = self.dve(lambda e: e.tensor_scalar(turns[:], turns[:], MAGIC, None, ALU.add), t)
                    t = self.dve(lambda e: e.tensor_scalar(turns[:], turns[:], MAGIC, None, ALU.subtract), t)
                    for c in (C1, C2, C3):
                        t = self.dve(lambda e, ang=ang, c=c: e.scalar_tensor_tensor(
                            out=ang, in0=turns[:], scalar=-c, in1=ang, op0=ALU.mult, op1=ALU.add), t)
                    t = self.dve(lambda e, ang=ang: e.tensor_scalar(ang, ang, shift[:], PI, ALU.add, ALU.min), t)
                    t = self.dve(lambda e, ang=ang: e.tensor_scalar(ang, ang, -PI, None, ALU.max), t)
                    self.act(lambda e, ang=ang: e.activation(ang, ang, ACT.Sin), t)
                self.normalized_T(tmp)
                self.q.emit()
            e_sb = [self.sbuf(ctx, "energy", [P, T], F32) for _ in range(3)]
            mh = [self.sbuf(ctx, "decay", [P, TT, T], F32) for _ in range(2)]
            for m in range(DT):
                bank = self.banks[m % 2]
                tok = self.gather(bank.t[:], [(w["u"][:, k, m * P:(m + 1) * P], self.xnT[:, k, :])
                                              for k in range(DT)], ld_w, bank.free)
                bank.free = self.dve(lambda e, b=bank, m=m: e.tensor_scalar(
                    uT[:, m, :], b.t[:], bu[:, m:m + 1], None, ALU.add), tok)
            for i in range(TT):
                bank = self.banks[i % 2]
                tok = self.gather(bank.t[:], [(self.xnT[:, k, i * P:(i + 1) * P], w["v"][:, k, :])
                                              for k in range(DT)] + [(self.ones[0:1, :], bv[:])], bank.free)
                bank.free = v_ready = self.dve(lambda e, b=bank, i=i: e.tensor_copy(v[:, i, :], b.t[:]), tok)
            qk_free, e_free, mh_free = [None, None], [None] * 3, [None, None]
            qk_ready, mh_ready = {}, {}

            def project(h):
                for n, name in enumerate(("q", "k")):
                    bank = self.banks[n]
                    buf = qk[2 * (h % 2) + n]
                    tok = self.gather(bank.t[:], [(w[name][:, k, h * P:(h + 1) * P], self.xnT[:, k, :])
                                                  for k in range(DT)], bank.free)
                    bank.free = t = self.act(lambda e, b=bank, n=n, buf=buf: e.activation(
                        buf[:], b.t[:], ACT.Silu, bias=bqk[:, n, h:h + 1]), tok, qk_free[h % 2])
                    qk_ready[h] = self.dve(lambda e, buf=buf: e.tensor_tensor(buf[:], buf[:], tab[:, h, :],
                                                                              ALU.mult), t)
                mh_ready[h] = self.act(lambda e: e.activation(mh[h % 2][:], tril[:], ACT.Exp,
                                                              scale=slope[:, h:h + 1]), mh_free[h % 2])

            n_e = 0
            project(0)
            for h in range(LH):
                if h + 1 < LH:
                    project(h + 1)
                q_h, k_h = qk[2 * (h % 2)], qk[2 * (h % 2) + 1]
                rows = slice(LD * (h % 2), LD * (h % 2) + LD)
                obank = self.banks[6 + (h // 2) % 2]
                e_ready = []
                for m in range(TT):
                    bank = self.banks[2 + m]
                    tok = self.gather(bank.t[:], [(k_h[:, m * P:(m + 1) * P], q_h[:])], qk_ready[h], bank.free)
                    if m == TT - 1:
                        qk_free[h % 2] = tok
                    r = n_e % 3
                    n_e += 1
                    bank.free = mh_free[h % 2] = self.dve(lambda e, b=bank, r=r, m=m, h=h: e.tensor_tensor(
                        e_sb[r][:], b.t[:], mh[h % 2][:, m, :], ALU.mult), tok, mh_ready[h], e_free[r])
                    e_ready.append((r, bank.free))
                    if m > 0:
                        self.value_rows(obank, rows, v, h, m - 1, e_sb, e_ready, e_free)
                tok = self.value_rows(obank, rows, v, h, TT - 1, e_sb, e_ready, e_free)
                t = self.dve(lambda e, rows=rows, o=obank, h=h: e.tensor_copy(oT[rows, h // 2, :], o.t[rows, :]),
                             tok)
                obank.free = t
            bank = self.banks[0]
            sq = e_sb[0]
            for m in range(DT):
                t_sq = self.dve(lambda e, m=m: e.tensor_tensor(sq[:], oT[:, m, :], oT[:, m, :], ALU.mult), t,
                                e_free[0])
                tok = self.pe(lambda e, m=m: e.matmul(bank.t[:], self.ones[:], sq[:], start=m == 0,
                                                      stop=m == DT - 1), t_sq, bank.free, sig=True)
                e_free[0] = tok
            rs = e_sb[1]
            t = self.dve(lambda e: e.tensor_scalar(rs[:], bank.t[:], 1.0 / D, 1e-6, ALU.mult, ALU.add), tok)
            bank.free = t
            t = self.act(lambda e: e.activation(rs[:], rs[:], ACT.Sqrt), t)
            t_rs = self.dve(lambda e: e.reciprocal(rs[:], rs[:]), t)
            for m in range(DT):
                t = self.dve(lambda e, m=m: e.tensor_tensor(oT[:, m, :], oT[:, m, :], rs[:], ALU.mult), t_rs)
                t = self.dve(lambda e, m=m: e.tensor_tensor(oT[:, m, :], oT[:, m, :], uT[:, m, :], ALU.mult), t)
            self.project_residual(oT, w["o"], bo[:], DT, t, first_bank=2)
            self.q.emit()

    def value_rows(self, obank, rows, v, h, m, e_sb, e_ready, e_free):
        r, ready = e_ready[m]
        tok = self.pe(lambda e: e.matmul(obank.t[rows, :], v[:, m, h * LD:(h + 1) * LD], e_sb[r][:],
                                         start=m == 0, stop=m == TT - 1, skip_group_check=True),
                      ready, obank.free, sig=True)
        e_free[r] = tok
        return tok

    def l1_ffn(self):
        with ExitStack() as outer:
            hh = self.sbuf(outer, "h", [P, TT, D], F32)
            weights = self.sbuf(outer, "weights", [P, TT, E], F32)
            up_b = self.sbuf(outer, "up_b", [P, E * FF // P], F32)
            down_b = self.sbuf(outer, "down_b", [E, D], F32)
            gains = [self.sbuf(outer, n, [P, D], F32) for n in ("g1", "b1", "g2", "b2")]
            s_c = self.sem("s_ffnc")
            with ExitStack() as ctx:
                w = self.sbuf(ctx, "w_qkv", [P, DT, 3 * D], F32)
                wo = self.sbuf(ctx, "w_o", [P, DT, D], F32)
                gw = self.sbuf(ctx, "gate_w", [P, DT, E], F32)
                xn = self.sbuf(ctx, "xn", [P, TT, D], F32)
                qT = self.sbuf(ctx, "qT", [P, DT, T], F32)
                kT = self.sbuf(ctx, "kT", [P, DT, T], F32)
                v = self.sbuf(ctx, "v", [P, TT, D], F32)
                o = self.sbuf(ctx, "o", [P, TT, D], F32)
                causal = self.sbuf(ctx, "causal", [P, (TT - 1) * P + T], F32)
                s_w = self.sem("s_ffnw")
                self.load(w[:], self.i["L1_ffn_w_qkv"].rearrange("(k p) n -> p k n", p=P), s_w)
                self.load(wo[:], self.i["L1_ffn_w_o"].rearrange("(k p) n -> p k n", p=P), s_w)
                self.load(gw[:], self.i["L1_ffn_wg"].rearrange("(k p) n -> p k n", p=P), s_w)
                self.load(up_b[:], self.i["L1_ffn_bb1C"], s_w)
                ld_w = self.load(down_b[:], self.i["L1_ffn_bb2"], s_w)
                for n, key in enumerate(("g1", "b1", "g2", "b2")):
                    ld_c = self.load(gains[n][:], self.i["L1_ffn_" + key].partition_broadcast(P), s_c)
                z = self.pool(lambda e: e.memset(causal[:], 0.0))
                t_causal = self.pool(lambda e: e.affine_select(
                    out=causal[:], in_=causal[:], compare_op=ALU.is_ge, fill=NEG_BIG, base=(TT - 1) * P,
                    pattern=[[-1, (TT - 1) * P + T]], channel_multiplier=1), z)
                done = self.layernorm(ctx, xn, self.x)
                self.transpose_all(self.xnT, xn, done)
                ready = self.banks[1].free
                for dst, base in ((qT, 0), (kT, D)):
                    for m in range(DT):
                        bank = self.banks[2 + m % 2]
                        tok = self.gather(bank.t[:], [(w[:, k, base + m * P:base + (m + 1) * P], self.xnT[:, k, :])
                                                      for k in range(DT)], ready, ld_w, bank.free)
                        bank.free = self.act(lambda e, b=bank, d=dst, m=m: e.activation(d[:, m, :], b.t[:],
                                                                                        ACT.Copy), tok)
                for i in range(TT):
                    bank = self.banks[2 + i % 2]
                    tok = self.gather(bank.t[:], [(self.xnT[:, k, i * P:(i + 1) * P], w[:, k, 2 * D:])
                                                  for k in range(DT)], bank.free)
                    bank.free = self.act(lambda e, b=bank, i=i: e.activation(v[:, i, :], b.t[:], ACT.Copy), tok)
                proj = bank.free
                NB = 3
                s_sb = [self.sbuf(ctx, "s", [P, T], F32) for _ in range(NB)]
                pT = [self.sbuf(ctx, "probT", [P, TT, P], F32) for _ in range(NB)]
                top = self.sbuf(ctx, "top", [P, TT, H], F32)
                den = self.sbuf(ctx, "den", [P, TT, H], F32)
                s_free, pT_free = [None] * NB, [None] * NB
                exp_ready, pT_ready = {}, {}
                scale = DH ** -0.5
                todo = [(i, h) for i in range(TT) for h in range(H)]

                def scores(n):
                    i, h = todo[n]
                    b, width = n % NB, (i + 1) * P
                    rows = slice(DH * (h % 4), DH * (h % 4) + DH)
                    bank = self.banks[2 + n % 2]
                    tok = self.gather(bank.t[:, 0:width], [(qT[rows, h // 4, i * P:(i + 1) * P],
                                                            kT[rows, h // 4, 0:width])], proj, bank.free)
                    off = (TT - 1 - i) * P
                    bank.free = t = self.dve(lambda e: e.tensor_tensor_reduce(
                        out=s_sb[b][:, 0:width], in0=bank.t[:, 0:width], in1=causal[:, off:off + width],
                        scale=1.0, scalar=-3.0e38, op0=ALU.add, op1=ALU.max, accum_out=top[:, i, h:h + 1]),
                        tok, s_free[b], t_causal)
                    t = self.dve(lambda e: e.tensor_scalar(top[:, i, h:h + 1], top[:, i, h:h + 1], -scale, None,
                                                           ALU.mult), t)
                    exp_ready[n] = self.act(lambda e: e.activation(
                        s_sb[b][:, 0:width], s_sb[b][:, 0:width], ACT.Exp, scale=scale, bias=top[:, i, h:h + 1],
                        accum_out=den[:, i, h:h + 1]), t)

                def turn(n):
                    i, h = todo[n]
                    b = n % NB
                    bank = self.banks[4 + n % 2]
                    for k in range(i + 1):
                        tok = self.pe(lambda e, k=k: e.transpose(bank.t[:, k * P:(k + 1) * P],
                                                                 s_sb[b][:, k * P:(k + 1) * P], self.ident[:]),
                                      exp_ready[n], bank.free, sig=k == i)
                    s_free[b] = tok
                    bank.free = pT_ready[n] = self.act(lambda e: e.activation(
                        pT[b][:, 0:i + 1, :], bank.t[:, 0:(i + 1) * P].rearrange("p (k q) -> p k q", q=P),
                        ACT.Copy), tok, pT_free[b])

                def values(n):
                    i, h = todo[n]
                    b = n % NB
                    bank = self.banks[6 + i % 2]
                    cols = slice(h * DH, (h + 1) * DH)
                    tok = self.gather(bank.t[:, cols], [(pT[b][:, k, :], v[:, k, cols]) for k in range(i + 1)],
                                      pT_ready[n], bank.free)
                    pT_free[b] = tok
                    if h == H - 1:
                        t = self.dve(lambda e: e.reciprocal(den[:, i, :], den[:, i, :]), tok, exp_ready[n])
                        bank.free = self.dve(lambda e: e.tensor_tensor(
                            o[:, i, :].rearrange("p (h d) -> p h d", d=DH),
                            bank.t[:].rearrange("p (h d) -> p h d", d=DH),
                            den[:, i, :].unsqueeze(2).to_broadcast([P, H, DH]), ALU.mult), t)

                for n in range(len(todo) + 2):
                    if n < len(todo):
                        scores(n)
                    if 1 <= n <= len(todo):
                        turn(n - 1)
                    if n >= 2:
                        values(n - 2)
                o_done = self.banks[6 + (TT - 1) % 2].free
                oT = qT
                t_oT = self.transpose_all(oT, o, o_done)
                for i in range(TT):
                    bank = self.banks[2 + i]
                    tok = self.gather(bank.t[:], [(oT[:, k, i * P:(i + 1) * P], wo[:, k, :]) for k in range(DT)],
                                      t_oT, bank.free)
                    bank.free = t = self.dve(lambda e, b=bank, i=i: e.tensor_tensor(
                        o[:, i, :], xn[:, i, :], b.t[:], ALU.add), tok)
                t = self.layernorm(ctx, hh, o, t)
                t = self.affine(hh, gains[0], gains[1], t, ld_c)
                t_T = self.transpose_all(self.xnT, hh, t)
                self.gate(ctx, weights, gw, None, True, t_T)
                self.q.emit()
            with ExitStack() as ctx:
                self.experts(ctx, lambda e, u: self.i["L1_ffn_w1"][e, u], lambda e, u: self.i["L1_ffn_w2"][e, u],
                             up_b, down_b, weights, hh, ACT.Gelu_apprx_tanh, None)
                self.q.emit()
            with ExitStack() as ctx:
                y = self.sbuf(ctx, "y", [P, TT, D], F32)
                t = self.layernorm(ctx, y, hh)
                t = self.affine(y, gains[2], gains[3], t, ld_c)
                self.dve(lambda e: e.tensor_tensor(self.x[:], self.x[:], y[:], ALU.add), t)
                self.q.emit()

    def affine(self, dst, g, b, *after):
        for i in range(TT):
            t = self.dve(lambda e, i=i: e.tensor_tensor(dst[:, i, :], dst[:, i, :], g[:], ALU.mult), *after)
            t = self.dve(lambda e, i=i: e.tensor_tensor(dst[:, i, :], dst[:, i, :], b[:], ALU.add), t)
        return t


def perceiver_kernel(nc, ins, out, stages):
    with ExitStack() as ctx:
        k = Kernel(nc, ins, out, ctx)
        k.constants()
        k.q.emit()
        for stage in stages:
            stage(k)
        k.finish()


STAGES = (Kernel.prepare_context, Kernel.l0_cross, Kernel.l0_scan, Kernel.l0_experts, Kernel.l1_cross,
          Kernel.l1_linear, Kernel.l1_ffn)


def _laid_out(inputs):
    import numpy as np
    a = {k: np.asarray(v) for k, v in inputs.items()}

    def columns(v):
        return v.reshape(-1, P).T

    def up(w):
        e = w.shape[0]
        w = w.reshape(e, DT, P, NU, FU, P)
        return w.transpose(0, 3, 2, 4, 1, 5).reshape(e, NU, P, FU, D)

    def down(w):
        e = w.shape[0]
        return w.reshape(e, NU, FU, P, D).transpose(0, 1, 3, 2, 4)

    ctx = a["ctx_1024"][0]
    mask = a["mask_Bx1xSxS2_ik1"][0, 0]
    d = {"x": a["x"], "ctxT": ctx.T, "mask": mask, "maskT": mask.T,
         "ctx_heads": ctx.reshape(KT, P, H, DH).transpose(2, 1, 0, 3).reshape(H, P, KT * DH)}
    for k in ("L0_xattn_Wq", "L0_xattn_Wk", "L0_xattn_bo", "L0_attn_in_proj_w", "L0_attn_conv_w",
              "L0_attn_x_proj_w", "L0_attn_dt_proj_w", "L0_attn_A_log", "L0_attn_out_proj_w", "L0_ffn_bd",
              "L0_ffn_sbd", "L0_ffn_gate_bias", "L1_xattn_bo", "L1_attn_slope_rate", "L1_attn_out_b",
              "L1_ffn_w_qkv", "L1_ffn_w_o", "L1_ffn_wg", "L1_ffn_bb2", "L1_ffn_g1", "L1_ffn_b1", "L1_ffn_g2",
              "L1_ffn_b2"):
        d[k] = a[k]
    for k in ("L0_xattn_Wv", "L0_xattn_Wo", "L1_xattn_Wk", "L1_xattn_Wv", "L1_xattn_Wo", "L0_ffn_gate_w",
              "L1_attn_out_w"):
        d[k + "T"] = a[k].T
    for k in ("L0_attn_ln_g", "L0_attn_ln_b", "L0_attn_conv_b", "L0_attn_dt_proj_b", "L0_attn_D"):
        d[k + "C"] = columns(a[k])
    d["L0_ffn_buC"] = columns(a["L0_ffn_bu"].reshape(-1))
    d["L0_ffn_sbuC"] = columns(a["L0_ffn_sbu"])
    d["L1_ffn_bb1C"] = columns(a["L1_ffn_bb1"].reshape(-1))
    d["L1_xattn_WqT3"] = np.tile(a["L1_xattn_Wq"].T.reshape(D, H, 1, DH), (1, 1, 3, 1)).reshape(D, H * QROWS)
    d["L0_ffn_Wu"] = up(a["L0_ffn_Wu"].transpose(0, 2, 1))
    d["L0_ffn_sWu"] = up(a["L0_ffn_sWu"].T[None])[0]
    d["L0_ffn_Wd"] = down(a["L0_ffn_Wd"].transpose(0, 2, 1))
    d["L0_ffn_sWd"] = down(a["L0_ffn_sWd"].T[None])[0]
    d["L1_ffn_w1"] = up(a["L1_ffn_w1"])
    d["L1_ffn_w2"] = down(a["L1_ffn_w2"])
    w = a["L1_attn_qkvu_w"].reshape(4, D, D)
    b = a["L1_attn_qkvu_b"].reshape(4, D)
    for n, k in ((0, "q"), (1, "k")):
        d[f"L1_attn_w_{k}T2"] = np.tile(w[n].T.reshape(D, LH, 1, LD), (1, 1, 2, 1)).reshape(D, LH * P)
        d[f"L1_attn_b_{k}2"] = np.tile(b[n].reshape(LH, LD), (1, 2)).T
    d["L1_attn_w_vT"], d["L1_attn_w_uT"] = w[2].T, w[3].T
    d["L1_attn_b_v"], d["L1_attn_b_uC"] = b[2:3], columns(b[3])
    d["L1_attn_theta2"] = np.tile(a["L1_attn_theta"].reshape(LH, LD), (1, 2)).T
    return d


def kernel(**inputs):
    import numpy as np
    import concourse.bacc as bacc
    from concourse.bass_utils import run_bass_kernel_spmd

    nc = bacc.Bacc("TRN2", target_bir_lowering=False, num_devices=1)
    arrays, aps = {}, {}
    for name, value in _laid_out(inputs).items():
        value = np.ascontiguousarray(value)
        arrays["in_" + name] = value
        aps[name] = nc.dram_tensor("in_" + name, value.shape, mybir.dt.from_np(value.dtype),
                                   kind="ExternalInput").ap()
    out = nc.dram_tensor("out_x", (1, T, D), F32, kind="ExternalOutput").ap()
    perceiver_kernel(nc, aps, out, STAGES)
    r = run_bass_kernel_spmd(nc, [arrays], core_ids=[0])
    return r.results[0]["out_x"]
```

```python
from contextlib import ExitStack

import concourse.bass as bass
from concourse import mybir

F32 = mybir.dt.float32
F32R = mybir.dt.float32r
BF16 = mybir.dt.bfloat16
F8 = mybir.dt.float8e4
I32 = mybir.dt.int32
ALU = mybir.AluOpType
ACT = mybir.ActivationFunctionType
AXIS_X = mybir.AxisListType.X

P = 128
T = 512
D = 512
S2 = 8192
TT = T // P
DT = D // P
H = 16
DH = D // H
E = 8
FF = 2048
BIG = 2.0 ** 67
NEG_BIG = -BIG

KC = 512
NKC = S2 // KC
LEAD = 1
KRING = NKC + LEAD + 2
KT = S2 // P
QROWS = 3 * DH

DIN = 1024
NST = 16
DTR = 32
GT = DIN // P

LH = 8
LD = D // LH

FU = 4
NU = FF // (FU * P)


class EngineQueues:

    NAMES = ("pe", "act", "dve", "pool", "sp")

    def __init__(self, nc, ctx):
        self.nc = nc
        self.sem = {n: ctx.enter_context(nc.semaphore("s_" + n)) for n in self.NAMES}
        self.count = {n: 0 for n in self.NAMES}
        self.dma_count = {}
        self.items = {n: [] for n in self.NAMES}
        self.waited = {n: {} for n in self.NAMES}
        self.stores = {}

    def wait(self, eng, *after):
        for token in after:
            if token is None:
                continue
            name, sem, value = token
            if self.waited[eng].get(name, 0) < value:
                self.waited[eng][name] = value
                self.items[eng].append(("wait", sem, value))

    def do(self, eng, fn, *after, sig=True):
        self.wait(eng, *after)
        if sig:
            self.count[eng] += 1
            self.items[eng].append(("op", fn, self.sem[eng], 1))
            return (eng, self.sem[eng], self.count[eng])
        self.items[eng].append(("op", fn, None, 0))
        return None

    def dma(self, eng, out, in_, sem, *after, store=False):
        self.wait(eng, *after)
        name = sem.name
        self.dma_count[name] = self.dma_count.get(name, 0) + 16
        self.items[eng].append(("op", lambda e: e.dma_start(out, in_), sem, 16))
        token = (name, sem, self.dma_count[name])
        if store:
            self.stores[name] = token
        return token

    def emit(self):
        items, self.items = self.items, {n: [] for n in self.NAMES}
        with self.nc.Block() as block:
            for name, where in (("sp", block.sync), ("pe", block.tensor), ("act", block.scalar),
                                ("dve", block.vector), ("pool", block.gpsimd)):
                if not items[name]:
                    continue

                def run(eng, todo=items[name]):
                    for item in todo:
                        if item[0] == "wait":
                            eng.wait_ge(item[1], item[2])
                        else:
                            ins = item[1](eng)
                            if item[2] is not None:
                                ins.then_inc(item[2], item[3])

                where(run)


class Bank:

    def __init__(self, tensor):
        self.t = tensor
        self.free = None


class Kernel:
    def __init__(self, nc, ins, out, ctx):
        self.nc = nc
        self.i = ins
        self.out = out
        self.ctx = ctx
        self.q = EngineQueues(nc, ctx)
        self.nsem = 0
        self.last_pool = None
        self.k1 = None
        self.ntmp = 0
        sb = self.sbuf
        self.ident = sb(ctx, "ident", [P, P], F32)
        self.ident_big = sb(ctx, "ident_big", [P, P], BF16)
        self.ones = sb(ctx, "ones", [P, P], F32)
        self.x = sb(ctx, "x", [P, TT, D], F32)
        self.xnT = sb(ctx, "xnT", [P, DT, T], F32)
        self.x_ready = None
        self.psum = ctx.enter_context(nc.psum_tensor("psum", [P, 8, 512], F32))
        self.banks = [Bank(self.psum[:, i, :]) for i in range(8)]

    def sbuf(self, ctx, name, shape, dt):
        self.ntmp += 1
        return ctx.enter_context(self.nc.sbuf_tensor(f"{name}_{self.ntmp}", shape, dt))

    def sem(self, name):
        self.nsem += 1
        return self.ctx.enter_context(self.nc.semaphore(f"{name}_{self.nsem}"))

    def pe(self, fn, *after, sig=False):
        return self.q.do("pe", fn, *after, sig=sig)

    def act(self, fn, *after, sig=True):
        return self.q.do("act", fn, *after, sig=sig)

    def dve(self, fn, *after, sig=True):
        return self.q.do("dve", fn, *after, sig=sig)

    def pool(self, fn, *after):
        self.last_pool = self.q.do("pool", fn, *after, self.last_pool)
        return self.last_pool

    def load(self, out, in_, sem, *after, eng="sp"):
        return self.q.dma(eng, out, in_, sem, *after)

    def store(self, out, in_, sem, *after, eng="sp"):
        return self.q.dma(eng, out, in_, sem, *after, store=True)

    def gather(self, out, terms, *after, sig=True, start=True, stop=True):
        token = None
        for n, (lhsT, rhs) in enumerate(terms):
            last = n == len(terms) - 1
            token = self.pe(lambda e, a=lhsT, b=rhs, s=start and n == 0, z=stop and last:
                            e.matmul(out, a, b, start=s, stop=z), *(after if n == 0 else ()), sig=last and sig)
        return token

    def split(self, hi, lo, src, *after, hi_on="dve"):
        if hi_on == "act":
            t_hi = self.act(lambda e: e.activation(hi, src, ACT.Copy), *after)
        else:
            t_hi = self.dve(lambda e: e.tensor_copy(hi, src), *after)
        t_lo = self.dve(lambda e: e.tensor_tensor(lo, src, hi.bitcast(F32), ALU.subtract), t_hi, *after)
        return t_hi, t_lo

    def constants(self):
        zero = self.pool(lambda e: e.memset(self.ident[:], 0.0))
        self.pool(lambda e: e.affine_select(out=self.ident[:], in_=self.ident[:], compare_op=ALU.not_equal,
                                            fill=1.0, base=0, pattern=[[-1, P]], channel_multiplier=1), zero)
        zero = self.pool(lambda e: e.memset(self.ident_big[:], 0.0))
        self.pool(lambda e: e.affine_select(out=self.ident_big[:], in_=self.ident_big[:],
                                            compare_op=ALU.not_equal, fill=BIG, base=0, pattern=[[-1, P]],
                                            channel_multiplier=1), zero)
        self.pool(lambda e: e.memset(self.ones[:], 1.0))
        self.q.wait("sp", self.load(self.x[:], self.i["x"].rearrange("o (i p) d -> p (o i) d", p=P),
                                    self.sem("s_x")))

    def finish(self):
        self.store(self.out.rearrange("o (i p) d -> p (o i) d", p=P), self.x[:], self.sem("s_out"))
        self.q.wait("sp", *self.q.stores.values())
        self.q.emit()

    def layernorm(self, ctx, dst, src, *after):
        stats = self.sbuf(ctx, "ln_stats", [P, TT, 6], F32)
        mv = self.sbuf(ctx, "ln_mean_var", [P, TT, 2], F32)
        rstd = self.sbuf(ctx, "ln_rstd", [P, TT], F32)
        for i in range(TT):
            st = self.dve(lambda e, i=i: e.bn_stats(stats[:, i, :], src[:, i, :]), *after)
            agg = self.dve(lambda e, i=i: e.bn_aggr(mv[:, i, :], stats[:, i, :]), st)
        eps = self.dve(lambda e: e.tensor_scalar(rstd[:], mv[:, :, 1], 1e-5, None, ALU.add), agg)
        root = self.act(lambda e: e.activation(rstd[:], rstd[:], ACT.Sqrt), eps)
        rec = self.dve(lambda e: e.reciprocal(rstd[:], rstd[:]), root)
        for i in range(TT):
            done = self.dve(lambda e, i=i: e.tensor_scalar(dst[:, i, :], src[:, i, :], mv[:, i, 0:1],
                                                           rstd[:, i:i + 1], ALU.subtract, ALU.mult), rec)
        return done

    def transpose_all(self, dstT, src, *after, gain=None):
        for c in range(DT):
            bank = self.banks[c % 2]
            for i in range(TT):
                tr = self.pe(lambda e, b=bank, c=c, i=i: e.transpose(
                    b.t[:, i * P:(i + 1) * P], src[:, i, c * P:(c + 1) * P], self.ident[:]),
                    *after, bank.free, sig=i == TT - 1)
            if gain is None:
                bank.free = self.dve(lambda e, b=bank, c=c: e.tensor_copy(dstT[:, c, :], b.t[:]), tr)
            else:
                bank.free = self.dve(lambda e, b=bank, c=c: e.tensor_scalar(
                    dstT[:, c, :], b.t[:], gain[0][:, c:c + 1], gain[1][:, c:c + 1], ALU.mult, ALU.add), tr)
        return bank.free

    def normalized_T(self, ctx, *after, xn=None):
        if xn is None:
            xn = self.sbuf(ctx, "xn", [P, TT, D], F32)
        done = self.layernorm(ctx, xn, self.x, *after)
        return self.transpose_all(self.xnT, xn, done), xn

    def project_residual(self, lhsT, w, bias_row, kt, *after, first_bank=0):
        for i in range(TT):
            bank = self.banks[first_bank + i]
            terms = [(lhsT[:, k, i * P:(i + 1) * P], w[:, k, :]) for k in range(kt)]
            if bias_row is not None:
                terms.append((self.ones[0:1, :], bias_row))
            tok = self.gather(bank.t[:], terms, *after, bank.free)
            bank.free = self.dve(lambda e, b=bank, i=i: e.tensor_tensor(
                self.x[:, i, :], self.x[:, i, :], b.t[:], ALU.add), tok)
        return bank.free

    def prepare_context(self, mask_k=None):
        nc, i = self.nc, self.i
        self.k0 = [nc.dram_tensor(f"k0_{n}", [D, S2], F32, kind="Internal").ap() for n in ("hi", "lo")]
        self.k1 = [nc.dram_tensor(f"k1_{n}", [D, S2], F32, kind="Internal").ap() for n in ("hi", "lo")]
        self.v1 = nc.dram_tensor("v1_heads", [H, P, KT * DH], F32, kind="Internal").ap()
        CH = 512
        VT = CH // P
        STEPS = S2 // CH
        with ExitStack() as ctx:
            wk = [self.sbuf(ctx, f"wk{n}", [P, DT, D], F32R) for n in ("hi", "lo")]
            wv = [self.sbuf(ctx, f"wv{n}", [P, DT, D], F32R) for n in ("hi", "lo")]
            raw = [self.sbuf(ctx, "ctxT", [P, DT, CH], F32) for _ in range(2)]
            cx = [[self.sbuf(ctx, f"ctx{n}", [P, DT, CH], F32R) for n in ("hi", "lo")] for _ in range(2)]
            kst = [[self.sbuf(ctx, f"k1{n}", [P, DT, CH], F32R) for n in ("hi", "lo")] for _ in range(2)]
            vst = [self.sbuf(ctx, "v1", [P, H, VT, DH], F32) for _ in range(2)]
            s_raw = [self.sem("s_raw") for _ in range(2)]
            s_k0 = [self.sem("s_k0") for _ in range(2)]
            s_out = [self.sem("s_k1v1") for _ in range(2)]
            raw_free = [None, None]
            cx_free = [(), ()]
            st_free = [None, None]
            for b, (name, parts) in enumerate((("L1_xattn_WkT", wk), ("L1_xattn_WvT", wv))):
                ld = self.load(raw[b][:], i[name].rearrange("(k p) n -> p k n", p=P), s_raw[b])
                _, raw_free[b] = self.split(parts[0][:], parts[1][:], raw[b][:], ld)
            w_ready = raw_free[1]
            ctxT = i["ctxT"].rearrange("(k p) n -> p k n", p=P)
            loaded, split_done = {}, {}
            if mask_k is not None:
                m_raw = [self.sbuf(ctx, "mask_raw", [P, VT, T], I32) for _ in range(2)]
                s_m = [self.sem("s_mask_k") for _ in range(2)]
                m_free = [None, None]
                maskT = i["maskT"].rearrange("(k p) q -> p k q", p=P)
            m_loaded = {}

            def load_mask(s):
                if mask_k is not None and s < STEPS:
                    m_loaded[s] = self.load(m_raw[s % 2][:], maskT[:, s * VT:(s + 1) * VT, :], s_m[s % 2],
                                            m_free[s % 2])

            def load(s):
                b = s % 2
                loaded[s] = self.load(raw[b][:], ctxT[:, :, s * CH:(s + 1) * CH], s_raw[b], raw_free[b])

            def split(s):
                b = s % 2
                _, raw_free[b] = self.split(cx[b][0][:], cx[b][1][:], raw[b][:], loaded[s], *cx_free[b])
                split_done[s] = raw_free[b]

            load(0)
            load(1)
            load_mask(0)
            split(0)
            for s in range(STEPS):
                b = s % 2
                cols = slice(s * CH, (s + 1) * CH)
                if s + 2 < STEPS:
                    load(s + 2)
                load_mask(s + 1)
                for n in range(2):
                    k0_st = self.store(self.k0[n].rearrange("(k p) n -> p k n", p=P)[:, :, cols],
                                       cx[b][n][:].bitcast(F32), s_k0[b], split_done[s])
                if s + 1 < STEPS:
                    split(s + 1)
                if mask_k is not None:
                    m_free[b] = self.dve(lambda e, s=s, b=b: e.tensor_scalar(
                        mask_k[:, s * VT:(s + 1) * VT, :], m_raw[b][:], 0, -1.0, ALU.is_equal, ALU.mult,
                        saturate=False), m_loaded[s])
                for m in range(DT):
                    bank = self.banks[m]
                    rows = slice(m * P, (m + 1) * P)
                    tok = self.gather(bank.t[:], [
                        (wk[a][:, k, rows], cx[b][c][:, k, :])
                        for k in range(DT) for a, c in ((0, 0), (0, 1), (1, 0))], split_done[s], w_ready,
                        bank.free)
                    _, bank.free = self.split(kst[b][0][:, m, :], kst[b][1][:, m, :], bank.t[:], tok,
                                              st_free[b], hi_on="act")
                k_done = bank.free
                for t in range(VT):
                    bank = self.banks[4 + t]
                    rows = slice(t * P, (t + 1) * P)
                    tok = self.gather(bank.t[:], [
                        (cx[b][c][:, k, rows], wv[a][:, k, :])
                        for k in range(DT) for a, c in ((0, 0), (0, 1), (1, 0))], bank.free)
                    bank.free = self.act(lambda e, bank=bank, b=b, t=t: e.activation(
                        vst[b][:, :, t, :], bank.t[:].rearrange("p (h d) -> p h d", h=H), ACT.Copy),
                        tok, st_free[b])
                cx_free[b] = (tok, k0_st)
                for n in range(2):
                    self.store(self.k1[n].rearrange("(k p) n -> p k n", p=P)[:, :, cols],
                               kst[b][n][:].bitcast(F32), s_out[b], k_done)
                st_free[b] = self.store(self.v1.rearrange("h p n -> p h n")[:, :, s * VT * DH:(s + 1) * VT * DH],
                                        vst[b][:].rearrange("p h t d -> p h (t d)"), s_out[b], bank.free)
            self.q.wait("sp", st_free[0], st_free[1], cx_free[0][1], cx_free[1][1])
            self.q.emit()

    def cross_attention(self, ctx, k_hi_lo, v_heads, emit_query, comb, scale, masks, attT, ready):
        rows_q = slice(0, QROWS)
        rows_m = slice(QROWS, QROWS + 2)
        n_q, n_p = 3, 4 if masks else 8
        q_stack = [self.sbuf(ctx, "q_stack", [QROWS + 2, T], F32R) for _ in range(n_q)]
        k_ring = self.sbuf(ctx, "k_ring", [QROWS + 2, KRING, KC], F32R)
        v_buf = [self.sbuf(ctx, "v_buf", [P, KT * DH], F32)[:], self.x[:].rearrange("p i d -> p (i d)")]
        prob = [self.sbuf(ctx, "prob", [P, 2, T], F32) for _ in range(n_p)]
        trash = [self.sbuf(ctx, "max_trash", [P, KC], BF16) for _ in range(2)] if masks else None
        row_max = [self.sbuf(ctx, "row_max", [P, TT, NKC], F32) for _ in range(2)]
        top2 = self.sbuf(ctx, "row_top2", [P, TT, 2], F32)
        den_part = {e: self.sbuf(ctx, "den_" + e, [P, 2, T], F32) for e in ("pool", "dve")}
        m_hi = self.sbuf(ctx, "m_hi", [QROWS + 2, T], F32R)[rows_m, :]
        den4 = self.sbuf(ctx, "den_of_4_heads", [P, T], F32)
        lo_sign = self.sbuf(ctx, "lo_sign", [QROWS + 2, 1], F32)
        o_sb = self.sbuf(ctx, "o_sb", [P, T], F32)
        s_k = [self.sem("s_k") for _ in range(KRING)]
        s_v = [self.sem("s_v") for _ in range(2)]
        ring_init = self.pool(lambda e: e.memset(k_ring[rows_m, :, :].bitcast(F32), -1.0))
        self.pool(lambda e: e.memset(lo_sign[rows_m, :], -1.0))
        consts = self.pool(lambda e: e.memset(lo_sign[QROWS:QROWS + 1, :], 0.0))

        score = [(self.banks[0], self.banks[1]), (self.banks[2], self.banks[3])]
        maxbank = [self.banks[4], self.banks[5]]
        vbank, misc = self.banks[6], self.banks[7]

        k_loaded, k_used = {}, {}
        v_ready, v_used = {}, {}
        q_ready, m_ready = {}, {}
        exp_done = {}
        prob_free = [()] * n_p
        den_added = {"pool": None, "dve": None}
        last = {"top2": None, "o_sb": None, "den": None, "den4": None}

        def load_k(n):
            h, c = divmod(n, NKC)
            if h >= H:
                return
            slot = n % KRING
            rows, cols = slice(h * DH, (h + 1) * DH), slice(c * KC, (c + 1) * KC)
            for g, part in enumerate((0, 0, 1)):
                k_loaded[n] = self.load(k_ring[g * DH:(g + 1) * DH, slot, :].bitcast(F32),
                                        k_hi_lo[part][rows, cols], s_k[slot], k_used.get(n - KRING))

        def load_v(h):
            if h >= H:
                return
            v_ready[h] = self.load(v_buf[h % 2], v_heads[h], s_v[h % 2], v_used.get(h - 2))

        def query(h):
            if h >= H:
                return
            tok = emit_query(h, misc.t[rows_q, :], ready, misc.free)
            qs = q_stack[h % n_q]
            hi = self.act(lambda e: e.activation(qs[rows_q, :], misc.t[rows_q, :], ACT.Copy), tok,
                          k_used.get((h - n_q + 1) * NKC - 1))
            misc.free = q_ready[h] = self.dve(lambda e: e.tensor_tensor(
                qs[DH:2 * DH, :], misc.t[DH:2 * DH, :], qs[DH:2 * DH, :].bitcast(F32), ALU.subtract), hi)

        def max_step(n, i):
            h, c = divmod(n, NKC)
            if h >= H:
                return
            bank = maxbank[i % 2]
            tok = self.gather(bank.t[:], [(q_stack[h % n_q][rows_q, i * P:(i + 1) * P],
                                           k_ring[rows_q, n % KRING, :])], q_ready[h], k_loaded[n], bank.free)
            out = row_max[h % 2][:, i, c:c + 1]
            if masks is None:
                bank.free = self.dve(lambda e: e.reduce_max(out, bank.t[:], AXIS_X), tok)
            else:
                bank.free = self.dve(lambda e: e.tensor_tensor_reduce(
                    out=trash[i % 2][:], in0=bank.t[:], in1=masks[0][:, i, c * KC:(c + 1) * KC], scale=1.0,
                    scalar=-3.0e38, op0=ALU.add, op1=ALU.max, accum_out=out), tok, bank.free,
                    mask_ready[c])

        def top_of_rows(h):
            t = self.dve(lambda e: e.tensor_reduce(top2[:, :, 0:1], row_max[h % 2][:], AXIS_X, ALU.max),
                         maxbank[0].free, maxbank[1].free, last["top2"])
            return self.dve(lambda e: e.tensor_copy(top2[:, :, 1:2], top2[:, :, 0:1]), t)

        def max_rows(h, t):
            for i in range(TT):
                tok = self.pe(lambda e, i=i: e.matmul(misc.t[rows_m, i * P:(i + 1) * P], top2[:, i, :],
                                                      self.ident[:], start=True, stop=True),
                              t, misc.free, sig=i == TT - 1)
            last["top2"] = tok
            hi = self.act(lambda e: e.activation(m_hi, misc.t[rows_m, :], ACT.Copy), tok, m_ready.get(h - 1))
            misc.free = m_ready[h] = self.dve(lambda e: e.scalar_tensor_tensor(
                out=q_stack[h % n_q][rows_m, :], in0=m_hi.bitcast(F32), scalar=lo_sign[rows_m, :],
                in1=misc.t[rows_m, :], op0=ALU.mult, op1=ALU.add), hi, consts,
                k_used.get((h - n_q + 1) * NKC - 1))

        def score_step(n, j2):
            h = n // NKC
            banks = score[j2]
            b = (2 * n + j2) % n_p
            for j in range(2):
                kt = 2 * j2 + j
                after = (m_ready[h], k_loaded[n], banks[0].free, ring_init)
                if masks is not None:
                    self.pe(lambda e, j=j, kt=kt: e.matmul(
                        banks[j].t[:], self.ident_big[:], masks[1][:, n % NKC * (KC // P) + kt, :], start=True,
                        stop=False), *after)
                tok = self.pe(lambda e, j=j, kt=kt: e.matmul(
                    banks[j].t[:], k_ring[:, n % KRING, kt * P:(kt + 1) * P], q_stack[h % n_q][:],
                    start=masks is None, stop=True), *after, sig=j == 1)
            k_used[n] = tok
            banks[0].free = exp_done[2 * n + j2] = self.act(lambda e: e.activation(
                prob[b][:], self.psum[:, 2 * j2:2 * j2 + 2, :], ACT.Exp, scale=scale), tok, *prob_free[b])

        def value_step(n):
            h, c = divmod(n, NKC)
            for kt in range(KC // P):
                j2, j = divmod(kt, 2)
                b = (2 * n + j2) % n_p
                k = c * (KC // P) + kt
                tok = self.pe(lambda e, j=j, k=k, b=b, g=kt * DH: e.matmul(
                    vbank.t[g:g + DH, :], v_buf[h % 2][:, k * DH:(k + 1) * DH], prob[b][:, j, :],
                    start=c == 0, stop=c == NKC - 1, skip_group_check=True),
                    exp_done[2 * n + j2], v_ready[h], vbank.free, sig=j == 1)
                if j == 1:
                    prob_free[b] = (tok, *summed[2 * n + j2])
            v_used[h] = tok

        summed_chunks = set()
        summed = {}

        def add_den(name, n, j2, tiles, slots, first):
            p, d = prob[(2 * n + j2) % n_p][:, tiles, :], den_part[name][:, slots, :]
            fn = ((lambda e: e.tensor_scalar(d, p, 1.0, None, ALU.mult)) if first else
                  (lambda e: e.tensor_tensor(d, d, p, ALU.add)))
            den_added[name] = (self.pool if name == "pool" else self.dve)(
                fn, exp_done[2 * n + j2], den_added[name], last["den"])
            return den_added[name]

        def den_step(n):
            summed_chunks.add(n)
            first = n % NKC == 0
            both = slice(0, 2)
            summed[2 * n] = (add_den("pool", n, 0, both, both, first),)
            if masks is not None or first or n % 3 == 0:
                summed[2 * n + 1] = (add_den("dve", n, 1, both, both, first),)
            else:
                summed[2 * n + 1] = (add_den("pool", n, 1, slice(0, 1), slice(0, 1), False),
                                     add_den("dve", n, 1, slice(1, 2), slice(1, 2), False))

        def take_values(h):
            vbank.free = self.act(lambda e: e.activation(o_sb[:], vbank.t[:], ACT.Copy), v_used[h], last["o_sb"])
            a, d = den_part["pool"], den_part["dve"]
            last["den"] = self.pool(lambda e: e.tensor_tensor(d[:], d[:], a[:], ALU.add), den_added["dve"])

        def head_out(h):
            g = slice(DH * (h % 4), DH * (h % 4) + DH)
            self.pe(lambda e: e.matmul(misc.t[0:DH, :], comb, o_sb[:], start=True, stop=True),
                    vbank.free, misc.free)
            tok = self.gather(misc.t[DH:2 * DH, :], [(self.ones[:, 0:DH], den_part["dve"][:, j, :])
                                                     for j in range(2)], last["den"])
            last["o_sb"] = last["den"] = tok
            out = attT[:, h // 4, :]
            self.act(lambda e: e.activation(out[g, :], misc.t[0:DH, :], ACT.Copy), tok)
            misc.free = t = self.act(lambda e: e.activation(den4[g, :], misc.t[DH:2 * DH, :], ACT.Copy), tok,
                                     last["den4"])
            if h % 4 == 3:
                rec = self.dve(lambda e: e.reciprocal(den4[:], den4[:]), t)
                last["den4"] = self.dve(lambda e: e.tensor_tensor(out, out, den4[:], ALU.mult), rec)

        mask_ready = {}
        if masks is not None:
            s_mq = [self.sem("s_mask_q") for _ in range(n_p)]
            mask_rows = self.i["mask"].rearrange("(i p) k -> p i k", p=P)

        def mask_step(c):
            for j in range(2):
                b = (2 * c + j) % n_p
                two = slice(2 * j, 2 * j + 2)
                raw = prob[b][:].bitcast(I32)
                ld = self.load(raw, mask_rows[:, two, c * KC:(c + 1) * KC], s_mq[b], *prob_free[b], eng="act")
                mask_ready[c] = self.dve(lambda e, raw=raw, two=two: e.tensor_scalar(
                    masks[0][:, two, c * KC:(c + 1) * KC], raw, 0, NEG_BIG, ALU.is_equal, ALU.mult), ld)
                prob_free[b] = (mask_ready[c],)

        for n in range(KRING):
            load_k(n)
        load_v(0)
        query(0)
        query(1)
        for n in range(NKC + LEAD):
            if masks is not None and n < NKC:
                mask_step(n)
            if n == NKC:
                max_rows(0, top_of_rows(0))
            for i in range(TT):
                max_step(n, i)
        for n in range(H * NKC):
            h, c = divmod(n, NKC)
            ahead = n + NKC + LEAD
            t_top = top_of_rows(h + 1) if c == NKC - LEAD and h + 1 < H else None
            max_step(ahead, 0)
            if masks is not None:
                max_step(ahead, 1)
            score_step(n, 0)
            if t_top is not None:
                max_rows(h + 1, t_top)
            if masks is None:
                max_step(ahead, 1)
            score_step(n, 1)
            load_k(n + KRING)
            if c == 1 and h > 0:
                head_out(h - 1)
            max_step(ahead, 2)
            if masks is not None:
                max_step(ahead, 3)
            if n > 0 and n - 1 not in summed_chunks:
                den_step(n - 1)
            if n > 0:
                value_step(n - 1)
            if c == 0 and h > 0:
                take_values(h - 1)
            if masks is None:
                max_step(ahead, 3)
            elif c > 0:
                den_step(n)
            if c == 1:
                load_v(h + 1)
            if c == NKC // 2:
                query(h + 2)
        if masks is None:
            den_step(H * NKC - 1)
        value_step(H * NKC - 1)
        take_values(H - 1)
        head_out(H - 1)
        return last["den4"]

    def output_projection(self, attT, w_name, b_name, x_rows):
        with ExitStack() as ctx:
            w = self.sbuf(ctx, "wo", [P, DT, D], F32)
            b = self.sbuf(ctx, "bo", [1, D], F32)
            s = self.sem("s_wo")
            self.load(w[:], self.i[w_name].rearrange("(k p) n -> p k n", p=P), s)
            ld = self.load(b[:], self.i[b_name].rearrange("(o n) -> o n", o=1), s)
            self.q.wait("dve", self.load(self.x[:], x_rows, self.sem("s_x_back")))
            self.project_residual(attT, w, b[:], DT, ld)
            self.q.emit()

    def l0_cross(self):
        x_rows = self.i["x"].rearrange("o (i p) d -> p (o i) d", p=P)
        with ExitStack() as outer:
            attT = self.sbuf(outer, "attT", [P, DT, T], F32)
            with ExitStack() as ctx:
                mask_k = self.sbuf(ctx, "mask_k", [P, KT, T], F8)
                m4 = self.sbuf(ctx, "m4", [P, QROWS], F32)
                comb = self.sbuf(ctx, "comb", [P, DH], F32)
                wq = self.sbuf(ctx, "wq", [DH, DH], F32)
                wk = self.sbuf(ctx, "wk", [DH, DH], F32)
                s = self.sem("s_l0w")
                self.load(wq[:], self.i["L0_xattn_Wq"], s)
                self.load(wk[:], self.i["L0_xattn_Wk"], s)
                for g in range(4):
                    ld = self.load(comb[g * DH:(g + 1) * DH, :], self.i["L0_xattn_WvT"], s)
                bank = self.banks[7]
                for g in range(4):
                    for r in range(3):
                        tok = self.pe(lambda e, g=g, r=r: e.matmul(
                            bank.t[DH * g:DH * (g + 1), DH * r:DH * (r + 1)], wq[:], wk[:], start=True,
                            stop=True), ld, bank.free, sig=True)
                bank.free = self.dve(lambda e: e.tensor_copy(m4[:], bank.t[:, 0:QROWS]), tok)
                self.normalized_T(ctx, xn=attT)
                self.prepare_context(mask_k)
                mask_q = self.sbuf(ctx, "mask_q", [P, TT, S2], BF16)

                def emit_query(h, out, *after):
                    rows = slice(DH * (h % 4), DH * (h % 4) + DH)
                    return self.gather(out, [(m4[rows, :], self.xnT[rows, h // 4, :])], *after)

                self.cross_attention(ctx, self.k0, self.i["ctx_heads"], emit_query, comb[:], D ** -0.5,
                                     (mask_q, mask_k), attT, None)
                self.q.emit()
            self.output_projection(attT, "L0_xattn_WoT", "L0_xattn_bo", x_rows)

    def l1_cross(self):
        if self.k1 is None:
            self.prepare_context()
        x_rows = self.nc.dram_tensor("x_kept", [P, TT, D], F32, kind="Internal").ap()
        with ExitStack() as outer:
            attT = self.sbuf(outer, "attT", [P, DT, T], F32)
            with ExitStack() as ctx:
                wq = self.sbuf(ctx, "wq3", [P, DT, H * QROWS], F32)
                comb = self.sbuf(ctx, "comb", [P, DH], F32)
                with ExitStack() as tmp:
                    wq_loaded = self.load(wq[:], self.i["L1_xattn_WqT3"].rearrange("(k p) n -> p k n", p=P),
                                          self.sem("s_wq3"))
                    self.q.wait("sp", self.store(x_rows, self.x[:], self.sem("s_x_kept")))
                    for g in range(4):
                        rows = slice(g * DH, (g + 1) * DH)
                        self.pool(lambda e, rows=rows: e.tensor_copy(comb[rows, :], self.ident[rows, rows]))
                    self.normalized_T(tmp)
                    self.q.emit()

                def emit_query(h, out, *after):
                    cols = slice(h * QROWS, (h + 1) * QROWS)
                    return self.gather(out, [(wq[:, k, cols], self.xnT[:, k, :]) for k in range(DT)], *after,
                                       wq_loaded)

                self.cross_attention(ctx, self.k1, self.v1, emit_query, comb[:], DH ** -0.5, None, attT, None)
                self.q.emit()
            self.output_projection(attT, "L1_xattn_WoT", "L1_xattn_bo", x_rows)

    def l0_scan(self):
        with ExitStack() as outer:
            u = self.sbuf(outer, "u", [P, GT, T], F32)
            zs = self.sbuf(outer, "z_silu", [P, GT, T], F32)
            with ExitStack() as ctx:
                w = self.sbuf(ctx, "in_proj", [P, DT, 2 * DIN], F32)
                xn = self.sbuf(ctx, "xn", [P, TT, D], F32)
                xm = self.sbuf(ctx, "xm", [P, TT, D], F32)
                col = self.sbuf(ctx, "ln_gb", [P, 2, DT], F32)
                cw = self.sbuf(ctx, "conv_w", [P, GT, 4], F32)
                cb = self.sbuf(ctx, "conv_b", [P, GT], F32)
                PAD = 3
                up = [self.sbuf(ctx, "u_pad", [P, PAD + T], F32) for _ in range(3)]
                s_w, s_c = self.sem("s_inw"), self.sem("s_cols")
                ld_w = self.load(w[:], self.i["L0_attn_in_proj_w"].rearrange("(k p) n -> p k n", p=P), s_w)
                self.load(col[:, 0, :], self.i["L0_attn_ln_gC"], s_c)
                self.load(col[:, 1, :], self.i["L0_attn_ln_bC"], s_c)
                self.load(cw[:], self.i["L0_attn_conv_w"].rearrange("(k p) n -> p k n", p=P), s_c)
                ld_c = self.load(cb[:], self.i["L0_attn_conv_bC"], s_c)
                done = self.layernorm(ctx, xn, self.x)
                for i in range(TT):
                    self.dve(lambda e, i=i: e.tensor_tensor(self.x[:, i, :], self.x[:, i, :], xn[:, i, :],
                                                            ALU.add), done)
                done = self.layernorm(ctx, xm, xn, done)
                ready = self.transpose_all(self.xnT, xm, done, ld_c, gain=(col[:, 0, :], col[:, 1, :]))
                up_free = [None] * 3
                pads = [self.pool(lambda e, b=b: e.memset(up[b][:, 0:PAD], 0.0)) for b in range(3)]
                for m in range(2 * GT):
                    bank = self.banks[2 + m % 4]
                    tok = self.gather(bank.t[:], [(w[:, k, m * P:(m + 1) * P], self.xnT[:, k, :])
                                                  for k in range(DT)], ready, ld_w, bank.free)
                    if m >= GT:
                        bank.free = self.act(lambda e, b=bank, m=m: e.activation(zs[:, m - GT, :], b.t[:],
                                                                                 ACT.Silu), tok)
                        continue
                    b = m % 3
                    bank.free = c = self.act(lambda e, k=bank, b=b: e.activation(up[b][:, PAD:], k.t[:], ACT.Copy),
                                             tok, up_free[b])
                    for j in range(4):
                        if j == 0:
                            c = self.dve(lambda e, b=b, m=m: e.tensor_scalar(
                                u[:, m, :], up[b][:, 0:T], cw[:, m, 0:1], None, ALU.mult), c, pads[b], ld_c)
                        else:
                            c = self.dve(lambda e, b=b, m=m, j=j: e.scalar_tensor_tensor(
                                out=u[:, m, :], in0=up[b][:, j:j + T], scalar=cw[:, m, j:j + 1],
                                in1=u[:, m, :], op0=ALU.mult, op1=ALU.add), c)
                    up_free[b] = c
                    self.act(lambda e, m=m: e.activation(u[:, m, :], u[:, m, :], ACT.Silu, bias=cb[:, m:m + 1]), c)
                self.q.emit()
            NH = 4
            with ExitStack() as ctx:
                delta = self.sbuf(ctx, "delta", [P, GT, T], F32)
                du = self.sbuf(ctx, "delta_u", [P, GT, T], F32)
                bc = [self.sbuf(ctx, f"{n}_all", [P, NST, T], F32) for n in "BC"]
                xp = self.sbuf(ctx, "x_proj", [P, GT, DTR + 2 * NST], F32)
                dtw = self.sbuf(ctx, "dt_proj", [DTR, DIN], F32)
                dtb = self.sbuf(ctx, "dt_bias", [P, GT], F32)
                dcol = self.sbuf(ctx, "D_col", [P, GT], F32)
                a = self.sbuf(ctx, "A", [P, GT, NST], F32)
                dbc = self.sbuf(ctx, "dbc", [DTR + 2 * NST, T], F32)
                with ExitStack() as tmp:
                    sel = self.sbuf(tmp, "row_select", [DTR + 2 * NST, 2 * NST, P], F32)
                    mag = self.sbuf(tmp, "minus_abs", [P, GT, T], F32)
                    s = self.sem("s_scanw")
                    self.load(xp[:], self.i["L0_attn_x_proj_w"].rearrange("(k p) n -> p k n", p=P), s)
                    self.load(dtw[:], self.i["L0_attn_dt_proj_w"], s)
                    self.load(dtb[:], self.i["L0_attn_dt_proj_bC"], s)
                    self.load(dcol[:], self.i["L0_attn_DC"], s)
                    ld = self.load(a[:], self.i["L0_attn_A_log"].rearrange("(k p) n -> p k n", p=P), s)
                    ea = self.act(lambda e: e.activation(a[:], a[:], ACT.Exp), ld)
                    self.dve(lambda e: e.tensor_scalar(a[:], a[:], -1.0, None, ALU.mult), ea)
                    rows = DTR + 2 * NST
                    t_sel = self.dve(lambda e: e.tensor_copy(
                        sel[:], self.ident[0:rows, DTR:rows].unsqueeze(2).to_broadcast([rows, 2 * NST, P])))
                    bank = self.banks[0]
                    tok = self.gather(bank.t[0:rows, :], [(xp[:, m, :], u[:, m, :]) for m in range(GT)],
                                      ld, bank.free)
                    t_dbc = bank.free = self.dve(lambda e, b=bank: e.tensor_copy(dbc[:], b.t[0:rows, :]), tok)
                    for m in range(GT):
                        bank = self.banks[1 + m % 2]
                        tok = self.gather(bank.t[:], [(dtw[:, m * P:(m + 1) * P], dbc[0:DTR, :])], t_dbc,
                                          bank.free)
                        bank.free = pre = self.dve(lambda e, b=bank, m=m: e.tensor_scalar(
                            delta[:, m, :], b.t[:], dtb[:, m:m + 1], None, ALU.add), tok)
                    ab = self.act(lambda e: e.activation(mag[:], delta[:], ACT.Abs), pre)
                    ex = self.act(lambda e: e.activation(mag[:], mag[:], ACT.Exp, scale=-1.0), ab)
                    ln = self.act(lambda e: e.activation(mag[:], mag[:], ACT.Ln, bias=1.0), ex)
                    for m in range(GT):
                        d = self.dve(lambda e, m=m: e.scalar_tensor_tensor(
                            out=delta[:, m, :], in0=delta[:, m, :], scalar=0.0, in1=mag[:, m, :], op0=ALU.max,
                            op1=ALU.add), ln)
                        self.dve(lambda e, m=m: e.tensor_tensor(du[:, m, :], delta[:, m, :], u[:, m, :],
                                                                ALU.mult), d)
                    for n in range(2 * NST):
                        bank = self.banks[3 + n % 4]
                        tok = self.gather(bank.t[:], [(sel[:, n, :], dbc[:])], t_sel, t_dbc, bank.free)
                        bank.free = self.act(lambda e, b=bank, n=n: e.activation(
                            bc[n // NST][:, n % NST, :], b.t[:], ACT.Copy), tok)
                    self.q.emit()
                with ExitStack() as tmp:
                    da = [self.sbuf(tmp, "dA", [P, NH, T], F32) for _ in range(2)]
                    n_db = 4
                    db = [self.sbuf(tmp, "dB_u", [P, NH, T], F32) for _ in range(n_db)]
                    da_free, db_free = [None, None], [None] * n_db
                    for m in range(GT):
                        ybank = self.banks[m % 2]
                        for g in range(NST // NH):
                            b, r = g % 2, (m * (NST // NH) + g) % n_db
                            for j in range(NH):
                                n = g * NH + j
                                t_a = self.act(lambda e, b=b, j=j, m=m, n=n: e.activation(
                                    da[b][:, j, :], delta[:, m, :], ACT.Exp, scale=a[:, m, n:n + 1]), da_free[b])
                            t_a = self.dve(lambda e, b=b: e.memset(da[b][:, :, 0:1], 0.0), t_a)
                            t_b = self.pool(lambda e, r=r, m=m, g=g: e.tensor_tensor(
                                db[r][:], du[:, m, :].unsqueeze(1).to_broadcast([P, NH, T]),
                                bc[0][:, g * NH:(g + 1) * NH, :], ALU.mult), db_free[r])
                            t_h = da_free[b] = self.dve(lambda e, b=b, r=r: e.tensor_tensor_scan(
                                out=db[r][:].rearrange("p n t -> p (n t)"),
                                data0=da[b][:].rearrange("p n t -> p (n t)"),
                                data1=db[r][:].rearrange("p n t -> p (n t)"), initial=0.0, op0=ALU.mult,
                                op1=ALU.add), t_a, t_b)
                            t_c = self.dve(lambda e, r=r, g=g: e.tensor_tensor(
                                db[r][:], db[r][:], bc[1][:, g * NH:(g + 1) * NH, :], ALU.mult), t_h)
                            for j in range(NH):
                                first, last = g == 0 and j == 0, g == NST // NH - 1 and j == NH - 1
                                db_free[r] = tok = self.pe(lambda e, r=r, j=j, y=ybank, f=first, z=last: e.matmul(
                                    y.t[:], self.ident[:], db[r][:, j, :], start=f, stop=z), t_c,
                                    ybank.free if first else None, sig=j == NH - 1)
                        y = self.dve(lambda e, m=m, y=ybank: e.scalar_tensor_tensor(
                            out=u[:, m, :], in0=u[:, m, :], scalar=dcol[:, m:m + 1], in1=y.t[:], op0=ALU.mult,
                            op1=ALU.add), tok)
                        ybank.free = y
                        self.dve(lambda e, m=m: e.tensor_tensor(zs[:, m, :], zs[:, m, :], u[:, m, :], ALU.mult), y)
                    self.q.emit()
            with ExitStack() as ctx:
                w = self.sbuf(ctx, "out_proj", [P, GT, D], F32)
                ld = self.load(w[:], self.i["L0_attn_out_proj_w"].rearrange("(k p) n -> p k n", p=P),
                               self.sem("s_outw"))
                self.project_residual(zs, w, None, GT, ld)
                self.q.emit()

    def gate(self, ctx, weights, w_gate, bias_row, softmax, ready):
        s = self.sbuf(ctx, "scores", [P, TT, E], F32)
        before = self.sbuf(ctx, "before", [P, E, E], F32)
        beats = self.sbuf(ctx, "beats", [P, E, E], F32)
        ties = self.sbuf(ctx, "ties", [P, E, E], F32)
        rank = self.sbuf(ctx, "rank", [P, E], F32)
        tot = self.sbuf(ctx, "score_sum", [P, TT], F32)
        one = self.pool(lambda e: e.memset(before[:], 1.0))
        tri = self.pool(lambda e: e.affine_select(out=before[:], in_=before[:], compare_op=ALU.is_gt, fill=0.0,
                                                  base=0, pattern=[[1, E], [-1, E]], channel_multiplier=0), one)
        bank = self.banks[7]
        for i in range(TT):
            terms = [(self.xnT[:, k, i * P:(i + 1) * P], w_gate[:, k, :]) for k in range(DT)]
            if bias_row is not None:
                terms.append((self.ones[0:1, :], bias_row))
            tok = self.gather(bank.t[:, i * E:(i + 1) * E], terms, ready, bank.free)
        logits = bank.t[:, 0:TT * E].rearrange("p (i e) -> p i e", e=E)
        if softmax:
            t = self.dve(lambda e: e.tensor_reduce(tot[:], logits, AXIS_X, ALU.max), tok)
            t = self.dve(lambda e: e.tensor_tensor(s[:], logits, tot[:].unsqueeze(2).to_broadcast([P, TT, E]),
                                                   ALU.subtract), t)
            bank.free = t
            t = self.act(lambda e: e.activation(s[:], s[:], ACT.Exp), t)
            t = self.dve(lambda e: e.tensor_reduce(tot[:], s[:], AXIS_X, ALU.add), t)
            t = self.dve(lambda e: e.reciprocal(tot[:], tot[:]), t)
            t = self.dve(lambda e: e.tensor_tensor(s[:], s[:], tot[:].unsqueeze(2).to_broadcast([P, TT, E]),
                                                   ALU.mult), t)
        else:
            t = bank.free = self.act(lambda e: e.activation(s[:], logits, ACT.Sigmoid), tok)
        yield t
        for i in range(TT):
            mine = s[:, i, :].unsqueeze(2).to_broadcast([P, E, E])
            other = s[:, i, :].unsqueeze(1).to_broadcast([P, E, E])
            t = self.dve(lambda e, a=other, b=mine: e.tensor_tensor(beats[:], a, b, ALU.is_gt), t)
            t = self.dve(lambda e, a=other, b=mine: e.tensor_tensor(ties[:], a, b, ALU.is_equal), t)
            t = self.dve(lambda e: e.tensor_tensor(ties[:], ties[:], before[:], ALU.mult), t, tri)
            t = self.dve(lambda e: e.tensor_tensor(beats[:], beats[:], ties[:], ALU.add), t)
            t = self.dve(lambda e: e.tensor_reduce(rank[:], beats[:], AXIS_X, ALU.add), t)
            t = self.dve(lambda e: e.tensor_scalar(rank[:], rank[:], 1.5, None, ALU.is_lt), t)
            t = self.dve(lambda e, i=i: e.tensor_tensor(weights[:, i, 0:E], s[:, i, :], rank[:], ALU.mult), t)
            t = self.dve(lambda e, i=i: e.tensor_reduce(tot[:, i:i + 1], weights[:, i, 0:E], AXIS_X, ALU.add), t)
            if not softmax:
                t = self.dve(lambda e, i=i: e.tensor_scalar(tot[:, i:i + 1], tot[:, i:i + 1], 1e-6, None,
                                                            ALU.add), t)
            t = self.dve(lambda e, i=i: e.reciprocal(tot[:, i:i + 1], tot[:, i:i + 1]), t)
            t = self.dve(lambda e, i=i: e.tensor_scalar(weights[:, i, 0:E], weights[:, i, 0:E], tot[:, i:i + 1],
                                                        None, ALU.mult), t)
            yield t

    def experts(self, ctx, up_w, down_w, up_b, down_b, weights, acc, func, normalize, gating):
        n_exp = down_b.shape[0]
        n_load = n_exp * NU
        per_exp = NU * FU
        x_part = [self.sbuf(ctx, f"x_{n}", [P, DT, T], F32R) for n in ("hi", "lo")]
        raw = [[self.sbuf(ctx, f"{n}_raw", [P, FU, D], F32) for n in ("up", "down")] for _ in range(2)]
        part = [[[self.sbuf(ctx, f"{n}_{k}", [P, FU, D], F32R) for k in ("hi", "lo")] for n in ("up", "down")]
                for _ in range(2)]
        hidden = [self.sbuf(ctx, "hidden", [P, T], F32) for _ in range(3)]
        h_part = [[self.sbuf(ctx, f"hidden_{k}", [P, T], F32R) for k in ("hi", "lo")] for _ in range(3)]
        wT = self.sbuf(ctx, "weights_T", [n_exp, TT, P], F32)
        s_raw = [[self.sem("s_up"), self.sem("s_down")] for _ in range(2)]
        raw_free = [[None, None], [None, None]]
        part_free = [[None, None], [None, None]]
        part_ready = {}
        loaded = {}

        def load(u):
            for n, src in enumerate((up_w, down_w)):
                loaded[u, n] = self.load(raw[u % 2][n][:], src(*divmod(u, NU)), s_raw[u % 2][n],
                                         raw_free[u % 2][n])

        def split(u, n, hi_on="dve"):
            b = u % 2
            _, raw_free[b][n] = self.split(part[b][n][0][:], part[b][n][1][:], raw[b][n][:], loaded[u, n],
                                           part_free[b][n], hi_on=hi_on)
            part_ready[u, n] = raw_free[b][n]

        hid_ready, hid_free = {}, [None] * 3

        def up(s):
            u, j = divmod(s, FU)
            b, r = u % 2, s % 3
            bank = self.banks[4 + s % 3]
            tok = self.gather(bank.t[:], [(part[b][0][a][:, j, k * P:(k + 1) * P], x_part[c][:, k, :])
                                          for k in range(DT) for a, c in ((0, 0), (0, 1), (1, 0))],
                              part_ready[u, 0], x_ready, bank.free)
            if j == FU - 1:
                part_free[b][0] = tok
            bank.free = t = self.act(lambda e: e.activation(hidden[r][:], bank.t[:], func, bias=up_b[:, s:s + 1]),
                                     tok, hid_free[r])
            t_hi = self.act(lambda e: e.activation(h_part[r][0][:], hidden[r][:], ACT.Copy), t)
            hid_ready[s] = self.dve(lambda e: e.tensor_tensor(h_part[r][1][:], hidden[r][:],
                                                              h_part[r][0][:].bitcast(F32), ALU.subtract), t_hi)

        def down(s):
            u, j = divmod(s, FU)
            b, r = u % 2, s % 3
            first, last = s % per_exp == 0, s % per_exp == per_exp - 1
            for i in range(TT):
                bank = self.banks[i]
                cols = slice(i * P, (i + 1) * P)
                tok = self.gather(bank.t[:], [(h_part[r][a][:, cols], part[b][1][c][:, j, :])
                                              for a, c in ((0, 0), (0, 1), (1, 0))],
                                  hid_ready[s], part_ready[u, 1], bank.free if first else None,
                                  sig=last or i == TT - 1, start=first, stop=last)
                if last:
                    ex = s // per_exp
                    bank.free = self.dve(lambda e, i=i, k=bank: e.scalar_tensor_tensor(
                        out=acc[:, i, :], in0=k.t[:], scalar=weights[:, i, ex:ex + 1], in1=acc[:, i, :],
                        op0=ALU.mult, op1=ALU.add), tok, bank.free)
            hid_free[r] = tok
            if j == FU - 1:
                part_free[b][1] = tok

        load(0)
        load(1)
        ready = normalize()
        _, x_ready = self.split(x_part[0][:], x_part[1][:], self.xnT[:], ready, hi_on="act")
        split(0, 0, hi_on="act")
        split(0, 1, hi_on="act")

        def side_steps():
            for t in gating(ready):
                yield
            bank = self.banks[7]
            for i in range(TT):
                tok = self.pe(lambda e, i=i: e.transpose(bank.t[0:n_exp, i * P:(i + 1) * P], weights[:, i, :],
                                                         self.ident[:]), t, bank.free, sig=i == TT - 1)
            t = bank.free = self.dve(lambda e: e.tensor_copy(
                wT[:], bank.t[0:n_exp, :].rearrange("p (i q) -> p i q", q=P)), tok)
            for i in range(TT):
                yield
                tok = self.gather(bank.t[:], [(wT[:, i, :], down_b[:])], t, bank.free)
                bank.free = self.dve(lambda e, i=i: e.tensor_tensor(acc[:, i, :], acc[:, i, :], bank.t[:],
                                                                    ALU.add), tok)

        side = side_steps()
        for s in range(n_load * FU + 2):
            u, j = divmod(s, FU)
            if s < n_load * FU:
                up(s)
            if s > 0:
                next(side, None)
            if s >= 2:
                down(s - 2)
            if u + 1 < n_load and j in (1, 2):
                split(u + 1, j - 1)
                if j == 2 and u + 2 < n_load:
                    load(u + 2)
        return self.banks[TT - 1].free

    def l0_experts(self):
        n_exp = E + 1
        with ExitStack() as ctx:
            weights = self.sbuf(ctx, "weights", [P, TT, n_exp], F32)
            up_b = self.sbuf(ctx, "up_b", [P, n_exp * FF // P], F32)
            down_b = self.sbuf(ctx, "down_b", [n_exp, D], F32)
            gw = self.sbuf(ctx, "gate_w", [P, DT, E], F32)
            gb = self.sbuf(ctx, "gate_b", [1, E], F32)
            s = self.sem("s_moe0")
            nb = E * FF // P
            self.load(up_b[:, 0:nb], self.i["L0_ffn_buC"], s)
            self.load(up_b[:, nb:], self.i["L0_ffn_sbuC"], s)
            self.load(down_b[0:E, :], self.i["L0_ffn_bd"], s)
            self.load(down_b[E:, :], self.i["L0_ffn_sbd"].rearrange("(o n) -> o n", o=1), s)
            self.load(gw[:], self.i["L0_ffn_gate_wT"].rearrange("(k p) n -> p k n", p=P), s)
            ld = self.load(gb[:], self.i["L0_ffn_gate_bias"].rearrange("(o n) -> o n", o=1), s)
            self.dve(lambda e: e.memset(weights[:, :, E:], 0.1))
            self.q.wait("act", ld)

            def gating(ready):
                self.q.wait("pe", ld)
                return self.gate(ctx, weights, gw, gb[:], False, ready)

            def up_w(e, u):
                return self.i["L0_ffn_Wu"][e, u] if e < E else self.i["L0_ffn_sWu"][u]

            def down_w(e, u):
                return self.i["L0_ffn_Wd"][e, u] if e < E else self.i["L0_ffn_sWd"][u]

            self.experts(ctx, up_w, down_w, up_b, down_b, weights, self.x, ACT.Gelu,
                         lambda: self.normalized_T(ctx)[0], gating)
            self.q.emit()

    def l1_linear(self):
        with ExitStack() as ctx:
            w = {n: self.sbuf(ctx, f"w_{n}", [P, DT, c], F32)
                 for n, c in (("q", LH * P), ("k", LH * P), ("v", D), ("u", D), ("o", D))}
            tab = self.sbuf(ctx, "cos_sin", [P, LH, T], F32)
            qk = [self.sbuf(ctx, "qk_cat", [P, T], F32) for _ in range(4)]
            theta = self.sbuf(ctx, "theta", [P, LH], F32)
            shift = self.sbuf(ctx, "shift", [P, 1], F32)
            bqk = self.sbuf(ctx, "b_qk", [P, 2, LH], F32)
            bu = self.sbuf(ctx, "b_u", [P, DT], F32)
            bv = self.sbuf(ctx, "b_v", [1, D], F32)
            bo = self.sbuf(ctx, "b_o", [1, D], F32)
            slope = self.sbuf(ctx, "slope", [P, LH], F32)
            v = self.sbuf(ctx, "v", [P, TT, D], F32)
            uT = self.sbuf(ctx, "uT", [P, DT, T], F32)
            oT = self.sbuf(ctx, "oT", [P, DT, T], F32)
            tril = self.sbuf(ctx, "tril", [P, TT, T], F32)
            s_c = self.sem("s_linc")
            ld_w = {}
            self.load(theta[:], self.i["L1_attn_theta2"], s_c)
            self.load(bqk[:, 0, :], self.i["L1_attn_b_q2"], s_c)
            self.load(bqk[:, 1, :], self.i["L1_attn_b_k2"], s_c)
            self.load(bu[:], self.i["L1_attn_b_uC"], s_c)
            self.load(bv[:], self.i["L1_attn_b_v"], s_c)
            self.load(bo[:], self.i["L1_attn_out_b"].rearrange("(o n) -> o n", o=1), s_c)
            ld_c = self.load(slope[:], self.i["L1_attn_slope_rate"].rearrange("h a b -> (h a b)")
                             .partition_broadcast(P), s_c)
            for n, key in (("u", "w_uT"), ("v", "w_vT"), ("q", "w_qT2"), ("k", "w_kT2"), ("o", "out_wT")):
                ld_w[n] = self.load(w[n][:], self.i["L1_attn_" + key].rearrange("(k p) n -> p k n", p=P),
                                    self.sem("s_linw"))
            one = self.pool(lambda e: e.memset(tril[:], 1.0))
            for m in range(TT):
                t_tril = self.pool(lambda e, m=m: e.affine_select(
                    out=tril[:, m, :], in_=tril[:, m, :], compare_op=ALU.is_ge, fill=0.0, base=-m * P,
                    pattern=[[1, T]], channel_multiplier=-1), one)
            idx = self.sbuf(ctx, "idx", [P, T], F32)
            turns = self.sbuf(ctx, "turns", [P, T], F32)
            frac = self.sbuf(ctx, "turn_shift", [P, 1], F32)
            e_sb = [self.sbuf(ctx, "energy", [P, T], F32) for _ in range(3)]
            mh = [self.sbuf(ctx, "decay", [P, TT, T], F32) for _ in range(2)]
            t_idx = self.pool(lambda e: e.iota(idx[:], [[1, T]], base=0, channel_multiplier=0,
                                               allow_small_or_imprecise_dtypes=True))
            xn_ready, _ = self.normalized_T(ctx)
            for m in range(DT):
                bank = self.banks[m % 2]
                tok = self.gather(bank.t[:], [(w["u"][:, k, m * P:(m + 1) * P], self.xnT[:, k, :])
                                              for k in range(DT)], xn_ready, ld_w["u"], bank.free)
                bank.free = u_ready = self.act(lambda e, b=bank, m=m: e.activation(
                    uT[:, m, :], b.t[:], ACT.Identity, bias=bu[:, m:m + 1]), tok, ld_c)
            for i in range(TT):
                bank = self.banks[i % 2]
                tok = self.gather(bank.t[:], [(self.xnT[:, k, i * P:(i + 1) * P], w["v"][:, k, :])
                                              for k in range(DT)] + [(self.ones[0:1, :], bv[:])], ld_w["v"],
                                  bank.free)
                bank.free = v_ready = self.act(lambda e, b=bank, i=i: e.activation(v[:, i, :], b.t[:], ACT.Copy),
                                               tok)
            PI = 3.141592653589793
            MAGIC = 12582912.0
            C1 = 6.28125
            C2 = 0.0019350051879882812
            C3 = 2 * PI - C1 - C2
            z = self.pool(lambda e: e.memset(shift[0:LD, :], PI / 2))
            z = self.pool(lambda e: e.memset(shift[LD:, :], 0.0))
            z = self.dve(lambda e: e.tensor_scalar(frac[:], shift[:], 1 / (2 * PI), None, ALU.mult), z)
            for h in range(LH):
                ang = tab[:, h, :]
                t = self.dve(lambda e, h=h, ang=ang: e.tensor_scalar(ang, idx[:], theta[:, h:h + 1], None,
                                                                     ALU.mult), t_idx, ld_c)
                t = self.dve(lambda e, ang=ang: e.tensor_scalar(turns[:], ang, 1 / (2 * PI), frac[:], ALU.mult,
                                                                ALU.add), t, z)
                t = self.dve(lambda e: e.tensor_scalar(turns[:], turns[:], MAGIC, None, ALU.add), t)
                t = self.dve(lambda e: e.tensor_scalar(turns[:], turns[:], MAGIC, None, ALU.subtract), t)
                for c in (C1, C2, C3):
                    t = self.dve(lambda e, ang=ang, c=c: e.scalar_tensor_tensor(
                        out=ang, in0=turns[:], scalar=-c, in1=ang, op0=ALU.mult, op1=ALU.add), t)
                t = self.dve(lambda e, ang=ang: e.tensor_scalar(ang, ang, shift[:], PI, ALU.add, ALU.min), t)
                t = self.dve(lambda e, ang=ang: e.tensor_scalar(ang, ang, -PI, None, ALU.max), t)
                tab_ready = self.act(lambda e, ang=ang: e.activation(ang, ang, ACT.Sin), t)
            self.q.wait("pe", ld_w["q"], ld_w["k"])
            self.q.wait("dve", tab_ready, u_ready)
            self.q.wait("pe", v_ready)
            qk_free, e_free, mh_free = [None, None], [None] * 3, [None, None]
            qk_ready, mh_ready = {}, {}

            def project(h):
                for n, name in enumerate(("q", "k")):
                    bank = self.banks[n]
                    buf = qk[2 * (h % 2) + n]
                    tok = self.gather(bank.t[:], [(w[name][:, k, h * P:(h + 1) * P], self.xnT[:, k, :])
                                                  for k in range(DT)], bank.free)
                    bank.free = t = self.act(lambda e, b=bank, n=n, buf=buf: e.activation(
                        buf[:], b.t[:], ACT.Silu, bias=bqk[:, n, h:h + 1]), tok, qk_free[h % 2])
                    qk_ready[h] = self.dve(lambda e, buf=buf: e.tensor_tensor(buf[:], buf[:], tab[:, h, :],
                                                                              ALU.mult), t)
                mh_ready[h] = self.act(lambda e: e.activation(mh[h % 2][:], tril[:], ACT.Exp,
                                                              scale=slope[:, h:h + 1]), mh_free[h % 2])

            n_e = 0
            project(0)
            for h in range(LH):
                if h + 1 < LH:
                    project(h + 1)
                q_h, k_h = qk[2 * (h % 2)], qk[2 * (h % 2) + 1]
                rows = slice(LD * (h % 2), LD * (h % 2) + LD)
                obank = self.banks[6 + (h // 2) % 2]
                e_ready = []
                for m in range(TT):
                    bank = self.banks[2 + m]
                    tok = self.gather(bank.t[:], [(k_h[:, m * P:(m + 1) * P], q_h[:])], qk_ready[h], bank.free)
                    if m == TT - 1:
                        qk_free[h % 2] = tok
                    r = n_e % 3
                    n_e += 1
                    bank.free = mh_free[h % 2] = self.dve(lambda e, b=bank, r=r, m=m, h=h: e.tensor_tensor(
                        e_sb[r][:], b.t[:], mh[h % 2][:, m, :], ALU.mult), tok, mh_ready[h], e_free[r])
                    e_ready.append((r, bank.free))
                    if m > 0:
                        self.value_rows(obank, rows, v, h, m - 1, e_sb, e_ready, e_free)
                tok = self.value_rows(obank, rows, v, h, TT - 1, e_sb, e_ready, e_free)
                t = self.dve(lambda e, rows=rows, o=obank, h=h: e.tensor_copy(oT[rows, h // 2, :], o.t[rows, :]),
                             tok)
                obank.free = t
            bank = self.banks[0]
            sq = e_sb[0]
            for m in range(DT):
                t_sq = self.dve(lambda e, m=m: e.tensor_tensor(sq[:], oT[:, m, :], oT[:, m, :], ALU.mult), t,
                                e_free[0])
                tok = self.pe(lambda e, m=m: e.matmul(bank.t[:], self.ones[:], sq[:], start=m == 0,
                                                      stop=m == DT - 1), t_sq, bank.free, sig=True)
                e_free[0] = tok
            rs = e_sb[1]
            t = self.dve(lambda e: e.tensor_scalar(rs[:], bank.t[:], 1.0 / D, 1e-6, ALU.mult, ALU.add), tok)
            bank.free = t
            t = self.act(lambda e: e.activation(rs[:], rs[:], ACT.Sqrt), t)
            t_rs = self.dve(lambda e: e.reciprocal(rs[:], rs[:]), t)
            for m in range(DT):
                t = self.dve(lambda e, m=m: e.tensor_tensor(oT[:, m, :], oT[:, m, :], rs[:], ALU.mult), t_rs)
                t = self.dve(lambda e, m=m: e.tensor_tensor(oT[:, m, :], oT[:, m, :], uT[:, m, :], ALU.mult), t)
            self.q.wait("pe", ld_w["o"])
            self.project_residual(oT, w["o"], bo[:], DT, t, first_bank=2)
            self.q.emit()

    def value_rows(self, obank, rows, v, h, m, e_sb, e_ready, e_free):
        r, ready = e_ready[m]
        tok = self.pe(lambda e: e.matmul(obank.t[rows, :], v[:, m, h * LD:(h + 1) * LD], e_sb[r][:],
                                         start=m == 0, stop=m == TT - 1, skip_group_check=True),
                      ready, obank.free, sig=True)
        e_free[r] = tok
        return tok

    def l1_ffn(self):
        with ExitStack() as outer:
            hh = self.sbuf(outer, "h", [P, TT, D], F32)
            weights = self.sbuf(outer, "weights", [P, TT, E], F32)
            up_b = self.sbuf(outer, "up_b", [P, E * FF // P], F32)
            down_b = self.sbuf(outer, "down_b", [E, D], F32)
            gains = [self.sbuf(outer, n, [P, D], F32) for n in ("g1", "b1", "g2", "b2")]
            wo = self.sbuf(outer, "w_o", [P, DT, D], F32)
            gw = self.sbuf(outer, "gate_w", [P, DT, E], F32)
            xn = self.sbuf(outer, "xn", [P, TT, D], F32)
            o = self.sbuf(outer, "o", [P, TT, D], F32)
            s_c = self.sem("s_ffnc")
            with ExitStack() as ctx:
                w = self.sbuf(ctx, "w_qkv", [P, DT, 3 * D], F32)
                qT = self.sbuf(ctx, "qT", [P, DT, T], F32)
                kT = self.sbuf(ctx, "kT", [P, DT, T], F32)
                v = self.sbuf(ctx, "v", [P, TT, D], F32)
                part = [self.sbuf(ctx, n, [P, DT, T], F32R) for n in ("part_hi", "part_lo")]
                stack = [self.sbuf(ctx, n, [QROWS, 4, DT, T], F32R) for n in ("q_stack", "k_stack")]
                causal = self.sbuf(ctx, "causal", [P, (TT - 1) * P + T], F32)
                s_w = self.sem("s_ffnw")
                self.load(w[:], self.i["L1_ffn_w_qkv"].rearrange("(k p) n -> p k n", p=P), s_w)
                self.load(wo[:], self.i["L1_ffn_w_o"].rearrange("(k p) n -> p k n", p=P), s_w)
                self.load(gw[:], self.i["L1_ffn_wg"].rearrange("(k p) n -> p k n", p=P), s_w)
                self.load(up_b[:], self.i["L1_ffn_bb1C"], s_w)
                ld_w = self.load(down_b[:], self.i["L1_ffn_bb2"], s_w)
                for n, key in enumerate(("g1", "b1", "g2", "b2")):
                    ld_c = self.load(gains[n][:], self.i["L1_ffn_" + key].partition_broadcast(P), s_c)
                self.q.wait("sp", ld_c, ld_w)
                z = self.pool(lambda e: e.memset(causal[:], 0.0))
                t_causal = self.pool(lambda e: e.affine_select(
                    out=causal[:], in_=causal[:], compare_op=ALU.is_ge, fill=NEG_BIG, base=(TT - 1) * P,
                    pattern=[[-1, (TT - 1) * P + T]], channel_multiplier=1), z)
                done = self.layernorm(ctx, xn, self.x)
                self.transpose_all(self.xnT, xn, done)
                ready = self.banks[1].free
                s_stack = self.sem("s_stack")
                stacked = []
                for n, (dst, base) in enumerate(((qT, 0), (kT, D))):
                    for m in range(DT):
                        bank = self.banks[2 + m % 2]
                        tok = self.gather(bank.t[:], [(w[:, k, base + m * P:base + (m + 1) * P], self.xnT[:, k, :])
                                                      for k in range(DT)], ready, ld_w, bank.free)
                        bank.free = self.act(lambda e, b=bank, d=dst, m=m: e.activation(d[:, m, :], b.t[:],
                                                                                        ACT.Copy), tok)
                    t_part = self.split(part[0][:], part[1][:], dst[:], bank.free, stacked[-1] if stacked else None)
                    for r, lo in enumerate(((0, 1, 0), (0, 0, 1))[n]):
                        for g in range(4):
                            stacked.append(self.load(
                                stack[n][r * DH:(r + 1) * DH, g, :, :].bitcast(F32),
                                part[lo][g * DH:(g + 1) * DH, :, :].bitcast(F32), s_stack, t_part[1]))
                for i in range(TT):
                    bank = self.banks[2 + i % 2]
                    tok = self.gather(bank.t[:], [(self.xnT[:, k, i * P:(i + 1) * P], w[:, k, 2 * D:])
                                                  for k in range(DT)], bank.free)
                    bank.free = self.act(lambda e, b=bank, i=i: e.activation(v[:, i, :], b.t[:], ACT.Copy), tok)
                proj = bank.free
                NB = 3
                s_sb = [self.sbuf(ctx, "s", [P, T], F32) for _ in range(NB)]
                pT = [self.sbuf(ctx, "probT", [P, TT, P], F32) for _ in range(NB)]
                top = self.sbuf(ctx, "top", [P, TT, H], F32)
                den = self.sbuf(ctx, "den", [P, TT, H], F32)
                s_free, pT_free = [None] * NB, [None] * NB
                exp_ready, pT_ready = {}, {}
                scale = DH ** -0.5
                todo = [(i, h) for i in range(TT) for h in range(H)]

                def scores(n):
                    i, h = todo[n]
                    b, width = n % NB, (i + 1) * P
                    bank = self.banks[2 + n % 2]
                    tok = self.gather(bank.t[:, 0:width], [(stack[0][:, h % 4, h // 4, i * P:(i + 1) * P],
                                                            stack[1][:, h % 4, h // 4, 0:width])],
                                      proj, stacked[-1], bank.free)
                    off = (TT - 1 - i) * P
                    bank.free = t = self.dve(lambda e: e.tensor_tensor_reduce(
                        out=s_sb[b][:, 0:width], in0=bank.t[:, 0:width], in1=causal[:, off:off + width],
                        scale=1.0, scalar=-3.0e38, op0=ALU.add, op1=ALU.max, accum_out=top[:, i, h:h + 1]),
                        tok, s_free[b], t_causal)
                    t = self.dve(lambda e: e.tensor_scalar(top[:, i, h:h + 1], top[:, i, h:h + 1], -scale, None,
                                                           ALU.mult), t)
                    exp_ready[n] = self.act(lambda e: e.activation(
                        s_sb[b][:, 0:width], s_sb[b][:, 0:width], ACT.Exp, scale=scale, bias=top[:, i, h:h + 1],
                        accum_out=den[:, i, h:h + 1]), t)

                def turn(n):
                    i, h = todo[n]
                    b = n % NB
                    bank = self.banks[4 + n % 2]
                    for k in range(i + 1):
                        tok = self.pe(lambda e, k=k: e.transpose(bank.t[:, k * P:(k + 1) * P],
                                                                 s_sb[b][:, k * P:(k + 1) * P], self.ident[:]),
                                      exp_ready[n], bank.free, sig=k == i)
                    s_free[b] = tok
                    bank.free = pT_ready[n] = self.act(lambda e: e.activation(
                        pT[b][:, 0:i + 1, :], bank.t[:, 0:(i + 1) * P].rearrange("p (k q) -> p k q", q=P),
                        ACT.Copy), tok, pT_free[b])

                def values(n):
                    i, h = todo[n]
                    b = n % NB
                    bank = self.banks[6 + i % 2]
                    cols = slice(h * DH, (h + 1) * DH)
                    tok = self.gather(bank.t[:, cols], [(pT[b][:, k, :], v[:, k, cols]) for k in range(i + 1)],
                                      pT_ready[n], bank.free)
                    pT_free[b] = tok
                    if h == H - 1:
                        t = self.dve(lambda e: e.reciprocal(den[:, i, :], den[:, i, :]), tok, exp_ready[n])
                        bank.free = self.dve(lambda e: e.tensor_tensor(
                            o[:, i, :].rearrange("p (h d) -> p h d", d=DH),
                            bank.t[:].rearrange("p (h d) -> p h d", d=DH),
                            den[:, i, :].unsqueeze(2).to_broadcast([P, H, DH]), ALU.mult), t)

                for n in range(len(todo) + 2):
                    if n < len(todo):
                        scores(n)
                    if 1 <= n <= len(todo):
                        turn(n - 1)
                    if n >= 2:
                        values(n - 2)
                self.q.emit()
            with ExitStack() as ctx:
                def normalize():
                    t_oT = self.transpose_all(self.xnT, o, None)
                    for i in range(TT):
                        bank = self.banks[2 + i]
                        tok = self.gather(bank.t[:], [(self.xnT[:, k, i * P:(i + 1) * P], wo[:, k, :])
                                                      for k in range(DT)], t_oT, bank.free)
                        bank.free = t = self.dve(lambda e, b=bank, i=i: e.tensor_tensor(
                            o[:, i, :], xn[:, i, :], b.t[:], ALU.add), tok)
                    t = self.layernorm(ctx, hh, o, t)
                    t = self.affine(hh, gains[0], gains[1], t)
                    return self.transpose_all(self.xnT, hh, t)

                self.experts(ctx, lambda e, u: self.i["L1_ffn_w1"][e, u], lambda e, u: self.i["L1_ffn_w2"][e, u],
                             up_b, down_b, weights, hh, ACT.Gelu_apprx_tanh, normalize,
                             lambda ready: self.gate(ctx, weights, gw, None, True, ready))
                self.q.emit()
            with ExitStack() as ctx:
                y = self.sbuf(ctx, "y", [P, TT, D], F32)
                t = self.layernorm(ctx, y, hh)
                t = self.affine(y, gains[2], gains[3], t)
                self.dve(lambda e: e.tensor_tensor(self.x[:], self.x[:], y[:], ALU.add), t)
                self.q.emit()

    def affine(self, dst, g, b, *after):
        for i in range(TT):
            t = self.dve(lambda e, i=i: e.tensor_tensor(dst[:, i, :], dst[:, i, :], g[:], ALU.mult), *after)
            t = self.dve(lambda e, i=i: e.tensor_tensor(dst[:, i, :], dst[:, i, :], b[:], ALU.add), t)
        return t


def perceiver_kernel(nc, ins, out, stages):
    with ExitStack() as ctx:
        k = Kernel(nc, ins, out, ctx)
        k.constants()
        k.q.emit()
        for stage in stages:
            stage(k)
        k.finish()


STAGES = (Kernel.l0_cross, Kernel.l0_scan, Kernel.l0_experts, Kernel.l1_cross,
          Kernel.l1_linear, Kernel.l1_ffn)


def _laid_out(inputs):
    import numpy as np
    a = {k: np.asarray(v) for k, v in inputs.items()}

    def columns(v):
        return v.reshape(-1, P).T

    def up(w):
        e = w.shape[0]
        w = w.reshape(e, DT, P, NU, FU, P)
        return w.transpose(0, 3, 2, 4, 1, 5).reshape(e, NU, P, FU, D)

    def down(w):
        e = w.shape[0]
        return w.reshape(e, NU, FU, P, D).transpose(0, 1, 3, 2, 4)

    ctx = a["ctx_1024"][0]
    mask = a["mask_Bx1xSxS2_ik1"][0, 0]
    d = {"x": a["x"], "ctxT": ctx.T, "mask": mask, "maskT": mask.T,
         "ctx_heads": ctx.reshape(KT, P, H, DH).transpose(2, 1, 0, 3).reshape(H, P, KT * DH)}
    for k in ("L0_xattn_Wq", "L0_xattn_Wk", "L0_xattn_bo", "L0_attn_in_proj_w", "L0_attn_conv_w",
              "L0_attn_x_proj_w", "L0_attn_dt_proj_w", "L0_attn_A_log", "L0_attn_out_proj_w", "L0_ffn_bd",
              "L0_ffn_sbd", "L0_ffn_gate_bias", "L1_xattn_bo", "L1_attn_slope_rate", "L1_attn_out_b",
              "L1_ffn_w_qkv", "L1_ffn_w_o", "L1_ffn_wg", "L1_ffn_bb2", "L1_ffn_g1", "L1_ffn_b1", "L1_ffn_g2",
              "L1_ffn_b2"):
        d[k] = a[k]
    for k in ("L0_xattn_Wv", "L0_xattn_Wo", "L1_xattn_Wk", "L1_xattn_Wv", "L1_xattn_Wo", "L0_ffn_gate_w",
              "L1_attn_out_w"):
        d[k + "T"] = a[k].T
    for k in ("L0_attn_ln_g", "L0_attn_ln_b", "L0_attn_conv_b", "L0_attn_dt_proj_b", "L0_attn_D"):
        d[k + "C"] = columns(a[k])
    d["L0_ffn_buC"] = columns(a["L0_ffn_bu"].reshape(-1))
    d["L0_ffn_sbuC"] = columns(a["L0_ffn_sbu"])
    d["L1_ffn_bb1C"] = columns(a["L1_ffn_bb1"].reshape(-1))
    d["L1_xattn_WqT3"] = np.tile(a["L1_xattn_Wq"].T.reshape(D, H, 1, DH), (1, 1, 3, 1)).reshape(D, H * QROWS)
    d["L0_ffn_Wu"] = up(a["L0_ffn_Wu"].transpose(0, 2, 1))
    d["L0_ffn_sWu"] = up(a["L0_ffn_sWu"].T[None])[0]
    d["L0_ffn_Wd"] = down(a["L0_ffn_Wd"].transpose(0, 2, 1))
    d["L0_ffn_sWd"] = down(a["L0_ffn_sWd"].T[None])[0]
    d["L1_ffn_w1"] = up(a["L1_ffn_w1"])
    d["L1_ffn_w2"] = down(a["L1_ffn_w2"])
    w = a["L1_attn_qkvu_w"].reshape(4, D, D)
    b = a["L1_attn_qkvu_b"].reshape(4, D)
    for n, k in ((0, "q"), (1, "k")):
        d[f"L1_attn_w_{k}T2"] = np.tile(w[n].T.reshape(D, LH, 1, LD), (1, 1, 2, 1)).reshape(D, LH * P)
        d[f"L1_attn_b_{k}2"] = np.tile(b[n].reshape(LH, LD), (1, 2)).T
    d["L1_attn_w_vT"], d["L1_attn_w_uT"] = w[2].T, w[3].T
    d["L1_attn_b_v"], d["L1_attn_b_uC"] = b[2:3], columns(b[3])
    d["L1_attn_theta2"] = np.tile(a["L1_attn_theta"].reshape(LH, LD), (1, 2)).T
    return d


def kernel(**inputs):
    import numpy as np
    import concourse.bacc as bacc
    from concourse.bass_utils import run_bass_kernel_spmd

    nc = bacc.Bacc("TRN2", target_bir_lowering=False, num_devices=1)
    arrays, aps = {}, {}
    for name, value in _laid_out(inputs).items():
        value = np.ascontiguousarray(value)
        arrays["in_" + name] = value
        aps[name] = nc.dram_tensor("in_" + name, value.shape, mybir.dt.from_np(value.dtype),
                                   kind="ExternalInput").ap()
    out = nc.dram_tensor("out_x", (1, T, D), F32, kind="ExternalOutput").ap()
    perceiver_kernel(nc, aps, out, STAGES)
    r = run_bass_kernel_spmd(nc, [arrays], core_ids=[0])
    return r.results[0]["out_x"]
```

```python
from contextlib import ExitStack

import concourse.bass as bass
from concourse import mybir

F32 = mybir.dt.float32
F32R = mybir.dt.float32r
BF16 = mybir.dt.bfloat16
F8 = mybir.dt.float8e4
I32 = mybir.dt.int32
ALU = mybir.AluOpType
ACT = mybir.ActivationFunctionType
AXIS_X = mybir.AxisListType.X

P = 128
T = 512
D = 512
S2 = 8192
TT = T // P
DT = D // P
H = 16
DH = D // H
E = 8
FF = 2048
BIG = 2.0 ** 67
NEG_BIG = -BIG

KC = 512
NKC = S2 // KC
LEAD = 1
KRING = NKC + LEAD + 2
KT = S2 // P
QROWS = 3 * DH

DEN_TURNS = 5

DIN = 1024
NST = 16
DTR = 32
GT = DIN // P

LH = 8
LD = D // LH

FU = 4
NU = FF // (FU * P)


class EngineQueues:

    NAMES = ("pe", "act", "dve", "pool", "sp")

    def __init__(self, nc, ctx):
        self.nc = nc
        self.sem = {n: ctx.enter_context(nc.semaphore("s_" + n)) for n in self.NAMES}
        self.count = {n: 0 for n in self.NAMES}
        self.dma_count = {}
        self.items = {n: [] for n in self.NAMES}
        self.waited = {n: {} for n in self.NAMES}
        self.stores = {}

    def wait(self, eng, *after):
        for token in after:
            if token is None:
                continue
            name, sem, value = token
            if self.waited[eng].get(name, 0) < value:
                self.waited[eng][name] = value
                self.items[eng].append(("wait", sem, value))

    def do(self, eng, fn, *after, sig=True):
        self.wait(eng, *after)
        if sig:
            self.count[eng] += 1
            self.items[eng].append(("op", fn, self.sem[eng], 1))
            return (eng, self.sem[eng], self.count[eng])
        self.items[eng].append(("op", fn, None, 0))
        return None

    def dma(self, eng, out, in_, sem, *after, store=False):
        self.wait(eng, *after)
        name = sem.name
        self.dma_count[name] = self.dma_count.get(name, 0) + 16
        self.items[eng].append(("op", lambda e: e.dma_start(out, in_), sem, 16))
        token = (name, sem, self.dma_count[name])
        if store:
            self.stores[name] = token
        return token

    def emit(self):
        items, self.items = self.items, {n: [] for n in self.NAMES}
        with self.nc.Block() as block:
            for name, where in (("sp", block.sync), ("pe", block.tensor), ("act", block.scalar),
                                ("dve", block.vector), ("pool", block.gpsimd)):
                if not items[name]:
                    continue

                def run(eng, todo=items[name]):
                    for item in todo:
                        if item[0] == "wait":
                            eng.wait_ge(item[1], item[2])
                        else:
                            ins = item[1](eng)
                            if item[2] is not None:
                                ins.then_inc(item[2], item[3])

                where(run)


class Bank:

    def __init__(self, tensor):
        self.t = tensor
        self.free = None


class Kernel:
    def __init__(self, nc, ins, out, ctx):
        self.nc = nc
        self.i = ins
        self.out = out
        self.ctx = ctx
        self.q = EngineQueues(nc, ctx)
        self.nsem = 0
        self.last_pool = None
        self.k1 = None
        self.ntmp = 0
        sb = self.sbuf
        self.ident = sb(ctx, "ident", [P, P], F32)
        self.ident_big = sb(ctx, "ident_big", [P, P], BF16)
        self.ones = sb(ctx, "ones", [P, P], F32)
        self.x = sb(ctx, "x", [P, TT, D], F32)
        self.xnT = sb(ctx, "xnT", [P, DT, T], F32)
        self.x_done = [None] * TT
        self.psum = ctx.enter_context(nc.psum_tensor("psum", [P, 8, 512], F32))
        self.banks = [Bank(self.psum[:, i, :]) for i in range(8)]

    def sbuf(self, ctx, name, shape, dt):
        self.ntmp += 1
        return ctx.enter_context(self.nc.sbuf_tensor(f"{name}_{self.ntmp}", shape, dt))

    def sem(self, name):
        self.nsem += 1
        return self.ctx.enter_context(self.nc.semaphore(f"{name}_{self.nsem}"))

    def pe(self, fn, *after, sig=False):
        return self.q.do("pe", fn, *after, sig=sig)

    def act(self, fn, *after, sig=True):
        return self.q.do("act", fn, *after, sig=sig)

    def dve(self, fn, *after, sig=True):
        return self.q.do("dve", fn, *after, sig=sig)

    def pool(self, fn, *after):
        self.last_pool = self.q.do("pool", fn, *after, self.last_pool)
        return self.last_pool

    def load(self, out, in_, sem, *after, eng="sp"):
        return self.q.dma(eng, out, in_, sem, *after)

    def store(self, out, in_, sem, *after, eng="sp"):
        return self.q.dma(eng, out, in_, sem, *after, store=True)

    def gather(self, out, terms, *after, sig=True, start=True, stop=True):
        token = None
        for n, (lhsT, rhs) in enumerate(terms):
            last = n == len(terms) - 1
            token = self.pe(lambda e, a=lhsT, b=rhs, s=start and n == 0, z=stop and last:
                            e.matmul(out, a, b, start=s, stop=z), *(after if n == 0 else ()), sig=last and sig)
        return token

    def split(self, hi, lo, src, *after, hi_on="dve"):
        if hi_on == "act":
            t_hi = self.act(lambda e: e.activation(hi, src, ACT.Copy), *after)
        else:
            t_hi = self.dve(lambda e: e.tensor_copy(hi, src), *after)
        t_lo = self.dve(lambda e: e.tensor_tensor(lo, src, hi.bitcast(F32), ALU.subtract), t_hi, *after)
        return t_hi, t_lo

    def constants(self):
        zero = self.pool(lambda e: e.memset(self.ident[:], 0.0))
        self.pool(lambda e: e.affine_select(out=self.ident[:], in_=self.ident[:], compare_op=ALU.not_equal,
                                            fill=1.0, base=0, pattern=[[-1, P]], channel_multiplier=1), zero)
        zero = self.pool(lambda e: e.memset(self.ident_big[:], 0.0))
        self.pool(lambda e: e.affine_select(out=self.ident_big[:], in_=self.ident_big[:],
                                            compare_op=ALU.not_equal, fill=BIG, base=0, pattern=[[-1, P]],
                                            channel_multiplier=1), zero)
        self.pool(lambda e: e.memset(self.ones[:], 1.0))
        self.q.wait("sp", self.load(self.x[:], self.i["x"].rearrange("o (i p) d -> p (o i) d", p=P),
                                    self.sem("s_x")))

    def finish(self):
        rows = self.out.rearrange("o (i p) d -> p (o i) d", p=P)
        for i in range(TT):
            self.store(rows[:, i, :], self.x[:, i, :], self.sem("s_out"), self.x_done[i])
        self.q.wait("sp", *self.q.stores.values())
        self.q.emit()

    def layernorm(self, ctx, dst, src, *after, gain=None, plus=None):
        stats = self.sbuf(ctx, "ln_stats", [P, TT, 6], F32)
        mv = self.sbuf(ctx, "ln_mean_var", [P, TT, 2], F32)
        rstd = self.sbuf(ctx, "ln_rstd", [P, TT], F32)
        for i in range(TT):
            st = self.dve(lambda e, i=i: e.bn_stats(stats[:, i, :], src[:, i, :]), *after)
        for i in range(TT):
            agg = self.dve(lambda e, i=i: e.bn_aggr(mv[:, i, :], stats[:, i, :]), st)
        eps = self.dve(lambda e: e.tensor_scalar(rstd[:], mv[:, :, 1], 1e-5, None, ALU.add), agg)
        root = self.act(lambda e: e.activation(rstd[:], rstd[:], ACT.Sqrt), eps)
        if gain is not None:
            scaled = [self.dve(lambda e, i=i: e.scalar_tensor_tensor(
                out=src[:, i, :], in0=src[:, i, :], scalar=mv[:, i, 0:1], in1=gain[:], op0=ALU.subtract,
                op1=ALU.mult), agg) for i in range(TT)]
        rec = self.dve(lambda e: e.reciprocal(rstd[:], rstd[:]), root)
        if gain is not None:
            return [self.dve(lambda e, i=i: e.scalar_tensor_tensor(
                out=dst[:, i, :], in0=src[:, i, :], scalar=rstd[:, i:i + 1], in1=plus(i), op0=ALU.mult,
                op1=ALU.add), rec, scaled[i]) for i in range(TT)]
        for i in range(TT):
            done = self.dve(lambda e, i=i: e.tensor_scalar(dst[:, i, :], src[:, i, :], mv[:, i, 0:1],
                                                           rstd[:, i:i + 1], ALU.subtract, ALU.mult), rec)
        return done

    def transpose_all(self, dstT, src, *after, gain=None):
        for c in range(DT):
            bank = self.banks[c % 2]
            for i in range(TT):
                tr = self.pe(lambda e, b=bank, c=c, i=i: e.transpose(
                    b.t[:, i * P:(i + 1) * P], src[:, i, c * P:(c + 1) * P], self.ident[:]),
                    *after, bank.free, sig=i == TT - 1)
            if gain is None:
                bank.free = self.dve(lambda e, b=bank, c=c: e.tensor_copy(dstT[:, c, :], b.t[:]), tr)
            else:
                bank.free = self.dve(lambda e, b=bank, c=c: e.tensor_scalar(
                    dstT[:, c, :], b.t[:], gain[0][:, c:c + 1], gain[1][:, c:c + 1], ALU.mult, ALU.add), tr)
        return bank.free

    def normalized_T(self, ctx, *after, xn=None):
        if xn is None:
            xn = self.sbuf(ctx, "xn", [P, TT, D], F32)
        done = self.layernorm(ctx, xn, self.x, *after)
        return self.transpose_all(self.xnT, xn, done), xn

    def project_residual(self, lhsT, w, bias_row, kt, *after, first_bank=0):
        for i in range(TT):
            bank = self.banks[first_bank + i]
            terms = [(lhsT[:, k, i * P:(i + 1) * P], w[k]) for k in range(kt)]
            if bias_row is not None:
                terms.append((self.ones[0:1, :], bias_row))
            tok = self.gather(bank.t[:], terms, *after, bank.free)
            bank.free = self.dve(lambda e, b=bank, i=i: e.tensor_tensor(
                self.x[:, i, :], self.x[:, i, :], b.t[:], ALU.add), tok)
        return bank.free

    def prepare_context(self, mask_k=None, spare=None, meanwhile=()):
        nc, i = self.nc, self.i
        self.k0 = [nc.dram_tensor(f"k0_{n}", [D, S2], F32, kind="Internal").ap() for n in ("hi", "lo")]
        self.k1 = [nc.dram_tensor(f"k1_{n}", [D, S2], F32, kind="Internal").ap() for n in ("hi", "lo")]
        self.v1 = nc.dram_tensor("v1_heads", [H, P, KT * DH], F32, kind="Internal").ap()
        CH = 512
        VT = CH // P
        STEPS = S2 // CH
        with ExitStack() as ctx:
            wk = [self.sbuf(ctx, f"wk{n}", [P, DT, D], F32R) for n in ("hi", "lo")]
            wv = [self.sbuf(ctx, f"wv{n}", [P, DT, D], F32R) for n in ("hi", "lo")]
            raw = [self.sbuf(ctx, "ctxT", [P, DT, CH], F32) for _ in range(2)]
            cx = [[self.sbuf(ctx, f"ctx{n}", [P, DT, CH], F32R) for n in ("hi", "lo")] for _ in range(2)]
            kst = [[self.sbuf(ctx, f"k1{n}", [P, DT, CH], F32R) for n in ("hi", "lo")] for _ in range(2)]
            vst = [self.sbuf(ctx, "v1", [P, H, VT, DH], F32) for _ in range(2)]
            s_raw = [self.sem("s_raw") for _ in range(2)]
            s_k0 = [self.sem("s_k0") for _ in range(2)]
            s_out = [self.sem("s_k1v1") for _ in range(2)]
            raw_free = [None, None]
            cx_free = [(), ()]
            st_free = [None, None]
            ctxT = i["ctxT"].rearrange("(k p) n -> p k n", p=P)
            loaded, split_done = {}, {}
            if mask_k is not None:
                m_raw = [self.sbuf(ctx, "mask_raw", [P, VT, T], I32)[:], spare[:].bitcast(I32)]
                s_m = [self.sem("s_mask_k") for _ in range(2)]
                m_free = [None, None]
                maskT = i["maskT"].rearrange("(k p) q -> p k q", p=P)
            m_loaded = {}

            def load_mask(s):
                if mask_k is not None and s < STEPS:
                    m_loaded[s] = self.load(m_raw[s % 2], maskT[:, s * VT:(s + 1) * VT, :], s_m[s % 2],
                                            m_free[s % 2])

            def load(s):
                b = s % 2
                loaded[s] = self.load(raw[b][:], ctxT[:, :, s * CH:(s + 1) * CH], s_raw[b], raw_free[b])

            def split(s):
                b = s % 2
                _, raw_free[b] = self.split(cx[b][0][:], cx[b][1][:], raw[b][:], loaded[s], *cx_free[b])
                split_done[s] = raw_free[b]

            w_in, s_w = kst[1], [self.sem("s_wk"), self.sem("s_wv")]
            w_split = []
            for n, (name, parts) in enumerate((("L1_xattn_WkT", wk), ("L1_xattn_WvT", wv))):
                ld = self.load(w_in[n][:].bitcast(F32), i[name].rearrange("(k p) n -> p k n", p=P), s_w[n])
                load(n)
                w_split.append(self.split(parts[0][:], parts[1][:], w_in[n][:].bitcast(F32), ld,
                                          hi_on="act")[1])
                if n == 0:
                    split(0)
            w_ready, st_free[1] = w_split[0], w_split[1]
            load_mask(0)
            for s in range(STEPS):
                b = s % 2
                cols = slice(s * CH, (s + 1) * CH)
                if s + 2 < STEPS:
                    load(s + 2)
                load_mask(s + 1)
                for n in range(2):
                    k0_st = self.store(self.k0[n].rearrange("(k p) n -> p k n", p=P)[:, :, cols],
                                       cx[b][n][:].bitcast(F32), s_k0[b], split_done[s])
                if s + 1 < STEPS:
                    split(s + 1)
                if mask_k is not None:
                    m_free[b] = self.dve(lambda e, s=s, b=b: e.tensor_scalar(
                        mask_k[:, s * VT:(s + 1) * VT, :], m_raw[b], 0, -1.0, ALU.is_equal, ALU.mult,
                        saturate=False), m_loaded[s])
                for m in range(DT):
                    bank = self.banks[m]
                    rows = slice(m * P, (m + 1) * P)
                    tok = self.gather(bank.t[:], [
                        (wk[a][:, k, rows], cx[b][c][:, k, :])
                        for k in range(DT) for a, c in ((0, 0), (0, 1), (1, 0))], split_done[s], w_ready,
                        bank.free)
                    _, bank.free = self.split(kst[b][0][:, m, :], kst[b][1][:, m, :], bank.t[:], tok,
                                              st_free[b], hi_on="act")
                k_done = bank.free
                for t in range(VT):
                    bank = self.banks[4 + t]
                    rows = slice(t * P, (t + 1) * P)
                    tok = self.gather(bank.t[:], [
                        (cx[b][c][:, k, rows], wv[a][:, k, :])
                        for k in range(DT) for a, c in ((0, 0), (0, 1), (1, 0))], w_split[1], bank.free)
                    bank.free = self.act(lambda e, bank=bank, b=b, t=t: e.activation(
                        vst[b][:, :, t, :], bank.t[:].rearrange("p (h d) -> p h d", h=H), ACT.Copy),
                        tok, st_free[b])
                cx_free[b] = (tok, k0_st)
                for n in range(2):
                    self.store(self.k1[n].rearrange("(k p) n -> p k n", p=P)[:, :, cols],
                               kst[b][n][:].bitcast(F32), s_out[b], k_done)
                st_free[b] = self.store(self.v1.rearrange("h p n -> p h n")[:, :, s * VT * DH:(s + 1) * VT * DH],
                                        vst[b][:].rearrange("p h t d -> p h (t d)"), s_out[b], bank.free)
                if 1 <= s <= len(meanwhile):
                    meanwhile[s - 1](ctx)
            self.q.wait("sp", st_free[0], st_free[1], cx_free[0][1], cx_free[1][1])
            self.q.emit()

    def cross_attention(self, ctx, k_hi_lo, v_heads, v_first, w_out, bias, x_rows, emit_query, comb,
                        scale, masks, attT):
        rows_q = slice(0, QROWS)
        rows_m = slice(QROWS, QROWS + 2)
        n_q, n_p = 3, 4 if masks else 8
        q_stack = [self.sbuf(ctx, "q_stack", [QROWS + 2, T], F32R) for _ in range(n_q)]
        k_ring = self.sbuf(ctx, "k_ring", [QROWS + 2, KRING, KC], F32R)
        v_buf = [v_first[:].rearrange("p k n -> p (k n)"), self.x[:].rearrange("p i d -> p (i d)")]
        prob = [self.sbuf(ctx, "prob", [P, 2, T], F32) for _ in range(n_p)]
        trash = [self.sbuf(ctx, "max_trash", [P, KC], BF16) for _ in range(2)] if masks else None
        row_max = [self.sbuf(ctx, "row_max", [P, TT, NKC], F32) for _ in range(2)]
        top2 = self.sbuf(ctx, "row_top2", [P, TT, 2], F32)
        den_part = {e: self.sbuf(ctx, "den_" + e, [P, 2, T], F32) for e in ("pool", "dve")}
        small = self.sbuf(ctx, "bias_and_m_hi", [QROWS + 2, T], F32)
        bias_row, m_hi = small[0:1, :], small[rows_m, :].bitcast(F32R)
        den4 = self.sbuf(ctx, "den_of_4_heads", [P, T], F32)
        lo_sign = self.sbuf(ctx, "lo_sign", [QROWS + 2, 1], F32)
        o_sb = self.sbuf(ctx, "o_sb", [P, T], F32)
        s_k = [self.sem("s_k") for _ in range(KRING)]
        s_v = [self.sem("s_v") for _ in range(2)]
        ring_init = self.pool(lambda e: e.memset(k_ring[rows_m, :, :].bitcast(F32), -1.0))
        self.pool(lambda e: e.memset(lo_sign[rows_m, :], -1.0))
        consts = self.pool(lambda e: e.memset(lo_sign[QROWS:QROWS + 1, :], 0.0))

        score = [(self.banks[0], self.banks[1]), (self.banks[2], self.banks[3])]
        maxbank = [self.banks[4], self.banks[5]]
        vbank, misc = self.banks[6], self.banks[7]

        k_loaded, k_used = {}, {}
        v_ready, v_used = {}, {}
        q_ready, m_ready = {}, {}
        exp_done = {}
        prob_free = [()] * n_p
        den_added = {"pool": None, "dve": None}
        last = {"top2": None, "o_sb": None, "den": None, "den4": None}

        def load_k(n):
            h, c = divmod(n, NKC)
            if h >= H:
                return
            slot = n % KRING
            rows, cols = slice(h * DH, (h + 1) * DH), slice(c * KC, (c + 1) * KC)
            for g, part in enumerate((0, 0, 1)):
                k_loaded[n] = self.load(k_ring[g * DH:(g + 1) * DH, slot, :].bitcast(F32),
                                        k_hi_lo[part][rows, cols], s_k[slot], k_used.get(n - KRING))

        def load_v(h):
            if h >= H:
                return
            v_ready[h] = self.load(v_buf[h % 2], v_heads[h], s_v[h % 2], v_used.get(h - 2))

        def query(h):
            if h >= H:
                return
            tok = emit_query(h, misc.t[rows_q, :], misc.free)
            qs = q_stack[h % n_q]
            hi = self.act(lambda e: e.activation(qs[rows_q, :], misc.t[rows_q, :], ACT.Copy), tok,
                          k_used.get((h - n_q + 1) * NKC - 1))
            misc.free = q_ready[h] = self.dve(lambda e: e.tensor_tensor(
                qs[DH:2 * DH, :], misc.t[DH:2 * DH, :], qs[DH:2 * DH, :].bitcast(F32), ALU.subtract), hi)

        def max_step(n, i):
            h, c = divmod(n, NKC)
            if h >= H:
                return
            bank = maxbank[i % 2]
            tok = self.gather(bank.t[:], [(q_stack[h % n_q][rows_q, i * P:(i + 1) * P],
                                           k_ring[rows_q, n % KRING, :])], q_ready[h], k_loaded[n], bank.free)
            out = row_max[h % 2][:, i, c:c + 1]
            if masks is None:
                bank.free = self.dve(lambda e: e.reduce_max(out, bank.t[:], AXIS_X), tok)
            else:
                bank.free = self.dve(lambda e: e.tensor_tensor_reduce(
                    out=trash[i % 2][:], in0=bank.t[:], in1=masks[0][:, i, c * KC:(c + 1) * KC], scale=1.0,
                    scalar=-3.0e38, op0=ALU.add, op1=ALU.max, accum_out=out), tok, bank.free,
                    mask_ready[c])

        def top_of_rows(h):
            t = self.dve(lambda e: e.tensor_reduce(top2[:, :, 0:1], row_max[h % 2][:], AXIS_X, ALU.max),
                         maxbank[0].free, maxbank[1].free, last["top2"])
            return self.dve(lambda e: e.tensor_copy(top2[:, :, 1:2], top2[:, :, 0:1]), t)

        def max_rows(h, t):
            for i in range(TT):
                tok = self.pe(lambda e, i=i: e.matmul(misc.t[rows_m, i * P:(i + 1) * P], top2[:, i, :],
                                                      self.ident[:], start=True, stop=True),
                              t, misc.free, sig=i == TT - 1)
            last["top2"] = tok
            hi = self.act(lambda e: e.activation(m_hi, misc.t[rows_m, :], ACT.Copy), tok, m_ready.get(h - 1))
            misc.free = m_ready[h] = self.dve(lambda e: e.scalar_tensor_tensor(
                out=q_stack[h % n_q][rows_m, :], in0=small[rows_m, :], scalar=lo_sign[rows_m, :],
                in1=misc.t[rows_m, :], op0=ALU.mult, op1=ALU.add), hi, consts,
                k_used.get((h - n_q + 1) * NKC - 1))

        def score_step(n, j2):
            h = n // NKC
            banks = score[j2]
            b = (2 * n + j2) % n_p
            for j in range(2):
                kt = 2 * j2 + j
                after = (m_ready[h], k_loaded[n], banks[0].free, ring_init)
                if masks is not None:
                    self.pe(lambda e, j=j, kt=kt: e.matmul(
                        banks[j].t[:], self.ident_big[:], masks[1][:, n % NKC * (KC // P) + kt, :], start=True,
                        stop=False), *after)
                tok = self.pe(lambda e, j=j, kt=kt: e.matmul(
                    banks[j].t[:], k_ring[:, n % KRING, kt * P:(kt + 1) * P], q_stack[h % n_q][:],
                    start=masks is None, stop=True), *after, sig=j == 1)
            k_used[n] = tok
            banks[0].free = exp_done[2 * n + j2] = self.act(lambda e: e.activation(
                prob[b][:], self.psum[:, 2 * j2:2 * j2 + 2, :], ACT.Exp, scale=scale), tok, *prob_free[b])

        def value_step(n):
            h, c = divmod(n, NKC)
            for kt in range(KC // P):
                j2, j = divmod(kt, 2)
                b = (2 * n + j2) % n_p
                k = c * (KC // P) + kt
                tok = self.pe(lambda e, j=j, k=k, b=b, g=kt * DH: e.matmul(
                    vbank.t[g:g + DH, :], v_buf[h % 2][:, k * DH:(k + 1) * DH], prob[b][:, j, :],
                    start=c == 0, stop=c == NKC - 1, skip_group_check=True),
                    exp_done[2 * n + j2], v_ready[h], vbank.free, sig=j == 1)
                if j == 1:
                    prob_free[b] = (tok, *summed[2 * n + j2])
            v_used[h] = tok

        summed_chunks = set()
        summed = {}

        def add_den(name, n, j2, tiles, slots, start):
            p, d = prob[(2 * n + j2) % n_p][:, tiles, :], den_part[name][:, slots, :]
            if start == "one":
                fn = lambda e: e.tensor_scalar(d, p, 1.0, None, ALU.mult)
            else:
                q = prob[(2 * n - 2 + j2) % n_p][:, tiles, :] if start == "two" else d
                fn = lambda e: e.tensor_tensor(d, q, p, ALU.add)
            den_added[name] = (self.pool if name == "pool" else self.dve)(
                fn, exp_done[2 * n + j2], den_added[name], last["den"])
            return den_added[name]

        def den_step(n):
            summed_chunks.add(n)
            c = n % NKC
            both = slice(0, 2)
            if masks is not None:
                for j2, name in enumerate(("pool", "dve")):
                    summed[2 * n + j2] = (add_den(name, n, j2, both, both, "one" if c == 0 else None),)
            elif c == 0:
                summed[2 * n] = summed[2 * n + 1] = ()
            elif c == 1:
                for j2, name in enumerate(("pool", "dve")):
                    summed[2 * n + j2] = (add_den(name, n, j2, both, both, "two"),)
                    prob_free[(2 * n - 2 + j2) % n_p] += summed[2 * n + j2]
            else:
                summed[2 * n] = (add_den("pool", n, 0, both, both, None),)
                if n % DEN_TURNS == 0:
                    summed[2 * n + 1] = (add_den("dve", n, 1, both, both, None),)
                else:
                    summed[2 * n + 1] = (add_den("pool", n, 1, slice(0, 1), slice(0, 1), None),
                                         add_den("dve", n, 1, slice(1, 2), slice(1, 2), None))

        def take_values(h):
            vbank.free = self.act(lambda e: e.activation(o_sb[:], vbank.t[:], ACT.Copy), v_used[h], last["o_sb"])
            a, d = den_part["pool"], den_part["dve"]
            last["den"] = self.pool(lambda e: e.tensor_tensor(d[:], d[:], a[:], ALU.add), den_added["dve"])

        def head_out(h):
            g = slice(DH * (h % 4), DH * (h % 4) + DH)
            self.pe(lambda e: e.matmul(misc.t[0:DH, :], comb, o_sb[:], start=True, stop=True),
                    vbank.free, misc.free)
            tok = self.gather(misc.t[DH:2 * DH, :], [(self.ones[:, 0:DH], den_part["dve"][:, j, :])
                                                     for j in range(2)], last["den"])
            last["o_sb"] = last["den"] = tok
            out = attT[:, h // 4, :]
            self.act(lambda e: e.activation(out[g, :], misc.t[0:DH, :], ACT.Copy), tok)
            misc.free = t = self.act(lambda e: e.activation(den4[g, :], misc.t[DH:2 * DH, :], ACT.Copy), tok,
                                     last["den4"])
            if h % 4 == 3:
                rec = self.dve(lambda e: e.reciprocal(den4[:], den4[:]), t)
                last["den4"] = self.dve(lambda e: e.tensor_tensor(out, out, den4[:], ALU.mult), rec)

        mask_ready = {}
        if masks is not None:
            s_mq = [self.sem("s_mask_q") for _ in range(n_p)]
            mask_rows = self.i["mask"].rearrange("(i p) k -> p i k", p=P)

        def mask_step(c):
            for j in range(2):
                b = (2 * c + j) % n_p
                two = slice(2 * j, 2 * j + 2)
                raw = prob[b][:].bitcast(I32)
                ld = self.load(raw, mask_rows[:, two, c * KC:(c + 1) * KC], s_mq[b], *prob_free[b], eng="act")
                mask_ready[c] = self.dve(lambda e, raw=raw, two=two: e.tensor_scalar(
                    masks[0][:, two, c * KC:(c + 1) * KC], raw, 0, NEG_BIG, ALU.is_equal, ALU.mult), ld)
                prob_free[b] = (mask_ready[c],)

        for n in range(KRING):
            load_k(n)
        load_v(0)
        query(0)
        query(1)
        for n in range(NKC + LEAD):
            if masks is not None and n < NKC:
                mask_step(n)
            if n == NKC:
                max_rows(0, top_of_rows(0))
            for i in range(TT):
                max_step(n, i)
        for n in range(H * NKC):
            h, c = divmod(n, NKC)
            ahead = n + NKC + LEAD
            t_top = top_of_rows(h + 1) if c == NKC - LEAD and h + 1 < H else None
            max_step(ahead, 0)
            if masks is not None:
                max_step(ahead, 1)
            score_step(n, 0)
            if t_top is not None:
                max_rows(h + 1, t_top)
            if masks is None:
                max_step(ahead, 1)
            score_step(n, 1)
            load_k(n + KRING)
            if c == 1 and h > 0:
                head_out(h - 1)
            max_step(ahead, 2)
            if masks is not None:
                max_step(ahead, 3)
            if n > 0 and n - 1 not in summed_chunks:
                den_step(n - 1)
            if n > 0:
                value_step(n - 1)
            if c == 0 and h > 0:
                take_values(h - 1)
            if masks is None:
                max_step(ahead, 3)
            elif c > 0:
                den_step(n)
            if c == 1 and h == H - 1:
                w_loaded = self.load(v_first[:], w_out, self.sem("s_wo"), v_used[H - 2])
                bias_loaded = self.load(bias_row, bias, self.sem("s_bo"))
            elif c == 1:
                load_v(h + 1)
            if c == NKC // 2:
                query(h + 2)
        if masks is None:
            den_step(H * NKC - 1)
        value_step(H * NKC - 1)
        take_values(H - 1)

        x_loaded = self.load(self.x[:], x_rows, self.sem("s_x_back"), v_used[H - 1])
        done_banks = (exp_done[2 * H * NKC - 1], exp_done[2 * H * NKC - 2])
        for i in range(TT):
            cols = slice(i * P, (i + 1) * P)
            self.gather(self.banks[i].t[:], [(attT[:, k, cols], v_first[:, k, :]) for k in range(DT - 1)],
                        w_loaded, last["den4"], *done_banks, sig=False, stop=False)
        head_out(H - 1)
        for i in range(TT):
            cols = slice(i * P, (i + 1) * P)
            tok = self.gather(self.banks[i].t[:], [(self.ones[0:1, :], bias_row),
                                                   (attT[:, DT - 1, cols], v_first[:, DT - 1, :])],
                              bias_loaded, last["den4"], start=False)
            self.banks[i].free = self.dve(lambda e, i=i: e.tensor_tensor(
                self.x[:, i, :], self.x[:, i, :], self.banks[i].t[:], ALU.add), tok, x_loaded)
        maxbank[0].free = maxbank[1].free = vbank.free = None

    def l0_cross(self):
        x_rows = self.i["x"].rearrange("o (i p) d -> p (o i) d", p=P)
        with ExitStack() as outer:
            attT = self.sbuf(outer, "attT", [P, DT, T], F32)
            v_wo = self.sbuf(outer, "v_then_wo", [P, DT, D], F32)
            with ExitStack() as ctx:
                mask_k = self.sbuf(ctx, "mask_k", [P, KT, T], F8)
                m4 = self.sbuf(ctx, "m4", [P, QROWS], F32)
                comb = self.sbuf(ctx, "comb", [P, DH], F32)
                wq = self.sbuf(ctx, "wq", [DH, DH], F32)
                wk = self.sbuf(ctx, "wk", [DH, DH], F32)
                s = self.sem("s_l0w")

                def normalize(tmp):
                    self.load(wq[:], self.i["L0_xattn_Wq"], s)
                    self.load(wk[:], self.i["L0_xattn_Wk"], s)
                    for g in range(4):
                        ready["weights"] = self.load(comb[g * DH:(g + 1) * DH, :], self.i["L0_xattn_WvT"], s)
                    ready["xn"] = self.layernorm(tmp, attT, self.x)

                def queries(tmp):
                    bank = self.banks[7]
                    for g in range(4):
                        for r in range(3):
                            tok = self.pe(lambda e, g=g, r=r: e.matmul(
                                bank.t[DH * g:DH * (g + 1), DH * r:DH * (r + 1)], wq[:], wk[:], start=True,
                                stop=True), ready["weights"], bank.free, sig=True)
                    bank.free = self.dve(lambda e: e.tensor_copy(m4[:], bank.t[:, 0:QROWS]), tok)
                    self.transpose_all(self.xnT, attT, ready["xn"])

                ready = {}
                self.prepare_context(mask_k, v_wo, (normalize, queries))
                mask_q = self.sbuf(ctx, "mask_q", [P, TT, S2], BF16)

                def emit_query(h, out, *after):
                    rows = slice(DH * (h % 4), DH * (h % 4) + DH)
                    return self.gather(out, [(m4[rows, :], self.xnT[rows, h // 4, :])], *after)

                self.cross_attention(ctx, self.k0, self.i["ctx_heads"], v_wo, self.i["L0_xattn_WoT"].rearrange(
                    "(k p) n -> p k n", p=P), self.i["L0_xattn_bo"].rearrange("(o n) -> o n", o=1), x_rows,
                    emit_query, comb[:], D ** -0.5, (mask_q, mask_k), attT)
                self.q.emit()

    def l1_cross(self):
        if self.k1 is None:
            self.prepare_context()
        x_rows = self.nc.dram_tensor("x_kept", [P, TT, D], F32, kind="Internal").ap()
        with ExitStack() as outer:
            attT = self.sbuf(outer, "attT", [P, DT, T], F32)
            v_wo = self.sbuf(outer, "v_then_wo", [P, DT, D], F32)
            with ExitStack() as ctx:
                wq = self.sbuf(ctx, "wq3", [P, DT, H * QROWS], F32)
                comb = self.sbuf(ctx, "comb", [P, DH], F32)
                with ExitStack() as tmp:
                    wq_loaded = self.load(wq[:], self.i["L1_xattn_WqT3"].rearrange("(k p) n -> p k n", p=P),
                                          self.sem("s_wq3"))
                    self.q.wait("sp", self.store(x_rows, self.x[:], self.sem("s_x_kept")))
                    for g in range(4):
                        rows = slice(g * DH, (g + 1) * DH)
                        self.pool(lambda e, rows=rows: e.tensor_copy(comb[rows, :], self.ident[rows, rows]))
                    self.normalized_T(tmp)
                    self.q.emit()

                def emit_query(h, out, *after):
                    cols = slice(h * QROWS, (h + 1) * QROWS)
                    return self.gather(out, [(wq[:, k, cols], self.xnT[:, k, :]) for k in range(DT)], *after,
                                       wq_loaded)

                self.cross_attention(ctx, self.k1, self.v1, v_wo, self.i["L1_xattn_WoT"].rearrange(
                    "(k p) n -> p k n", p=P), self.i["L1_xattn_bo"].rearrange("(o n) -> o n", o=1), x_rows,
                    emit_query, comb[:], DH ** -0.5, None, attT)
                self.q.emit()

    def l0_scan(self):
        with ExitStack() as outer:
            u = self.sbuf(outer, "u", [P, GT, T], F32)
            zs = self.sbuf(outer, "z_silu", [P, GT, T], F32)
            with ExitStack() as ctx:
                w = self.sbuf(ctx, "in_proj", [P, DT, 2 * DIN], F32)
                w_part = [self.sbuf(ctx, "in_proj_" + n, [P, DT, 2 * DIN], F32R) for n in ("hi", "lo")]
                x_part = [self.sbuf(ctx, "x_" + n, [P, DT, T], F32R) for n in ("hi", "lo")]
                xn = self.sbuf(ctx, "xn", [P, TT, D], F32)
                xm = self.sbuf(ctx, "xm", [P, TT, D], F32)
                col = self.sbuf(ctx, "ln_gb", [P, 2, DT], F32)
                cw = self.sbuf(ctx, "conv_w", [P, GT, 4], F32)
                cb = self.sbuf(ctx, "conv_b", [P, GT], F32)
                PAD = 3
                up = [self.sbuf(ctx, "u_pad", [P, PAD + T], F32) for _ in range(3)]
                s_c = self.sem("s_cols")
                w_loaded = [self.load(w[:, k, :], self.i["L0_attn_in_proj_w"][k * P:(k + 1) * P, :],
                                      self.sem("s_inw")) for k in range(DT)]
                self.load(col[:, 0, :], self.i["L0_attn_ln_gC"], s_c)
                self.load(col[:, 1, :], self.i["L0_attn_ln_bC"], s_c)
                self.load(cw[:], self.i["L0_attn_conv_w"].rearrange("(k p) n -> p k n", p=P), s_c)
                ld_c = self.load(cb[:], self.i["L0_attn_conv_bC"], s_c)
                done = self.layernorm(ctx, xn, self.x)
                w_ready = []
                for k in range(DT):
                    hi = self.act(lambda e, k=k: e.activation(w_part[0][:, k, :], w[:, k, :], ACT.Copy),
                                  w_loaded[k])
                    if k < DT - 1:
                        w_ready.append(self.pool(lambda e, k=k: e.tensor_tensor(
                            w_part[1][:, k, :], w[:, k, :], w_part[0][:, k, :].bitcast(F32), ALU.subtract), hi))
                done = self.layernorm(ctx, xm, xn, done)
                ready = self.transpose_all(self.xnT, xm, done, ld_c, gain=(col[:, 0, :], col[:, 1, :]))
                x_ready = [self.split(x_part[0][:, k, :], x_part[1][:, k, :], self.xnT[:, k, :], ready,
                                      hi_on="act")[1] for k in range(DT)]
                k = DT - 1
                w_ready.append(self.dve(lambda e: e.tensor_tensor(
                    w_part[1][:, k, :], w[:, k, :], w_part[0][:, k, :].bitcast(F32), ALU.subtract), hi))
                for i in range(TT):
                    self.dve(lambda e, i=i: e.tensor_tensor(self.x[:, i, :], self.x[:, i, :], xn[:, i, :],
                                                            ALU.add))
                up_free = [None] * 3
                pads = [self.pool(lambda e, b=b: e.memset(up[b][:, 0:PAD], 0.0)) for b in range(3)]
                for n in range(2 * GT):
                    m = n // 2 + GT * (n % 2)
                    bank = self.banks[2 + n % 4]
                    for k in range(DT):
                        tok = self.gather(bank.t[:], [(w_part[a][:, k, m * P:(m + 1) * P], x_part[c][:, k, :])
                                                      for a, c in ((0, 0), (0, 1), (1, 0))],
                                          x_ready[k], w_ready[k], bank.free if k == 0 else None,
                                          sig=k == DT - 1, start=k == 0, stop=k == DT - 1)
                    if m >= GT:
                        bank.free = self.act(lambda e, b=bank, m=m: e.activation(zs[:, m - GT, :], b.t[:],
                                                                                 ACT.Silu), tok)
                        continue
                    b = m % 3
                    bank.free = c = self.act(lambda e, k=bank, b=b: e.activation(up[b][:, PAD:], k.t[:], ACT.Copy),
                                             tok, up_free[b])
                    for j in range(4):
                        if j == 0:
                            c = self.dve(lambda e, b=b, m=m: e.tensor_scalar(
                                u[:, m, :], up[b][:, 0:T], cw[:, m, 0:1], None, ALU.mult), c, pads[b], ld_c)
                        else:
                            c = self.dve(lambda e, b=b, m=m, j=j: e.scalar_tensor_tensor(
                                out=u[:, m, :], in0=up[b][:, j:j + T], scalar=cw[:, m, j:j + 1],
                                in1=u[:, m, :], op0=ALU.mult, op1=ALU.add), c)
                    up_free[b] = c
                    self.act(lambda e, m=m: e.activation(u[:, m, :], u[:, m, :], ACT.Silu, bias=cb[:, m:m + 1]), c)
                self.q.emit()
            NH = 4
            with ExitStack() as ctx:
                delta = self.sbuf(ctx, "delta", [P, GT, T], F32)
                du = self.sbuf(ctx, "delta_u", [P, GT, T], F32)
                bc = [self.sbuf(ctx, f"{n}_all", [P, NST, T], F32) for n in "BC"]
                xp = self.sbuf(ctx, "x_proj", [P, GT, DTR + 2 * NST], F32)
                dtb = self.sbuf(ctx, "dt_bias", [P, GT], F32)
                dcol = self.sbuf(ctx, "D_col", [P, GT], F32)
                a = self.sbuf(ctx, "A", [P, GT, NST], F32)
                with ExitStack() as tmp:
                    dtw = self.sbuf(tmp, "dt_proj", [DTR, DIN], F32)
                    dbc = self.sbuf(tmp, "dbc", [DTR + 2 * NST, T], F32)
                    sel = self.sbuf(tmp, "row_select", [DTR + 2 * NST, 2 * NST, P], F32R)
                    dbc_part = [self.sbuf(tmp, f"dbc_{n}", [DTR + 2 * NST, T], F32R) for n in ("hi", "lo")]
                    mag = self.sbuf(tmp, "minus_abs", [P, GT, T], F32)
                    s = self.sem("s_scanw")
                    self.load(xp[:], self.i["L0_attn_x_proj_w"].rearrange("(k p) n -> p k n", p=P), s)
                    self.load(dtw[:], self.i["L0_attn_dt_proj_w"], s)
                    self.load(dtb[:], self.i["L0_attn_dt_proj_bC"], s)
                    self.load(dcol[:], self.i["L0_attn_DC"], s)
                    ld = self.load(a[:], self.i["L0_attn_A_log"].rearrange("(k p) n -> p k n", p=P), s)
                    ea = self.act(lambda e: e.activation(a[:], a[:], ACT.Exp), ld)
                    self.dve(lambda e: e.tensor_scalar(a[:], a[:], -1.0, None, ALU.mult), ea)
                    rows = DTR + 2 * NST
                    t_sel = self.dve(lambda e: e.tensor_copy(
                        sel[:], self.ident[0:rows, DTR:rows].unsqueeze(2).to_broadcast([rows, 2 * NST, P])))
                    bank = self.banks[0]
                    tok = self.gather(bank.t[0:rows, :], [(xp[:, m, :], u[:, m, :]) for m in range(GT)],
                                      ld, bank.free)
                    t_dbc = bank.free = self.dve(lambda e, b=bank: e.tensor_copy(dbc[:], b.t[0:rows, :]), tok)
                    _, t_parts = self.split(dbc_part[0][:], dbc_part[1][:], dbc[:], t_dbc)
                    for m in range(GT):
                        bank = self.banks[1 + m % 2]
                        tok = self.gather(bank.t[:], [(dtw[:, m * P:(m + 1) * P], dbc[0:DTR, :])], t_dbc,
                                          bank.free)
                        bank.free = pre = self.dve(lambda e, b=bank, m=m: e.tensor_scalar(
                            delta[:, m, :], b.t[:], dtb[:, m:m + 1], None, ALU.add), tok)
                    ab = self.act(lambda e: e.activation(mag[:], delta[:], ACT.Abs), pre)
                    ex = self.act(lambda e: e.activation(mag[:], mag[:], ACT.Exp, scale=-1.0), ab)
                    ln = self.act(lambda e: e.activation(mag[:], mag[:], ACT.Ln, bias=1.0), ex)

                    def broadcast(n):
                        bank = self.banks[3 + n % 5]
                        tok = self.gather(bank.t[:], [(sel[:, n, :], dbc_part[0][:]), (sel[:, n, :], dbc_part[1][:])],
                                          t_sel, t_parts, bank.free)
                        dst = bc[n // NST][:, n % NST, :]
                        if n < NST:
                            bank.free = self.dve(lambda e: e.tensor_copy(dst, bank.t[:]), tok)
                        else:
                            bank.free = self.act(lambda e: e.activation(dst, bank.t[:], ACT.Copy), tok)

                    for n in range(2 * NST):
                        broadcast(n)
                    for m in range(GT):
                        d = self.dve(lambda e, m=m: e.scalar_tensor_tensor(
                            out=delta[:, m, :], in0=delta[:, m, :], scalar=0.0, in1=mag[:, m, :], op0=ALU.max,
                            op1=ALU.add), ln)
                        self.dve(lambda e, m=m: e.tensor_tensor(du[:, m, :], delta[:, m, :], u[:, m, :],
                                                                ALU.mult), d)
                    self.q.emit()
                with ExitStack() as tmp:
                    out_w = self.i["L0_attn_out_proj_w"].rearrange("(k p) n -> p k n", p=P)
                    first_half = self.load(self.xnT[:], out_w[:, 0:DT, :], self.sem("s_outw_half"))
                    n_da, n_db = 3, 4
                    da = [self.sbuf(tmp, "dA", [P, NH, T], F32) for _ in range(n_da)]
                    db = [self.sbuf(tmp, "dB_u", [P, NH, T], F32) for _ in range(n_db)]
                    da_free, db_free = [None] * n_da, [None] * n_db
                    summed = {}

                    def gate_out(m):
                        ybank = self.banks[m % 2]
                        y = ybank.free = self.dve(lambda e: e.scalar_tensor_tensor(
                            out=u[:, m, :], in0=u[:, m, :], scalar=dcol[:, m:m + 1], in1=ybank.t[:],
                            op0=ALU.mult, op1=ALU.add), summed[m])
                        self.dve(lambda e: e.tensor_tensor(zs[:, m, :], zs[:, m, :], u[:, m, :], ALU.mult), y)

                    def scan_step(m, g):
                        step = m * (NST // NH) + g
                        a_t, b_t = da[step % n_da], db[step % n_db]
                        ybank = self.banks[m % 2]
                        states = slice(g * NH, (g + 1) * NH)
                        for j in range(NH):
                            n = g * NH + j
                            t_a = self.act(lambda e, j=j, n=n: e.activation(
                                a_t[:, j, :], delta[:, m, :], ACT.Exp, scale=a[:, m, n:n + 1]),
                                da_free[step % n_da])
                        t_a = self.dve(lambda e: e.memset(a_t[:, :, 0:1], 0.0), t_a)
                        t_b = self.pool(lambda e: e.tensor_tensor(
                            b_t[:], du[:, m, :].unsqueeze(1).to_broadcast([P, NH, T]), bc[0][:, states, :],
                            ALU.mult), db_free[step % n_db])
                        rows = "p n t -> p (n t)"
                        t_h = da_free[step % n_da] = self.dve(lambda e: e.tensor_tensor_scan(
                            out=b_t[:].rearrange(rows), data0=a_t[:].rearrange(rows),
                            data1=b_t[:].rearrange(rows), initial=0.0, op0=ALU.mult, op1=ALU.add), t_a, t_b)
                        t_c = self.dve(lambda e: e.tensor_tensor(b_t[:], b_t[:], bc[1][:, states, :], ALU.mult),
                                       t_h)
                        for j in range(NH):
                            first, last = g == 0 and j == 0, g == NST // NH - 1 and j == NH - 1
                            tok = self.pe(lambda e, j=j, f=first, z=last: e.matmul(
                                ybank.t[:], self.ident[:], b_t[:, j, :], start=f, stop=z), t_c,
                                ybank.free if first else None, sig=j == NH - 1)
                        db_free[step % n_db] = summed[m] = tok

                    for m in range(GT):
                        for g in range(NST // NH):
                            scan_step(m, g)
                            if g == 1 and m > 0:
                                gate_out(m - 1)
                    gate_out(GT - 1)
                    self.q.emit()
            with ExitStack() as ctx:
                w = self.sbuf(ctx, "out_proj", [P, GT - DT, D], F32)
                ld = self.load(w[:], out_w[:, DT:, :], self.sem("s_outw"))
                self.project_residual(zs, [self.xnT[:, k, :] for k in range(DT)] +
                                      [w[:, k, :] for k in range(GT - DT)], None, GT, ld, first_half)
                self.q.emit()

    def gate(self, ctx, weights, w_gate, bias_row, softmax, ready):
        s = self.sbuf(ctx, "scores", [P, TT, E], F32)
        before = self.sbuf(ctx, "before", [P, E, E], F32)
        beats = self.sbuf(ctx, "beats", [P, E, E], F32)
        ties = self.sbuf(ctx, "ties", [P, E, E], F32)
        rank = self.sbuf(ctx, "rank", [P, E], F32)
        tot = self.sbuf(ctx, "score_sum", [P, TT], F32)
        one = self.pool(lambda e: e.memset(before[:], 1.0))
        tri = self.pool(lambda e: e.affine_select(out=before[:], in_=before[:], compare_op=ALU.is_gt, fill=0.0,
                                                  base=0, pattern=[[1, E], [-1, E]], channel_multiplier=0), one)
        bank = self.banks[7]
        for i in range(TT):
            terms = [(self.xnT[:, k, i * P:(i + 1) * P], w_gate[:, k, :]) for k in range(DT)]
            if bias_row is not None:
                terms.append((self.ones[0:1, :], bias_row))
            tok = self.gather(bank.t[:, i * E:(i + 1) * E], terms, ready, bank.free)
        logits = bank.t[:, 0:TT * E].rearrange("p (i e) -> p i e", e=E)
        if softmax:
            t = self.dve(lambda e: e.tensor_reduce(tot[:], logits, AXIS_X, ALU.max), tok)
            t = self.dve(lambda e: e.tensor_tensor(s[:], logits, tot[:].unsqueeze(2).to_broadcast([P, TT, E]),
                                                   ALU.subtract), t)
            bank.free = t
            t = self.act(lambda e: e.activation(s[:], s[:], ACT.Exp), t)
            t = self.dve(lambda e: e.tensor_reduce(tot[:], s[:], AXIS_X, ALU.add), t)
            t = self.dve(lambda e: e.reciprocal(tot[:], tot[:]), t)
            t = self.dve(lambda e: e.tensor_tensor(s[:], s[:], tot[:].unsqueeze(2).to_broadcast([P, TT, E]),
                                                   ALU.mult), t)
        else:
            t = bank.free = self.act(lambda e: e.activation(s[:], logits, ACT.Sigmoid), tok)
        yield t
        for i in range(TT):
            mine = s[:, i, :].unsqueeze(2).to_broadcast([P, E, E])
            other = s[:, i, :].unsqueeze(1).to_broadcast([P, E, E])
            t = self.dve(lambda e, a=other, b=mine: e.tensor_tensor(beats[:], a, b, ALU.is_gt), t)
            t = self.dve(lambda e, a=other, b=mine: e.tensor_tensor(ties[:], a, b, ALU.is_equal), t)
            t = self.dve(lambda e: e.tensor_tensor(ties[:], ties[:], before[:], ALU.mult), t, tri)
            t = self.dve(lambda e: e.tensor_tensor(beats[:], beats[:], ties[:], ALU.add), t)
            t = self.dve(lambda e: e.tensor_reduce(rank[:], beats[:], AXIS_X, ALU.add), t)
            t = self.dve(lambda e: e.tensor_scalar(rank[:], rank[:], 1.5, None, ALU.is_lt), t)
            t = self.dve(lambda e, i=i: e.tensor_tensor(weights[:, i, 0:E], s[:, i, :], rank[:], ALU.mult), t)
            t = self.dve(lambda e, i=i: e.tensor_reduce(tot[:, i:i + 1], weights[:, i, 0:E], AXIS_X, ALU.add), t)
            if not softmax:
                t = self.dve(lambda e, i=i: e.tensor_scalar(tot[:, i:i + 1], tot[:, i:i + 1], 1e-6, None,
                                                            ALU.add), t)
            t = self.dve(lambda e, i=i: e.reciprocal(tot[:, i:i + 1], tot[:, i:i + 1]), t)
            t = self.dve(lambda e, i=i: e.tensor_scalar(weights[:, i, 0:E], weights[:, i, 0:E], tot[:, i:i + 1],
                                                        None, ALU.mult), t)
            yield t

    def experts(self, ctx, up_w, down_w, up_b, down_b, weights, acc, func, normalize, gating):
        n_exp = down_b.shape[0]
        n_load = n_exp * NU
        per_exp = NU * FU
        x_part = [self.sbuf(ctx, f"x_{n}", [P, DT, T], F32R) for n in ("hi", "lo")]
        raw = [[self.sbuf(ctx, f"{n}_raw", [P, FU, D], F32) for n in ("up", "down")] for _ in range(2)]
        part = [[[self.sbuf(ctx, f"{n}_{k}", [P, FU, D], F32R) for k in ("hi", "lo")] for n in ("up", "down")]
                for _ in range(2)]
        hidden = [self.sbuf(ctx, "hidden", [P, T], F32) for _ in range(3)]
        h_part = [[self.sbuf(ctx, f"hidden_{k}", [P, T], F32R) for k in ("hi", "lo")] for _ in range(3)]
        wT = self.sbuf(ctx, "weights_T", [n_exp, TT, P], F32)
        s_raw = [[self.sem("s_up"), self.sem("s_down")] for _ in range(2)]
        raw_free = [[None, None], [None, None]]
        part_free = [[None, None], [None, None]]
        part_ready = {}
        loaded = {}

        def load(u):
            for n, src in enumerate((up_w, down_w)):
                loaded[u, n] = self.load(raw[u % 2][n][:], src(*divmod(u, NU)), s_raw[u % 2][n],
                                         raw_free[u % 2][n])

        def split(u, n, hi_on="dve"):
            b = u % 2
            _, raw_free[b][n] = self.split(part[b][n][0][:], part[b][n][1][:], raw[b][n][:], loaded[u, n],
                                           part_free[b][n], hi_on=hi_on)
            part_ready[u, n] = raw_free[b][n]

        hid_ready, hid_free = {}, [None] * 3

        def up(s):
            u, j = divmod(s, FU)
            b, r = u % 2, s % 3
            bank = self.banks[4 + s % 3]
            tok = self.gather(bank.t[:], [(part[b][0][a][:, j, k * P:(k + 1) * P], x_part[c][:, k, :])
                                          for k in range(DT) for a, c in ((0, 0), (0, 1), (1, 0))],
                              part_ready[u, 0], x_ready, bank.free)
            if j == FU - 1:
                part_free[b][0] = tok
            bank.free = t = self.act(lambda e: e.activation(hidden[r][:], bank.t[:], func, bias=up_b[:, s:s + 1]),
                                     tok, hid_free[r])
            t_hi = self.act(lambda e: e.activation(h_part[r][0][:], hidden[r][:], ACT.Copy), t)
            hid_ready[s] = self.dve(lambda e: e.tensor_tensor(h_part[r][1][:], hidden[r][:],
                                                              h_part[r][0][:].bitcast(F32), ALU.subtract), t_hi)

        def down(s):
            u, j = divmod(s, FU)
            b, r = u % 2, s % 3
            first, last = s % per_exp == 0, s % per_exp == per_exp - 1
            for i in range(TT):
                bank = self.banks[i]
                cols = slice(i * P, (i + 1) * P)
                tok = self.gather(bank.t[:], [(h_part[r][a][:, cols], part[b][1][c][:, j, :])
                                              for a, c in ((0, 0), (0, 1), (1, 0))],
                                  hid_ready[s], part_ready[u, 1], bank.free if first else None,
                                  sig=last or i == TT - 1, start=first, stop=last)
                if last:
                    ex = s // per_exp
                    bank.free = self.dve(lambda e, i=i, k=bank: e.scalar_tensor_tensor(
                        out=acc[:, i, :], in0=k.t[:], scalar=weights[:, i, ex:ex + 1], in1=acc[:, i, :],
                        op0=ALU.mult, op1=ALU.add), tok, bank.free)
            hid_free[r] = tok
            if j == FU - 1:
                part_free[b][1] = tok

        load(0)
        load(1)

        def first_splits():
            split(0, 0, hi_on="act")
            split(0, 1, hi_on="act")

        ready = normalize(first_splits)
        for k in range(DT):
            _, x_ready = self.split(x_part[0][:, k, :], x_part[1][:, k, :], self.xnT[:, k, :], ready, hi_on="act")

        def side_steps():
            for t in gating(ready):
                yield
            bank = self.banks[7]
            for i in range(TT):
                tok = self.pe(lambda e, i=i: e.transpose(bank.t[0:n_exp, i * P:(i + 1) * P], weights[:, i, :],
                                                         self.ident[:]), t, bank.free, sig=i == TT - 1)
            t = bank.free = self.dve(lambda e: e.tensor_copy(
                wT[:], bank.t[0:n_exp, :].rearrange("p (i q) -> p i q", q=P)), tok)
            for i in range(TT):
                yield
                tok = self.gather(bank.t[:], [(wT[:, i, :], down_b[:])], t, bank.free)
                bank.free = self.dve(lambda e, i=i: e.tensor_tensor(acc[:, i, :], acc[:, i, :], bank.t[:],
                                                                    ALU.add), tok)

        side = side_steps()
        for s in range(n_load * FU + 2):
            u, j = divmod(s, FU)
            if s < n_load * FU:
                up(s)
            if s > 0:
                next(side, None)
            if s >= 2:
                down(s - 2)
            if u + 1 < n_load and j in (1, 2):
                split(u + 1, j - 1)
                if j == 2 and u + 2 < n_load:
                    load(u + 2)
        return self.banks[TT - 1].free

    def l0_experts(self):
        n_exp = E + 1
        with ExitStack() as ctx:
            weights = self.sbuf(ctx, "weights", [P, TT, n_exp], F32)
            up_b = self.sbuf(ctx, "up_b", [P, n_exp * FF // P], F32)
            down_b = self.sbuf(ctx, "down_b", [n_exp, D], F32)
            gw = self.sbuf(ctx, "gate_w", [P, DT, E], F32)
            gb = self.sbuf(ctx, "gate_b", [1, E], F32)
            s = self.sem("s_moe0")
            nb = E * FF // P
            self.load(up_b[:, 0:nb], self.i["L0_ffn_buC"], s)
            self.load(up_b[:, nb:], self.i["L0_ffn_sbuC"], s)
            self.load(down_b[0:E, :], self.i["L0_ffn_bd"], s)
            self.load(down_b[E:, :], self.i["L0_ffn_sbd"].rearrange("(o n) -> o n", o=1), s)
            self.load(gw[:], self.i["L0_ffn_gate_wT"].rearrange("(k p) n -> p k n", p=P), s)
            ld = self.load(gb[:], self.i["L0_ffn_gate_bias"].rearrange("(o n) -> o n", o=1), s)
            self.dve(lambda e: e.memset(weights[:, :, E:], 0.1))
            self.q.wait("act", ld)

            def gating(ready):
                self.q.wait("pe", ld)
                return self.gate(ctx, weights, gw, gb[:], False, ready)

            def normalize(first_splits):
                xn = self.sbuf(ctx, "xn", [P, TT, D], F32)
                done = self.transpose_all(self.xnT, xn, self.layernorm(ctx, xn, self.x))
                first_splits()
                return done

            def up_w(e, u):
                return self.i["L0_ffn_Wu"][e, u] if e < E else self.i["L0_ffn_sWu"][u]

            def down_w(e, u):
                return self.i["L0_ffn_Wd"][e, u] if e < E else self.i["L0_ffn_sWd"][u]

            self.experts(ctx, up_w, down_w, up_b, down_b, weights, self.x, ACT.Gelu,
                         normalize, gating)
            self.q.emit()

    def l1_linear(self):
        with ExitStack() as ctx:
            w = {n: self.sbuf(ctx, f"w_{n}", [P, DT, c], F32)
                 for n, c in (("q", LH * P), ("k", LH * P), ("v", D), ("u", D), ("o", D))}
            tab = self.sbuf(ctx, "cos_sin", [P, LH, T], F32)
            qk = [self.sbuf(ctx, "qk_cat", [P, T], F32) for _ in range(4)]
            theta = self.sbuf(ctx, "theta", [P, LH], F32)
            shift = self.sbuf(ctx, "shift", [P, 1], F32)
            bqk = self.sbuf(ctx, "b_qk", [P, 2, LH], F32)
            bu = self.sbuf(ctx, "b_u", [P, DT], F32)
            bv = self.sbuf(ctx, "b_v", [1, D], F32)
            bo = self.sbuf(ctx, "b_o", [1, D], F32)
            slope = self.sbuf(ctx, "slope", [P, LH], F32)
            v = self.sbuf(ctx, "v", [P, TT, D], F32)
            uT = self.sbuf(ctx, "uT", [P, DT, T], F32)
            oT = self.sbuf(ctx, "oT", [P, DT, T], F32)
            tril = self.sbuf(ctx, "tril", [P, TT, T], F32)
            s_c = self.sem("s_linc")
            ld_w = {}
            self.load(theta[:], self.i["L1_attn_theta2"], s_c)
            self.load(bqk[:, 0, :], self.i["L1_attn_b_q2"], s_c)
            self.load(bqk[:, 1, :], self.i["L1_attn_b_k2"], s_c)
            self.load(bu[:], self.i["L1_attn_b_uC"], s_c)
            self.load(bv[:], self.i["L1_attn_b_v"], s_c)
            self.load(bo[:], self.i["L1_attn_out_b"].rearrange("(o n) -> o n", o=1), s_c)
            ld_c = self.load(slope[:], self.i["L1_attn_slope_rate"].rearrange("h a b -> (h a b)")
                             .partition_broadcast(P), s_c)
            for n, key in (("u", "w_uT"), ("v", "w_vT"), ("q", "w_qT2"), ("k", "w_kT2"), ("o", "out_wT")):
                ld_w[n] = self.load(w[n][:], self.i["L1_attn_" + key].rearrange("(k p) n -> p k n", p=P),
                                    self.sem("s_linw"))
            one = self.pool(lambda e: e.memset(tril[:], 1.0))
            for m in range(TT):
                t_tril = self.pool(lambda e, m=m: e.affine_select(
                    out=tril[:, m, :], in_=tril[:, m, :], compare_op=ALU.is_ge, fill=0.0, base=-m * P,
                    pattern=[[1, T]], channel_multiplier=-1), one)
            idx = self.sbuf(ctx, "idx", [P, T], F32)
            turns = self.sbuf(ctx, "turns", [P, T], F32)
            frac = self.sbuf(ctx, "turn_shift", [P, 1], F32)
            e_sb = [self.sbuf(ctx, "energy", [P, T], F32) for _ in range(3)]
            mh = [self.sbuf(ctx, "decay", [P, TT, T], F32) for _ in range(2)]
            t_idx = self.pool(lambda e: e.iota(idx[:], [[1, T]], base=0, channel_multiplier=0,
                                               allow_small_or_imprecise_dtypes=True))
            xn_ready, _ = self.normalized_T(ctx)
            for m in range(DT):
                bank = self.banks[m % 2]
                tok = self.gather(bank.t[:], [(w["u"][:, k, m * P:(m + 1) * P], self.xnT[:, k, :])
                                              for k in range(DT)], xn_ready, ld_w["u"], bank.free)
                bank.free = u_ready = self.act(lambda e, b=bank, m=m: e.activation(
                    uT[:, m, :], b.t[:], ACT.Identity, bias=bu[:, m:m + 1]), tok, ld_c)
            for i in range(TT):
                bank = self.banks[i % 2]
                tok = self.gather(bank.t[:], [(self.xnT[:, k, i * P:(i + 1) * P], w["v"][:, k, :])
                                              for k in range(DT)] + [(self.ones[0:1, :], bv[:])], ld_w["v"],
                                  bank.free)
                bank.free = v_ready = self.act(lambda e, b=bank, i=i: e.activation(v[:, i, :], b.t[:], ACT.Copy),
                                               tok)
            PI = 3.141592653589793
            MAGIC = 12582912.0
            C1 = 6.28125
            C2 = 0.0019350051879882812
            C3 = 2 * PI - C1 - C2
            z = self.pool(lambda e: e.memset(shift[0:LD, :], PI / 2))
            z = self.pool(lambda e: e.memset(shift[LD:, :], 0.0))
            z = self.dve(lambda e: e.tensor_scalar(frac[:], shift[:], 1 / (2 * PI), None, ALU.mult), z)
            for h in range(LH):
                ang = tab[:, h, :]
                t = self.dve(lambda e, h=h, ang=ang: e.tensor_scalar(ang, idx[:], theta[:, h:h + 1], None,
                                                                     ALU.mult), t_idx, ld_c)
                t = self.dve(lambda e, ang=ang: e.tensor_scalar(turns[:], ang, 1 / (2 * PI), frac[:], ALU.mult,
                                                                ALU.add), t, z)
                t = self.dve(lambda e: e.tensor_scalar(turns[:], turns[:], MAGIC, None, ALU.add), t)
                t = self.dve(lambda e: e.tensor_scalar(turns[:], turns[:], MAGIC, None, ALU.subtract), t)
                for c in (C1, C2, C3):
                    t = self.dve(lambda e, ang=ang, c=c: e.scalar_tensor_tensor(
                        out=ang, in0=turns[:], scalar=-c, in1=ang, op0=ALU.mult, op1=ALU.add), t)
                t = self.dve(lambda e, ang=ang: e.tensor_scalar(ang, ang, shift[:], PI, ALU.add, ALU.min), t)
                t = self.dve(lambda e, ang=ang: e.tensor_scalar(ang, ang, -PI, None, ALU.max), t)
                tab_ready = self.act(lambda e, ang=ang: e.activation(ang, ang, ACT.Sin), t)
            self.q.wait("pe", ld_w["q"], ld_w["k"])
            self.q.wait("dve", tab_ready, u_ready)
            self.q.wait("pe", v_ready)
            qk_free, e_free, mh_free = [None, None], [None] * 3, [None, None]
            qk_ready, mh_ready = {}, {}

            def project(h):
                for n, name in enumerate(("q", "k")):
                    bank = self.banks[n]
                    buf = qk[2 * (h % 2) + n]
                    tok = self.gather(bank.t[:], [(w[name][:, k, h * P:(h + 1) * P], self.xnT[:, k, :])
                                                  for k in range(DT)], bank.free)
                    bank.free = t = self.act(lambda e, b=bank, n=n, buf=buf: e.activation(
                        buf[:], b.t[:], ACT.Silu, bias=bqk[:, n, h:h + 1]), tok, qk_free[h % 2])
                    qk_ready[h] = self.dve(lambda e, buf=buf: e.tensor_tensor(buf[:], buf[:], tab[:, h, :],
                                                                              ALU.mult), t)
                mh_ready[h] = self.act(lambda e: e.activation(mh[h % 2][:], tril[:], ACT.Exp,
                                                              scale=slope[:, h:h + 1]), mh_free[h % 2])

            n_e = 0
            project(0)
            for h in range(LH):
                if h + 1 < LH:
                    project(h + 1)
                q_h, k_h = qk[2 * (h % 2)], qk[2 * (h % 2) + 1]
                rows = slice(LD * (h % 2), LD * (h % 2) + LD)
                obank = self.banks[6 + (h // 2) % 2]
                e_ready = []
                for m in range(TT):
                    bank = self.banks[2 + m]
                    tok = self.gather(bank.t[:], [(k_h[:, m * P:(m + 1) * P], q_h[:])], qk_ready[h], bank.free)
                    if m == TT - 1:
                        qk_free[h % 2] = tok
                    r = n_e % 3
                    n_e += 1
                    bank.free = mh_free[h % 2] = self.dve(lambda e, b=bank, r=r, m=m, h=h: e.tensor_tensor(
                        e_sb[r][:], b.t[:], mh[h % 2][:, m, :], ALU.mult), tok, mh_ready[h], e_free[r])
                    e_ready.append((r, bank.free))
                    if m > 0:
                        self.value_rows(obank, rows, v, h, m - 1, e_sb, e_ready, e_free)
                tok = self.value_rows(obank, rows, v, h, TT - 1, e_sb, e_ready, e_free)
                t = self.dve(lambda e, rows=rows, o=obank, h=h: e.tensor_copy(oT[rows, h // 2, :], o.t[rows, :]),
                             tok)
                obank.free = t
            bank = self.banks[0]
            sq = e_sb[0]
            for m in range(DT):
                t_sq = self.dve(lambda e, m=m: e.tensor_tensor(sq[:], oT[:, m, :], oT[:, m, :], ALU.mult), t,
                                e_free[0])
                tok = self.pe(lambda e, m=m: e.matmul(bank.t[:], self.ones[:], sq[:], start=m == 0,
                                                      stop=m == DT - 1), t_sq, bank.free, sig=True)
                e_free[0] = tok
            rs = e_sb[1]
            t = self.dve(lambda e: e.tensor_scalar(rs[:], bank.t[:], 1.0 / D, 1e-6, ALU.mult, ALU.add), tok)
            bank.free = t
            t = self.act(lambda e: e.activation(rs[:], rs[:], ACT.Sqrt), t)
            t_rs = self.dve(lambda e: e.reciprocal(rs[:], rs[:]), t)
            for m in range(DT):
                t = self.dve(lambda e, m=m: e.tensor_tensor(oT[:, m, :], oT[:, m, :], rs[:], ALU.mult), t_rs)
                t = self.dve(lambda e, m=m: e.tensor_tensor(oT[:, m, :], oT[:, m, :], uT[:, m, :], ALU.mult), t)
            self.q.wait("pe", ld_w["o"])
            self.project_residual(oT, [w["o"][:, k, :] for k in range(DT)], bo[:], DT, t, first_bank=2)
            self.q.emit()

    def value_rows(self, obank, rows, v, h, m, e_sb, e_ready, e_free):
        r, ready = e_ready[m]
        tok = self.pe(lambda e: e.matmul(obank.t[rows, :], v[:, m, h * LD:(h + 1) * LD], e_sb[r][:],
                                         start=m == 0, stop=m == TT - 1, skip_group_check=True),
                      ready, obank.free, sig=True)
        e_free[r] = tok
        return tok

    def l1_ffn(self):
        with ExitStack() as outer:
            hh = self.sbuf(outer, "h", [P, TT, D], F32)
            weights = self.sbuf(outer, "weights", [P, TT, E], F32)
            up_b = self.sbuf(outer, "up_b", [P, E * FF // P], F32)
            down_b = self.sbuf(outer, "down_b", [E, D], F32)
            gains = [self.sbuf(outer, n, [P, D], F32) for n in ("g1", "b1", "g2", "b2")]
            wo = self.sbuf(outer, "w_o", [P, DT, D], F32)
            gw = self.sbuf(outer, "gate_w", [P, DT, E], F32)
            xn = self.sbuf(outer, "xn", [P, TT, D], F32)
            o = self.sbuf(outer, "o", [P, TT, D], F32)
            s_c = self.sem("s_ffnc")
            with ExitStack() as ctx:
                v = self.sbuf(ctx, "v", [P, TT, D], F32)
                stack = [self.sbuf(ctx, n, [QROWS, 4, DT, T], F32R) for n in ("q_stack", "k_stack")]
                causal = self.sbuf(ctx, "causal", [P, (TT - 1) * P + T], F32)
                tmp = ctx.enter_context(ExitStack())
                w = self.sbuf(tmp, "w_qkv", [P, DT, 3 * D], F32)
                qT = self.sbuf(tmp, "qT", [P, DT, T], F32)
                kT = self.sbuf(tmp, "kT", [P, DT, T], F32)
                part = [self.sbuf(tmp, n, [P, DT, T], F32R) for n in ("part_hi", "part_lo")]
                s_w = self.sem("s_ffnw")
                self.load(w[:], self.i["L1_ffn_w_qkv"].rearrange("(k p) n -> p k n", p=P), s_w)
                self.load(wo[:], self.i["L1_ffn_w_o"].rearrange("(k p) n -> p k n", p=P), s_w)
                self.load(gw[:], self.i["L1_ffn_wg"].rearrange("(k p) n -> p k n", p=P), s_w)
                self.load(up_b[:], self.i["L1_ffn_bb1C"], s_w)
                ld_w = self.load(down_b[:], self.i["L1_ffn_bb2"], s_w)
                for n, key in enumerate(("g1", "b1", "g2", "b2")):
                    ld_c = self.load(gains[n][:], self.i["L1_ffn_" + key].partition_broadcast(P), s_c)
                self.q.wait("sp", ld_c, ld_w)
                z = self.pool(lambda e: e.memset(causal[:], 0.0))
                t_causal = self.pool(lambda e: e.affine_select(
                    out=causal[:], in_=causal[:], compare_op=ALU.is_ge, fill=NEG_BIG, base=(TT - 1) * P,
                    pattern=[[-1, (TT - 1) * P + T]], channel_multiplier=1), z)
                done = self.layernorm(tmp, xn, self.x)
                ready = self.transpose_all(self.xnT, xn, done)
                s_stack = self.sem("s_stack")
                stacked = []
                for n, (dst, base) in enumerate(((qT, 0), (kT, D))):
                    for m in range(DT):
                        bank = self.banks[2 + m % 2]
                        tok = self.gather(bank.t[:], [(w[:, k, base + m * P:base + (m + 1) * P], self.xnT[:, k, :])
                                                      for k in range(DT)], ready, ld_w, bank.free)
                        bank.free = self.act(lambda e, b=bank, d=dst, m=m: e.activation(d[:, m, :], b.t[:],
                                                                                        ACT.Copy), tok)
                    t_part = self.split(part[0][:], part[1][:], dst[:], bank.free, stacked[-1] if stacked else None)
                    for r, lo in enumerate(((0, 1, 0), (0, 0, 1))[n]):
                        for g in range(4):
                            stacked.append(self.load(
                                stack[n][r * DH:(r + 1) * DH, g, :, :].bitcast(F32),
                                part[lo][g * DH:(g + 1) * DH, :, :].bitcast(F32), s_stack, t_part[1]))
                for i in range(TT):
                    bank = self.banks[2 + i % 2]
                    tok = self.gather(bank.t[:], [(self.xnT[:, k, i * P:(i + 1) * P], w[:, k, 2 * D:])
                                                  for k in range(DT)], bank.free)
                    bank.free = self.act(lambda e, b=bank, i=i: e.activation(v[:, i, :], b.t[:], ACT.Copy), tok)
                self.q.wait("sp", stacked[-1])
                self.q.emit()
                tmp.close()
                NG = 4
                NS, NB = 5, NG + 3
                s_sb = [self.sbuf(ctx, "s", [P, T], F32) for _ in range(NS)]
                pT = [self.sbuf(ctx, "probT", [P, TT, P], F32) for _ in range(NB)]
                top = self.sbuf(ctx, "top", [P, TT, H], F32)
                den = self.sbuf(ctx, "den", [P, TT, H], F32)
                s_free, pT_free = [None] * NS, [None] * NB
                prob_ready, pT_ready = {}, {}
                scale = DH ** -0.5
                todo = [(i, h) for i in range(TT) for h in range(H)]

                def scores(n):
                    i, h = todo[n]
                    b, width = n % NS, (i + 1) * P
                    s, t1 = s_sb[b][:, 0:width], top[:, i, h:h + 1]
                    d1 = den[:, i, h:h + 1]
                    bank = self.banks[n % 3]
                    tok = self.gather(bank.t[:, 0:width], [(stack[0][:, h % 4, h // 4, i * P:(i + 1) * P],
                                                            stack[1][:, h % 4, h // 4, 0:width])], bank.free)
                    off = (TT - 1 - i) * P
                    bank.free = t = self.dve(lambda e: e.tensor_tensor_reduce(
                        out=s, in0=bank.t[:, 0:width], in1=causal[:, off:off + width], scale=1.0,
                        scalar=-3.0e38, op0=ALU.add, op1=ALU.max, accum_out=t1), tok, s_free[b], t_causal)
                    t = self.dve(lambda e: e.tensor_scalar(t1, t1, -scale, None, ALU.mult), t)
                    exp_ready[n] = self.act(lambda e: e.activation(s, s, ACT.Exp, scale=scale, bias=t1,
                                                                   accum_out=d1), t)

                exp_ready = {}

                def divide(n):
                    i, h = todo[n]
                    s, d1 = s_sb[n % NS][:, 0:(i + 1) * P], den[:, i, h:h + 1]
                    t = self.dve(lambda e: e.reciprocal(d1, d1), exp_ready[n])
                    prob_ready[n] = self.dve(lambda e: e.tensor_scalar(s, s, d1, None, ALU.mult), t)

                def turn(n):
                    i, h = todo[n]
                    b = n % NB
                    bank = self.banks[3 + n % 3]
                    for k in range(i + 1):
                        tok = self.pe(lambda e, k=k: e.transpose(bank.t[:, k * P:(k + 1) * P],
                                                                 s_sb[n % NS][:, k * P:(k + 1) * P],
                                                                 self.ident[:]),
                                      prob_ready[n], bank.free, sig=k == i)
                    s_free[n % NS] = tok
                    dst, src = pT[b][:, 0:i + 1, :], bank.t[:, 0:(i + 1) * P].rearrange("p (k q) -> p k q", q=P)
                    if n % 4 == 0:
                        t = self.dve(lambda e: e.tensor_copy(dst, src), tok, pT_free[b])
                    else:
                        t = self.act(lambda e: e.activation(dst, src, ACT.Copy), tok, pT_free[b])
                    bank.free = pT_ready[n] = t

                def values(n):
                    i, h = todo[n]
                    bank = self.banks[6 + i % 2]
                    out = bank.t[:, (h // NG) * P:(h // NG + 1) * P]
                    for k in range(i + 1):
                        for g in range(NG):
                            cols = slice((h + g) * DH, (h + g + 1) * DH)
                            tok = self.pe(lambda e, k=k, g=g, cols=cols: e.matmul(
                                out[g * DH:(g + 1) * DH, :], v[:, k, cols], pT[(n + g) % NB][:, k, :],
                                start=k == 0, stop=k == i, skip_group_check=True),
                                pT_ready[n + g], bank.free, sig=g == NG - 1)
                    for g in range(NG):
                        pT_free[(n + g) % NB] = tok
                    if h + NG == H:
                        bank.free = self.act(lambda e: e.activation(
                            self.xnT[:, :, i * P:(i + 1) * P], bank.t[:].rearrange("p (c q) -> p c q", q=P),
                            ACT.Copy), tok)

                for n in range(len(todo) + 5):
                    if n < len(todo):
                        scores(n)
                    if 1 <= n <= len(todo):
                        divide(n - 1)
                    if 3 <= n <= len(todo) + 2:
                        turn(n - 3)
                    if n >= 5 and (n - 5) % NG == NG - 1:
                        values(n - 5 - (NG - 1))
                self.q.emit()
            with ExitStack() as ctx:
                def normalize(first_splits):
                    first_splits()
                    for i in range(TT):
                        bank = self.banks[2 + i]
                        tok = self.gather(bank.t[:], [(self.xnT[:, k, i * P:(i + 1) * P], wo[:, k, :])
                                                      for k in range(DT)], bank.free)
                        bank.free = t = self.dve(lambda e, b=bank, i=i: e.tensor_tensor(
                            o[:, i, :], xn[:, i, :], b.t[:], ALU.add), tok)
                    t = self.layernorm(ctx, hh, o, t, gain=gains[0], plus=lambda i: gains[1][:])
                    return self.transpose_all(self.xnT, hh, t[-1])

                def gating(ready):
                    for i, t in enumerate(self.gate(ctx, weights, gw, None, True, ready)):
                        if i < TT:
                            self.dve(lambda e, i=i: e.tensor_tensor(self.x[:, i, :], self.x[:, i, :],
                                                                    gains[3][:], ALU.add))
                        yield t

                self.experts(ctx, lambda e, u: self.i["L1_ffn_w1"][e, u], lambda e, u: self.i["L1_ffn_w2"][e, u],
                             up_b, down_b, weights, hh, ACT.Gelu_apprx_tanh, normalize, gating)
                self.q.emit()
            self.x_done = self.layernorm(outer, self.x, hh, gain=gains[2], plus=lambda i: self.x[:, i, :])


def perceiver_kernel(nc, ins, out, stages):
    with ExitStack() as ctx:
        k = Kernel(nc, ins, out, ctx)
        k.constants()
        k.q.emit()
        for stage in stages:
            stage(k)
        k.finish()


STAGES = (Kernel.l0_cross, Kernel.l0_scan, Kernel.l0_experts, Kernel.l1_cross,
          Kernel.l1_linear, Kernel.l1_ffn)


def _laid_out(inputs):
    import numpy as np
    a = {k: np.asarray(v) for k, v in inputs.items()}

    def columns(v):
        return v.reshape(-1, P).T

    def up(w):
        e = w.shape[0]
        w = w.reshape(e, DT, P, NU, FU, P)
        return w.transpose(0, 3, 2, 4, 1, 5).reshape(e, NU, P, FU, D)

    def down(w):
        e = w.shape[0]
        return w.reshape(e, NU, FU, P, D).transpose(0, 1, 3, 2, 4)

    ctx = a["ctx_1024"][0]
    mask = a["mask_Bx1xSxS2_ik1"][0, 0]
    d = {"x": a["x"], "ctxT": ctx.T, "mask": mask, "maskT": mask.T,
         "ctx_heads": ctx.reshape(KT, P, H, DH).transpose(2, 1, 0, 3).reshape(H, P, KT * DH)}
    for k in ("L0_xattn_Wq", "L0_xattn_Wk", "L0_xattn_bo", "L0_attn_in_proj_w", "L0_attn_conv_w",
              "L0_attn_x_proj_w", "L0_attn_dt_proj_w", "L0_attn_A_log", "L0_attn_out_proj_w", "L0_ffn_bd",
              "L0_ffn_sbd", "L0_ffn_gate_bias", "L1_xattn_bo", "L1_attn_slope_rate", "L1_attn_out_b",
              "L1_ffn_w_qkv", "L1_ffn_w_o", "L1_ffn_wg", "L1_ffn_bb2", "L1_ffn_g1", "L1_ffn_b1", "L1_ffn_g2",
              "L1_ffn_b2"):
        d[k] = a[k]
    for k in ("L0_xattn_Wv", "L0_xattn_Wo", "L1_xattn_Wk", "L1_xattn_Wv", "L1_xattn_Wo", "L0_ffn_gate_w",
              "L1_attn_out_w"):
        d[k + "T"] = a[k].T
    for k in ("L0_attn_ln_g", "L0_attn_ln_b", "L0_attn_conv_b", "L0_attn_dt_proj_b", "L0_attn_D"):
        d[k + "C"] = columns(a[k])
    d["L0_ffn_buC"] = columns(a["L0_ffn_bu"].reshape(-1))
    d["L0_ffn_sbuC"] = columns(a["L0_ffn_sbu"])
    d["L1_ffn_bb1C"] = columns(a["L1_ffn_bb1"].reshape(-1))
    d["L1_xattn_WqT3"] = np.tile(a["L1_xattn_Wq"].T.reshape(D, H, 1, DH), (1, 1, 3, 1)).reshape(D, H * QROWS)
    d["L0_ffn_Wu"] = up(a["L0_ffn_Wu"].transpose(0, 2, 1))
    d["L0_ffn_sWu"] = up(a["L0_ffn_sWu"].T[None])[0]
    d["L0_ffn_Wd"] = down(a["L0_ffn_Wd"].transpose(0, 2, 1))
    d["L0_ffn_sWd"] = down(a["L0_ffn_sWd"].T[None])[0]
    d["L1_ffn_w1"] = up(a["L1_ffn_w1"])
    d["L1_ffn_w2"] = down(a["L1_ffn_w2"])
    w = a["L1_attn_qkvu_w"].reshape(4, D, D)
    b = a["L1_attn_qkvu_b"].reshape(4, D)
    for n, k in ((0, "q"), (1, "k")):
        d[f"L1_attn_w_{k}T2"] = np.tile(w[n].T.reshape(D, LH, 1, LD), (1, 1, 2, 1)).reshape(D, LH * P)
        d[f"L1_attn_b_{k}2"] = np.tile(b[n].reshape(LH, LD), (1, 2)).T
    d["L1_attn_w_vT"], d["L1_attn_w_uT"] = w[2].T, w[3].T
    d["L1_attn_b_v"], d["L1_attn_b_uC"] = b[2:3], columns(b[3])
    d["L1_attn_theta2"] = np.tile(a["L1_attn_theta"].reshape(LH, LD), (1, 2)).T
    return d


def kernel(**inputs):
    import numpy as np
    import concourse.bacc as bacc
    from concourse.bass_utils import run_bass_kernel_spmd

    nc = bacc.Bacc("TRN2", target_bir_lowering=False, num_devices=1)
    arrays, aps = {}, {}
    for name, value in _laid_out(inputs).items():
        value = np.ascontiguousarray(value)
        arrays["in_" + name] = value
        aps[name] = nc.dram_tensor("in_" + name, value.shape, mybir.dt.from_np(value.dtype),
                                   kind="ExternalInput").ap()
    out = nc.dram_tensor("out_x", (1, T, D), F32, kind="ExternalOutput").ap()
    perceiver_kernel(nc, aps, out, STAGES)
    r = run_bass_kernel_spmd(nc, [arrays], core_ids=[0])
    return r.results[0]["out_x"]
```
